# Optimizing a Trainium2 kernel written in Bass

```python
import numpy as np
import jax
import jax.numpy as jnp

def _softmax(x, axis=-1):
    return jax.nn.softmax(x, axis=axis)

def _gelu(x):
    return jax.nn.gelu(x, approximate=True)

def _silu(x):
    return jax.nn.silu(x)

def _sigmoid(x):
    return jax.nn.sigmoid(x)

def _layernorm(x, axis=-1, eps=1e-05):
    m = jnp.mean(x, axis=axis, keepdims=True)
    v = jnp.var(x, axis=axis, keepdims=True)
    return (x - m) / jnp.sqrt(v + eps)

def _scatter_add(tgt, idx, src, axis=0):
    return tgt.at[idx].add(src)

def _segment_sum(src, seg, n):
    return jax.ops.segment_sum(src, seg, n)
kernel_name = 'mk_xattn_ffn_d2_seqx_r8_323319'

def setup_inputs(seed: int=0):
    np.random.seed(seed)
    _w = jnp.asarray

    def _rec_inputs():
        import jax
        import jax.numpy as jnp
        _rk = jax.random.key(seed)
        x = -0.0002928 + 1 * jax.random.normal(jax.random.fold_in(_rk, 1), (4, 512, 128), jnp.float32)
        _lenS = 512 - jax.random.randint(jax.random.fold_in(_rk, 7), (4,), 0, max(1, 512 // 4) + 1, jnp.int32)
        _lenS2 = 154 - jax.random.randint(jax.random.fold_in(_rk, 8), (4,), 0, max(1, 154 // 4) + 1, jnp.int32)
        _ctx_1024P = jax.random.normal(jax.random.fold_in(_rk, 11), (4, 16, 128), jnp.float32)
        _ctx_1024c = jax.random.dirichlet(jax.random.fold_in(_rk, 511), 0.3 * jnp.ones((16,), jnp.float32), (4, 154))
        _ctx_1024t = jnp.einsum('bsk,bkd->bsd', _ctx_1024c, _ctx_1024P)
        _ctx_1024t = _ctx_1024t * jax.lax.rsqrt(jnp.mean(jnp.square(_ctx_1024t)) + 1e-12) * 0.953939
        ctx_1024 = -1.39393e-06 + 0.999914 * (_ctx_1024t + 0.3 * jax.random.normal(jax.random.fold_in(_rk, 611), (4, 154, 128), jnp.float32))
        _validS = jnp.arange(512)[None, :] < _lenS[:, None]
        _validS2 = jnp.arange(154)[None, :] < _lenS2[:, None]
        _causal = jnp.tril(jnp.ones((512, 512), dtype=bool))
        mask_BxSxS2_bk1 = jnp.broadcast_to(_validS2[:, None, :], (4, 512, 154))
        return (x, ctx_1024, mask_BxSxS2_bk1)
    x, ctx_1024, mask_BxSxS2_bk1 = _rec_inputs()

    def _L0_xattn_setup():
        import jax, jax.numpy as jnp
        import numpy as np
        HEADS = 16
        B, S, D = (2, 256, 128)
        key = jax.random.key(seed)
        kq, kk, kv, km = jax.random.split(key, 4)
        q = jax.random.normal(kq, (B, S, D), dtype=jnp.float32)
        k = jax.random.normal(kk, (B, S, D), dtype=jnp.float32)
        v = jax.random.normal(kv, (B, S, D), dtype=jnp.float32)
        mask = jax.random.randint(km, (B, S, S), 0, 2).astype(bool)
        return {'q': q, 'k': k, 'v': v, 'mask': mask}
    _L0_xattn_all = _L0_xattn_setup()
    _L0_xattn_in = {k: v for k, v in _L0_xattn_all.items() if k in ()}
    del _L0_xattn_all

    def _L0_ffn_setup():
        import jax, jax.numpy as jnp
        import numpy as np
        B, S, D_MODEL, D_HIDDEN = (4, 256, 128, 512)

        def act_quant(x):
            scale = 127.0 / jnp.clip(jnp.max(jnp.abs(x), axis=-1, keepdims=True), 1e-05)
            return jnp.clip(jnp.round(x * scale), -128, 127) / scale

        def weight_quant(w):
            scale = 1.0 / jnp.clip(jnp.mean(jnp.abs(w)), 1e-05)
            return jnp.clip(jnp.round(w * scale), -1, 1) / scale

        def bit_linear(x, w):
            xq = x + jax.lax.stop_gradient(act_quant(x) - x)
            wq = w + jax.lax.stop_gradient(weight_quant(w) - w)
            return jnp.einsum('bsd,hd->bsh', xq, wq)

        def depthwise_conv1d(x_bcl, w, b):
            y = jax.lax.conv_general_dilated(x_bcl, w, window_strides=(1,), padding=[(1, 1)], dimension_numbers=('NCH', 'OIH', 'NCH'), feature_group_count=x_bcl.shape[1])
            return y + b[None, :, None]
        key = jax.random.key(seed)
        ks = jax.random.split(key, 5)
        lim1 = 1.0 / np.sqrt(D_MODEL)
        lim2 = 1.0 / np.sqrt(D_HIDDEN)
        limc = 1.0 / np.sqrt(3.0)
        return {'x': jax.random.normal(ks[0], (B, S, D_MODEL), dtype=jnp.float32), 'w1': jax.random.uniform(ks[1], (D_HIDDEN, D_MODEL), jnp.float32, -lim1, lim1), 'conv_w': jax.random.uniform(ks[2], (D_HIDDEN, 1, 3), jnp.float32, -limc, limc), 'conv_b': jax.random.uniform(ks[3], (D_HIDDEN,), jnp.float32, -limc, limc), 'w2': jax.random.uniform(ks[4], (D_MODEL, D_HIDDEN), jnp.float32, -lim2, lim2)}
    _L0_ffn_all = _L0_ffn_setup()
    _L0_ffn_in = {k: v for k, v in _L0_ffn_all.items() if k in ('w1', 'conv_w', 'conv_b', 'w2')}
    del _L0_ffn_all

    def _L1_xattn_setup():
        import jax, jax.numpy as jnp
        import numpy as np
        D_MODEL = 128
        NUM_HEADS = 16
        HEAD_DIM = D_MODEL // NUM_HEADS

        def _split_heads(x):
            B, S, _ = x.shape
            return x.reshape(B, S, NUM_HEADS, HEAD_DIM).transpose(0, 2, 1, 3)
        key = jax.random.key(seed)
        ks = jax.random.split(key, 11)
        B, S = (2, 256)
        scale = 1.0 / np.sqrt(D_MODEL)
        inp = {'query': jax.random.normal(ks[0], (B, S, D_MODEL), jnp.float32), 'key': jax.random.normal(ks[1], (B, S, D_MODEL), jnp.float32), 'value': jax.random.normal(ks[2], (B, S, D_MODEL), jnp.float32), 'Wq': jax.random.normal(ks[3], (D_MODEL, D_MODEL), jnp.float32) * scale, 'bq': jnp.zeros((D_MODEL,), jnp.float32), 'Wk': jax.random.normal(ks[4], (D_MODEL, D_MODEL), jnp.float32) * scale, 'bk': jnp.zeros((D_MODEL,), jnp.float32), 'Wv': jax.random.normal(ks[5], (D_MODEL, D_MODEL), jnp.float32) * scale, 'bv': jnp.zeros((D_MODEL,), jnp.float32), 'Wo': jax.random.normal(ks[6], (D_MODEL, D_MODEL), jnp.float32) * scale, 'bo': jnp.zeros((D_MODEL,), jnp.float32)}
        return inp
    _L1_xattn_all = _L1_xattn_setup()
    _L1_xattn_in = {k: v for k, v in _L1_xattn_all.items() if k in ('Wq', 'bq', 'Wk', 'bk', 'Wv', 'bv', 'Wo', 'bo')}
    del _L1_xattn_all

    def _L1_ffn_setup():
        import jax, jax.numpy as jnp
        import numpy as np
        import math
        MAX_NORM = 0.95
        CURVATURE = 1.0
        TOP_K = 2
        EPS = 1e-07

        def _project_to_ball(x):
            norm = jnp.clip(jnp.linalg.norm(x, axis=-1, keepdims=True), EPS, None)
            scale = jnp.where(norm > MAX_NORM, MAX_NORM / norm, jnp.ones_like(norm))
            return x * scale
        key = jax.random.key(seed)
        ks = jax.random.split(key, 8)
        B, N, D, E, F = (2, 256, 128, 8, 512)
        x = jax.random.normal(ks[0], (B, N, D), dtype=jnp.float32)
        c = jax.random.normal(ks[1], (E, D), dtype=jnp.float32)
        centroids = c / jnp.linalg.norm(c, axis=-1, keepdims=True) * 0.5
        Wp = jax.random.normal(ks[2], (D, D), dtype=jnp.float32) * 0.02
        bp = jnp.zeros((D,), dtype=jnp.float32)
        W1 = jax.random.normal(ks[3], (E, D, F), dtype=jnp.float32) * 0.02
        b1 = jnp.zeros((E, F), dtype=jnp.float32)
        W2 = jax.random.normal(ks[4], (E, F, D), dtype=jnp.float32) * 0.02
        b2 = jnp.zeros((E, D), dtype=jnp.float32)
        return {'x': x, 'centroids': centroids, 'Wp': Wp, 'bp': bp, 'W1': W1, 'b1': b1, 'W2': W2, 'b2': b2}
    _L1_ffn_all = _L1_ffn_setup()
    _L1_ffn_in = {k: v for k, v in _L1_ffn_all.items() if k in ('centroids', 'Wp', 'bp', 'W1', 'b1', 'W2', 'b2')}
    del _L1_ffn_all
    return {'x': x, 'ctx_1024': ctx_1024, 'mask_BxSxS2_bk1': mask_BxSxS2_bk1, 'L0_ffn_w1': _L0_ffn_in['w1'], 'L0_ffn_conv_w': _L0_ffn_in['conv_w'], 'L0_ffn_conv_b': _L0_ffn_in['conv_b'], 'L0_ffn_w2': _L0_ffn_in['w2'], 'L1_xattn_Wq': _L1_xattn_in['Wq'], 'L1_xattn_bq': _L1_xattn_in['bq'], 'L1_xattn_Wk': _L1_xattn_in['Wk'], 'L1_xattn_bk': _L1_xattn_in['bk'], 'L1_xattn_Wv': _L1_xattn_in['Wv'], 'L1_xattn_bv': _L1_xattn_in['bv'], 'L1_xattn_Wo': _L1_xattn_in['Wo'], 'L1_xattn_bo': _L1_xattn_in['bo'], 'L1_ffn_centroids': _L1_ffn_in['centroids'], 'L1_ffn_Wp': _L1_ffn_in['Wp'], 'L1_ffn_bp': _L1_ffn_in['bp'], 'L1_ffn_W1': _L1_ffn_in['W1'], 'L1_ffn_b1': _L1_ffn_in['b1'], 'L1_ffn_W2': _L1_ffn_in['W2'], 'L1_ffn_b2': _L1_ffn_in['b2']}

def reference(x, ctx_1024, mask_BxSxS2_bk1, L0_ffn_w1, L0_ffn_conv_w, L0_ffn_conv_b, L0_ffn_w2, L1_xattn_Wq, L1_xattn_bq, L1_xattn_Wk, L1_xattn_bk, L1_xattn_Wv, L1_xattn_bv, L1_xattn_Wo, L1_xattn_bo, L1_ffn_centroids, L1_ffn_Wp, L1_ffn_bp, L1_ffn_W1, L1_ffn_b1, L1_ffn_W2, L1_ffn_b2):
    import jax
    import jax.numpy as jnp

    def _L0_xattn_ref(q, k, v, mask):
        import jax, jax.numpy as jnp
        import numpy as np
        HEADS = 16
        B, S, D = (2, 256, 128)
        hd = q.shape[-1] // HEADS

        def split_heads(x):
            return x.reshape(x.shape[:-1] + (HEADS, hd)).swapaxes(-3, -2)
        qh, kh, vh = (split_heads(q), split_heads(k), split_heads(v))
        scores = jnp.einsum('bhqd,bhkd->bhqk', qh, kh) / jnp.sqrt(jnp.float32(hd))
        scores = scores + mask[:, None, :, :].astype(scores.dtype) * jnp.float32(-10000.0)
        attn = jax.nn.softmax(scores, axis=-1)
        out = jnp.einsum('bhqk,bhkd->bhqd', attn, vh)
        return out.swapaxes(-3, -2).reshape(q.shape[:-2] + (q.shape[-2], HEADS * hd))

    def _L0_ffn_ref(x, w1, conv_w, conv_b, w2):
        import jax, jax.numpy as jnp
        import numpy as np
        B, S, D_MODEL, D_HIDDEN = (4, 256, 128, 512)

        def act_quant(x):
            scale = 127.0 / jnp.clip(jnp.max(jnp.abs(x), axis=-1, keepdims=True), 1e-05)
            return jnp.clip(jnp.round(x * scale), -128, 127) / scale

        def weight_quant(w):
            scale = 1.0 / jnp.clip(jnp.mean(jnp.abs(w)), 1e-05)
            return jnp.clip(jnp.round(w * scale), -1, 1) / scale

        def bit_linear(x, w):
            xq = x + jax.lax.stop_gradient(act_quant(x) - x)
            wq = w + jax.lax.stop_gradient(weight_quant(w) - w)
            return jnp.einsum('bsd,hd->bsh', xq, wq)

        def depthwise_conv1d(x_bcl, w, b):
            y = jax.lax.conv_general_dilated(x_bcl, w, window_strides=(1,), padding=[(1, 1)], dimension_numbers=('NCH', 'OIH', 'NCH'), feature_group_count=x_bcl.shape[1])
            return y + b[None, :, None]
        h = bit_linear(x, w1)
        h = depthwise_conv1d(h.transpose(0, 2, 1), conv_w, conv_b)
        h = h.transpose(0, 2, 1)
        h = jax.nn.silu(h)
        return bit_linear(h, w2)

    def _L1_xattn_ref(query, key, value, Wq, bq, Wk, bk, Wv, bv, Wo, bo):
        import jax, jax.numpy as jnp
        import numpy as np
        D_MODEL = 128
        NUM_HEADS = 16
        HEAD_DIM = D_MODEL // NUM_HEADS

        def _split_heads(x):
            B, S, _ = x.shape
            return x.reshape(B, S, NUM_HEADS, HEAD_DIM).transpose(0, 2, 1, 3)
        q = _split_heads(query @ Wq.T + bq)
        k = _split_heads(key @ Wk.T + bk)
        v = _split_heads(value @ Wv.T + bv)
        scores = jnp.einsum('bhqd,bhkd->bhqk', q, k) / jnp.sqrt(jnp.asarray(HEAD_DIM, q.dtype))
        probs = jax.nn.softmax(scores, axis=-1)
        ctx = jnp.einsum('bhqk,bhkd->bhqd', probs, v)
        B, H, S, Dh = ctx.shape
        ctx = ctx.transpose(0, 2, 1, 3).reshape(B, S, H * Dh)
        return ctx @ Wo.T + bo

    def _L1_ffn_ref(x, centroids, Wp, bp, W1, b1, W2, b2):
        import jax, jax.numpy as jnp
        import numpy as np
        import math
        MAX_NORM = 0.95
        CURVATURE = 1.0
        TOP_K = 2
        EPS = 1e-07

        def _project_to_ball(x):
            norm = jnp.clip(jnp.linalg.norm(x, axis=-1, keepdims=True), EPS, None)
            scale = jnp.where(norm > MAX_NORM, MAX_NORM / norm, jnp.ones_like(norm))
            return x * scale
        B, N, D = x.shape
        E = centroids.shape[0]
        x_hyper = _project_to_ball(x @ Wp + bp)
        c_proj = _project_to_ball(centroids)
        x_norm_sq = jnp.sum(x_hyper * x_hyper, axis=-1)
        c_norm_sq = jnp.sum(c_proj * c_proj, axis=-1)
        x_norm_sq = jnp.clip(x_norm_sq, None, 0.99)
        c_norm_sq = jnp.clip(c_norm_sq, None, 0.99)
        dot = jnp.einsum('bnd,ed->bne', x_hyper, c_proj)
        diff_sq = jnp.maximum(x_norm_sq[..., None] + c_norm_sq - 2.0 * dot, 0.0)
        denom = (1.0 - x_norm_sq)[..., None] * (1.0 - c_norm_sq) + EPS
        arg = jnp.clip(1.0 + 2.0 * diff_sq / denom, 1.0 + EPS, None)
        dist = jnp.arccosh(arg)
        routing_logits = -dist / math.sqrt(CURVATURE)
        top_v, top_i = jax.lax.top_k(routing_logits, TOP_K)
        top_w = jax.nn.softmax(top_v, axis=-1)
        comb = jnp.sum(jax.nn.one_hot(top_i, E, dtype=x.dtype) * top_w[..., None], axis=2)
        h = jax.nn.gelu(jnp.einsum('bnd,edf->bnef', x, W1) + b1, approximate=False)
        y = jnp.einsum('bnef,efd->bned', h, W2) + b2
        out = jnp.einsum('bne,bned->bnd', comb, y)
        return out
    x = x + _L0_xattn_ref(_layernorm(x, axis=-1), ctx_1024, ctx_1024, mask_BxSxS2_bk1)
    x = x + _L0_ffn_ref(_layernorm(x, axis=-1), L0_ffn_w1, L0_ffn_conv_w, L0_ffn_conv_b, L0_ffn_w2)
    x = x + _L1_xattn_ref(_layernorm(x, axis=-1), ctx_1024, ctx_1024, L1_xattn_Wq, L1_xattn_bq, L1_xattn_Wk, L1_xattn_bk, L1_xattn_Wv, L1_xattn_bv, L1_xattn_Wo, L1_xattn_bo)
    x = x + _L1_ffn_ref(_layernorm(x, axis=-1), L1_ffn_centroids, L1_ffn_Wp, L1_ffn_bp, L1_ffn_W1, L1_ffn_b1, L1_ffn_W2, L1_ffn_b2)
    return x

_drawn_inputs = setup_inputs


def setup_inputs(seed=0):
    import zlib

    import numpy as np

    out = dict(_drawn_inputs(seed))
    spreads = {'L1_xattn_bq': (0.0, 0.478),
     'L1_xattn_bk': (0.0, 0.8),
     'L1_xattn_bv': (0.0, 0.1),
     'L1_xattn_bo': (0.0, 0.1),
     'L1_ffn_bp': (0.0, 0.1),
     'L1_ffn_b1': (0.0, 0.73),
     'L1_ffn_b2': (0.0, 0.1)}
    factors = {}
    for name, (base, spread) in spreads.items():
        noise = np.random.default_rng([zlib.crc32(name.encode()), seed]).standard_normal(out[name].shape)
        drawn = base * np.exp(spread * noise) if base else spread * noise
        out[name] = jnp.asarray(drawn.astype(out[name].dtype))
    for name, factor in factors.items():
        out[name] = (out[name] * factor).astype(out[name].dtype)
    return out
```

```python
from contextlib import ExitStack

import numpy as np

import concourse.bass as bass
from concourse import mybir

F32 = mybir.dt.float32
F16 = mybir.dt.float16
U8 = mybir.dt.uint8
U32 = mybir.dt.uint32
ALU = mybir.AluOpType
ACT = mybir.ActivationFunctionType
AX_X = mybir.AxisListType.X

P = 128
BATCH, SEQ, D = 4, 512, 128
KEYS = 154
HEADS, HD = 16, 8
GROUPS, PER_GROUP = 4, 4
TILES = SEQ // P
REST = KEYS - P
QUAD = 32
HIDDEN = 512
CH = HIDDEN // P
EXPERTS = 8
ROUND = 12582912.0
W1_SCALE = 256.0
MASKED = -10000.0
LN_EPS = 1e-5
PAIRS = (CH + 1) * GROUPS // 2
ROUTE_STEPS = 38
MAX_HEADS = ((0, 3), (3, 3), (6, 3), (9, 3), (12, 2), (14, 2))


class Signal:

    def __init__(self, sem, per, first=0):
        self.sem, self.per, self.first = sem, per, first

    def at(self, b, k):
        return b * self.per + (k + self.first)


def build(nc, x, ctxt, ctx_km, mask_tm, mask_t, w1t, conv_w, conv_b, w2t, wq_t, bq, wk_t, bk, bk_col, wv_t, bv,
          wo_t, bo, cent, wp, bp_col, moe_w1, moe_b1, moe_w2, moe_b2, ident_in, blocks_in, iota_in, out):
    with ExitStack() as ctx:
        def sb(name, shape, dt=F32):
            return ctx.enter_context(nc.sbuf_tensor(name, shape, dt))

        def sem(name):
            return ctx.enter_context(nc.semaphore(name))

        def sig(name, per, first=0):
            return Signal(sem(name), per, first)

        ident = sb("ident", [P, P])
        ident16 = sb("ident16", [P, P], F16)
        mask_diag = sb("mask_diag", [P, P], F16)
        ones = sb("ones", [P, P])
        head_blocks = sb("head_blocks", [P, HEADS])
        iota8 = sb("iota8", [P, EXPERTS])
        w1_raw = sb("w1_raw", [P, HIDDEN])
        w2_raw = sb("w2_raw", [P, CH, D])
        bit_w1 = sb("bit_w1", [P, HIDDEN], F16)
        bit_w2 = sb("bit_w2", [P, CH, D], F16)
        abs_sums = sb("abs_sums", [P, 2])
        w_mean = sb("w_mean", [P, 2])
        w_scale = sb("w_scale", [P, 2])
        w_step = sb("w_step", [P, 2])
        cw = sb("cw", [P, CH, 3])
        cb = sb("cb", [P, CH])
        wq_s = sb("wq_s", [P, D])
        wkv_s = sb("wkv_s", [P, 2 * D])
        wo_s = sb("wo_s", [P, D])
        wp_s = sb("wp_s", [P, D])
        bq_s = sb("bq_s", [P, D])
        bo_s = sb("bo_s", [P, D])
        kv_bias = sb("kv_bias", [P, 2, 2 * D])
        bk_s = sb("bk_s", [P, 1])
        bp_s = sb("bp_s", [P, 1])
        cent_s = sb("cent_s", [EXPERTS, D])
        cent_sq = sb("cent_sq", [EXPERTS, D])
        cent_n = sb("cent_n", [EXPERTS, 3])
        cent_t = sb("cent_t", [P, EXPERTS])
        cent_t_sq = sb("cent_t_sq", [P, EXPERTS])
        c_norm = sb("c_norm", [P, EXPERTS])
        c_rest = sb("c_rest", [P, EXPERTS])
        big = sb("big", [P, 10 * SEQ])
        ew1_raw = big[:, 0:EXPERTS * HIDDEN].rearrange("p (e f) -> p e f", e=EXPERTS)
        ew1_hi = sb("ew1_hi", [P, EXPERTS, HIDDEN], F16)
        ew1_lo = sb("ew1_lo", [P, EXPERTS, HIDDEN], F16)
        ew2 = sb("ew2", [P, EXPERTS, CH, D])
        eb1 = sb("eb1", [P, EXPERTS * CH])
        eb2 = sb("eb2", [EXPERTS, D])

        x_in = sb("x_in", [P, TILES, D])
        ctx_t = sb("ctx_t", [P, KEYS + P])
        ctx_k = sb("ctx_k", [P, 2, D])
        m_tok8 = sb("m_tok8", [P, TILES, KEYS], U8)
        m_key8 = sb("m_key8", [P, 2, SEQ], U8)
        m_tok = sb("m_tok", [P, TILES, KEYS], F16)
        m_key = sb("m_key", [P, 2, SEQ], F16)

        k_blocks = [sb(f"k_blocks{l}", [P, HEADS, KEYS], F16) for l in range(2)]
        k_feat = [sb(f"k_feat{l}", [P, 2, HEADS, QUAD], F16) for l in range(2)]
        k_main = [sb(f"k_main{l}", [P, HEADS, P], F16) for l in range(2)]
        k_rest = [sb(f"k_rest{l}", [P, GROUPS, P], F16) for l in range(2)]
        v_main = [sb(f"v_main{l}", [P, HEADS, QUAD]) for l in range(2)]
        v_rest = [sb(f"v_rest{l}", [P, HEADS, QUAD]) for l in range(2)]
        kv1 = sb("kv1", [P, 2, 2 * D])
        k1_t = sb("k1_t", [P, KEYS])
        q_f = sb("q_f", [P, TILES, D])
        q_feat = sb("q_feat", [P, TILES, HEADS, QUAD], F16)
        q_hi = sb("q_hi", [P, TILES, D], F16)
        q_hi_t = sb("q_hi_t", [P, SEQ], F16)
        q_op = sb("q_op", [P, GROUPS, SEQ], F16)
        neg_max = sb("neg_max", [P, TILES, HEADS])
        probs = big[:, :].rearrange("p (n t) -> p n t", t=SEQ)
        o_t = sb("o_t", [P, GROUPS, SEQ])
        denom = sb("denom", [P, TILES * HEADS])
        attn = sb("attn", [P, TILES, D])
        attn_t = sb("attn_t", [P, SEQ])

        gate = sb("gate", [P, 1])
        moments = sb("moments", [P, TILES, 6])
        mean_var = sb("mean_var", [P, TILES, 2])
        std = sb("std", [P, TILES])
        rstd = sb("rstd", [P, TILES])
        xn = sb("xn", [P, TILES, D])
        xn_t = sb("xn_t", [P, SEQ])
        x1 = sb("x1", [P, TILES, D])
        x2 = sb("x2", [P, TILES, D])
        x2_bo = sb("x2_bo", [P, TILES, D])
        x3 = sb("x3", [P, TILES, D])
        y_sum = sb("y_sum", [P, TILES, D])

        top = sb("top", [P, TILES])
        a_scale = sb("a_scale", [P, TILES])
        a_step = sb("a_step", [P, TILES])
        x_whole = sb("x_whole", [P, TILES, D])
        xq = sb("xq", [P, TILES, D], F16)
        xq_t = sb("xq_t", [P, SEQ], F16)
        step_diag = sb("step_diag", [P, TILES, P])
        step_row = sb("step_row", [P, SEQ])
        h_pad = sb("h_pad", [P, CH, SEQ + 2])
        h_conv = sb("h_conv", [P, CH, SEQ])
        h_act = h_conv
        h_whole = o_t
        hq = sb("hq", [P, TILES, HIDDEN], F16)
        hq_t = sb("hq_t", [P, TILES, CH, P], F16)

        x_hi = sb("x_hi", [P, SEQ], F16)
        x_lo = sb("x_lo", [P, SEQ], F16)
        z_t = sb("z_t", [P, SEQ])
        z_sq = sb("z_sq", [P, SEQ])
        r1 = sb("r1", [P, 8, TILES])
        r8 = sb("r8", [P, 8, TILES, EXPERTS])
        best = sb("best", [P, TILES, 8])
        best_i = sb("best_i", [P, TILES, 8], U32)
        best_f = sb("best_f", [P, TILES, 8])
        comb = sb("comb", [P, TILES, EXPERTS])
        comb_t = sb("comb_t", [EXPERTS, SEQ])
        hidden = big[:, 0:2 * CH * SEQ].rearrange("p (r c t) -> p r c t", r=2, c=CH)

        ps = ctx.enter_context(nc.psum_tensor("ps", [P, 8 * 512], F32))

        def bank(i, n=1):
            return ps[:, 512 * i:512 * (i + n)]

        def bank16(i):
            return bank(i).bitcast(F16)

        s_const = sem("s_const_loaded")
        s_bit_w = sem("s_bitnet_weights_loaded")
        s_proj_w = sem("s_projection_weights_loaded")
        s_kv_w = sem("s_key_value_weights_loaded")
        s_exp_w1 = sem("s_expert_w1_loaded")
        s_exp_rest = sem("s_expert_rest_loaded")
        s_memset = sem("s_memset")
        s_pool_set = sem("s_pool_memset")
        s_bias_set = sem("s_bias_cleared")
        s_ident = sem("s_identities")
        s_wabs = sem("s_weight_abs_sums")
        s_wsum = sem("s_weight_sums")
        s_bit = sem("s_bitnet_weights")
        s_cent = sem("s_centroids")
        s_cent_a = sem("s_centroids_act")
        s_cent_pe = sem("s_centroids_pe")
        s_ew1 = sem("s_expert_w1_high")
        s_ew1_lo = sem("s_expert_w1_low")

        x_loaded = sig("x_loaded", 16)
        ctx_loaded = sig("ctx_loaded", 32)
        mask_loaded = sig("mask_loaded", 32)
        out_free = sig("out_free", 16, 16)
        masks = sig("masks_converted", 2)
        kb_ready = [sig(f"k_blocks_ready{l}", 1) for l in range(2)]
        kf_ready = [sig(f"k_features_ready{l}", 3) for l in range(2)]
        v_ready = [sig(f"values_ready{l}", 5) for l in range(2)]
        kf_t = [sig(f"k_features_transposed{l}", 1) for l in range(2)]
        k_ready = [sig(f"k_operands_ready{l}", 8) for l in range(2)]
        kv_mm = sig("kv_projected", 1)
        kv_out = sig("kv_biased", 1)
        k1t_out = sig("k1_transposed_biased", 1)
        ln_mom = [sig(f"ln_moments{n}", 8) for n in range(4)]
        ln_std = [sig(f"ln_std{n}", 1) for n in range(4)]
        ln_rstd = [sig(f"ln_rstd{n}", 2) for n in range(4)]
        ln_out = [sig(f"ln_out{n}", TILES) for n in range(4)]
        q_ready = sig("q_projected_scaled", 1)
        q_split = [sig(f"q_split{l}", 2) for l in range(2)]
        q_hi2 = [sig(f"q_hi_copied{l}", 2) for l in range(2)]
        qh_t = [sig(f"q_hi_transposed{l}", 1) for l in range(2)]
        qh_out = [sig(f"q_hi_ready{l}", 1) for l in range(2)]
        s_tok = [sig(f"token_scores{l}", 3 * TILES) for l in range(2)]
        maxed = [sig(f"maxima{l}", 3 * TILES) for l in range(2)]
        shift = [sig(f"shift_features{l}", 2 * TILES) for l in range(2)]
        qf_t = [sig(f"q_features_transposed{l}", TILES) for l in range(2)]
        q_out = [sig(f"q_operand_ready{l}", TILES) for l in range(2)]
        s_key = [sig(f"key_scores{l}", PAIRS) for l in range(2)]
        exped = [sig(f"exponentials{l}", PAIRS) for l in range(2)]
        pv = [sig(f"weighted_values{l}", GROUPS) for l in range(2)]
        o_out = [sig(f"weighted_values_copied{l}", GROUPS) for l in range(2)]
        o_tok = [sig(f"outputs_by_token{l}", 1) for l in range(2)]
        attn_out = [sig(f"attention_normalised{l}", 2) for l in range(2)]
        x1_out = sig("x1_ready", 1)
        xq_scale = sig("xq_scale", 5)
        xq_out = sig("xq_ready", 5)
        diag_out = sig("step_diagonals", TILES)
        xq_tr = sig("xq_transposed", 1)
        xqt_out = sig("xq_t_ready", 1)
        step_mm = sig("step_row_product", 1)
        step_out = sig("step_row_ready", 1)
        up = sig("bitnet_up_product", CH)
        h_scaled = sig("h_scaled", CH)
        tap0 = sig("conv_tap0", CH)
        taps = sig("conv_taps", 2 * CH)
        silu = sig("silu", CH)
        h_tr = sig("h_transposed", CH)
        hq_scale = sig("hq_scale", 6)
        hq_out = sig("hq_ready", 2 * TILES)
        hq_tr = sig("hq_transposed", TILES)
        hqt_out = sig("hq_t_ready", TILES)
        down = sig("bitnet_down_product", TILES)
        x2_out = sig("x2_ready", TILES)
        x2b_out = sig("x2_with_bias", 1)
        xn1_tr = sig("xn_transposed1", 1)
        xn1_out = sig("xn_t_ready1", 1)
        q_mm = sig("q_product", 1)
        a_tr = sig("attention_transposed", 1)
        at_out = sig("attention_t_ready", 1)
        o_mm = sig("output_product", 1)
        x3_out = sig("x3_ready", 1)
        xn2_tr = sig("xn_transposed2", 1)
        xn2_out = sig("xn_t_ready2", 2)
        xlo_out = sig("x_lo_ready", 1)
        z_mm = sig("z_product", 1)
        z_out = sig("z_ready", 2)
        dots = sig("centroid_dots", 1)
        route = sig("routing_steps", ROUTE_STEPS)
        route_n = sig("token_norms", 1)
        route_u = sig("arccosh_root", 1)
        comb_tr = sig("comb_transposed", 1)
        combt_out = sig("comb_t_ready", 1)
        b2_mm = sig("expert_bias_product", 1)
        h_mm = sig("expert_hidden_product", EXPERTS * CH)
        gelu = sig("gelu", EXPERTS * CH)
        y_mm = sig("expert_output", EXPERTS)
        y_used = sig("expert_output_added", 1 + TILES * EXPERTS)

        def wait(eng, signal, b, k):
            eng.wait_ge(signal.sem, signal.at(b, k))

        block = ctx.enter_context(nc.Block())

        @block.sync
        def _(sp):
            sp.sem_inc(out_free.sem, 16)

            def load_batch(b):
                sp.dma_start(x_in[:], x[b].rearrange("(t p) d -> p t d", p=P)).then_inc(x_loaded.sem, 16)
                sp.dma_start(ctx_t[:], ctxt[b]).then_inc(ctx_loaded.sem, 16)
                sp.dma_start(ctx_k[:], ctx_km[b]).then_inc(ctx_loaded.sem, 16)
                sp.dma_start(m_tok8[:], mask_tm[b].rearrange("(t p) k -> p t k", p=P)).then_inc(mask_loaded.sem, 16)
                sp.dma_start(m_key8[:], mask_t[b]).then_inc(mask_loaded.sem, 16)

            load_batch(0)
            sp.dma_start(w1_raw[:], w1t).then_inc(s_bit_w, 16)
            sp.dma_start(w2_raw[:], w2t.rearrange("(c p) d -> p c d", p=P)).then_inc(s_bit_w, 16)
            sp.dma_start(cw[:], conv_w.rearrange("(c p) k -> p c k", p=P)).then_inc(s_bit_w, 16)
            sp.dma_start(cb[:], conv_b).then_inc(s_bit_w, 16)
            sp.dma_start(ew1_raw, moe_w1.rearrange("e d f -> d e f")).then_inc(s_exp_w1, 16)
            sp.dma_start(ew2[:], moe_w2.rearrange("e (c p) d -> p e c d", p=P)).then_inc(s_exp_rest, 16)
            sp.dma_start(eb1[:], moe_b1).then_inc(s_exp_rest, 16)
            sp.dma_start(eb2[:], moe_b2).then_inc(s_exp_rest, 16)
            with sp.Fori(1, BATCH) as b:
                wait(sp, pv[1], b - 1, GROUPS)
                load_batch(b)
                wait(sp, y_used, b - 1, 1 + TILES * EXPERTS)
                sp.dma_start(out[b - 1].rearrange("(t p) d -> p t d", p=P), y_sum[:]).then_inc(out_free.sem, 16)
            sp.wait_ge(y_used.sem, y_used.per * BATCH)
            sp.dma_start(out[BATCH - 1].rearrange("(t p) d -> p t d", p=P), y_sum[:]).then_inc(out_free.sem, 16)
            sp.wait_ge(out_free.sem, 16 * (BATCH + 1))

        @block.gpsimd
        def _(pool):
            for n, t in enumerate([*k_main, *k_rest]):
                nc.gpsimd.memset(t[:].rearrange("p a b -> p (a b)").bitcast(F32), 0.0).then_inc(s_pool_set, 1)
            nc.gpsimd.memset(kv_bias[:], 0.0).then_inc(s_bias_set, 1)
            pool.dma_start(ident[:], ident_in).then_inc(s_const, 16)
            pool.dma_start(head_blocks[:], blocks_in).then_inc(s_const, 16)
            pool.dma_start(iota8[:], iota_in).then_inc(s_const, 16)
            pool.dma_start(wkv_s[:, 0:D], wk_t).then_inc(s_kv_w, 16)
            pool.dma_start(wkv_s[:, D:2 * D], wv_t).then_inc(s_kv_w, 16)
            pool.dma_start(bk_s[:], bk_col).then_inc(s_kv_w, 16)
            pool.wait_ge(s_bias_set, 1)
            for c, vec in enumerate((bk, bv)):
                part = slice(c * D, (c + 1) * D)
                pool.dma_start(kv_bias[:, 0, part], vec.partition_broadcast(P)).then_inc(s_kv_w, 16)
                for j in range(PER_GROUP):
                    pool.dma_start(kv_bias[QUAD * j:QUAD * j + REST, 1, part],
                                   vec.partition_broadcast(REST)).then_inc(s_kv_w, 16)
            pool.wait_ge(s_const, 48)
            pool.wait_ge(s_memset, 7)
            with pool.Fori(0, BATCH) as b:

                def blocks(l, k_t):
                    nc.gpsimd.tensor_tensor(k_blocks[l][:], k_t.unsqueeze(1).broadcast_to([P, HEADS, KEYS]),
                                            head_blocks[:].unsqueeze(2).broadcast_to([P, HEADS, KEYS]),
                                            ALU.mult).then_inc(kb_ready[l].sem, 1)

                def features(l, keys):
                    by_head = keys.rearrange("p c (h d) -> p c h d", d=HD)
                    nc.gpsimd.tensor_copy(k_feat[l][:, :, :, 0:HD], by_head).then_inc(kf_ready[l].sem, 1)
                    nc.gpsimd.tensor_copy(k_feat[l][:, :, :, HD:2 * HD], by_head).then_inc(kf_ready[l].sem, 1)
                    wait(pool, kf_ready[l], b, 1)
                    nc.gpsimd.tensor_tensor(k_feat[l][:, :, :, 2 * HD:3 * HD], by_head, k_feat[l][:, :, :, 0:HD],
                                            ALU.subtract).then_inc(kf_ready[l].sem, 1)

                wait(pool, ctx_loaded, b, 32)
                wait(pool, mask_loaded, b, 32)
                blocks(0, ctx_t[:, 0:KEYS])
                nc.gpsimd.tensor_copy(m_tok[:], m_tok8[:]).then_inc(masks.sem, 1)
                features(0, ctx_k[:])
                nc.gpsimd.tensor_copy(m_key[:], m_key8[:]).then_inc(masks.sem, 1)
                wait(pool, k1t_out, b, 1)
                wait(pool, kv_out, b, 1)
                blocks(1, k1_t[:])
                features(1, kv1[:, :, 0:D])
                wait(pool, x2_out, b, TILES)
                nc.gpsimd.tensor_tensor(x2_bo[:], x2[:], bo_s[:].unsqueeze(1).broadcast_to([P, TILES, D]),
                                        ALU.add).then_inc(x2b_out.sem, 1)

        @block.scalar
        def _(act):
            act.dma_start(wq_s[:], wq_t).then_inc(s_proj_w, 16)
            act.dma_start(bq_s[:], bq.partition_broadcast(P)).then_inc(s_proj_w, 16)
            act.dma_start(wo_s[:], wo_t).then_inc(s_proj_w, 16)
            act.dma_start(bo_s[:], bo.partition_broadcast(P)).then_inc(s_proj_w, 16)
            act.dma_start(wp_s[:], wp).then_inc(s_proj_w, 16)
            act.dma_start(bp_s[:], bp_col).then_inc(s_proj_w, 16)
            act.dma_start(cent_s[:], cent).then_inc(s_proj_w, 16)
            act.wait_ge(s_cent, 1)
            nc.scalar.activation(cent_n[:, 1:2], cent_n[:, 0:1], ACT.Sqrt).then_inc(s_cent_a, 1)
            act.wait_ge(s_exp_w1, 16)
            nc.scalar.activation(ew1_hi[:], ew1_raw, ACT.Copy, scale=W1_SCALE).then_inc(s_ew1, 1)
            with act.Fori(0, BATCH) as b:

                def root_of_variance(n):
                    wait(act, ln_mom[n], b, 2 * TILES)
                    nc.scalar.activation(std[:], mean_var[:, :, 1], ACT.Sqrt).then_inc(ln_std[n].sem, 1)

                def k_operands(l):
                    wait(act, kf_t[l], b, 1)
                    src = bank16(4 + l).rearrange("p (c g k) -> p c g k", c=2, g=GROUPS)
                    if l == 0:
                        act.wait_ge(s_pool_set, 4)
                    for j in range(PER_GROUP):
                        quad = slice(QUAD * j, QUAD * (j + 1))
                        nc.scalar.activation(k_main[l][quad, j::PER_GROUP, :], src[quad, 0],
                                             ACT.Copy).then_inc(k_ready[l].sem, 1)
                        nc.scalar.activation(k_rest[l][quad, :, quad], src[quad, 1, :, quad],
                                             ACT.Copy).then_inc(k_ready[l].sem, 1)

                def values(l, src):
                    v_by_head = src.rearrange("p c (h d) -> p c h d", d=HD)
                    nc.scalar.activation(v_main[l][:, :, 0:HD], v_by_head[:, 0], ACT.Copy).then_inc(v_ready[l].sem, 1)
                    for j in range(PER_GROUP):
                        quad = slice(QUAD * j, QUAD * (j + 1))
                        nc.scalar.activation(v_rest[l][quad, j::PER_GROUP, 0:HD], v_by_head[quad, 1, j::PER_GROUP],
                                             ACT.Copy).then_inc(v_ready[l].sem, 1)

                def attention(l):
                    wait(act, q_split[l], b, 1)
                    for part in (slice(0, HD), slice(2 * HD, 3 * HD)):
                        nc.scalar.activation(q_feat[:, :, :, part], q_hi[:].rearrange("p t (h d) -> p t h d", d=HD),
                                             ACT.Copy).then_inc(q_hi2[l].sem, 1)
                    wait(act, qh_t[l], b, 1)
                    nc.scalar.activation(q_hi_t[:], bank16(6)[:, 0:SEQ], ACT.Copy).then_inc(qh_out[l].sem, 1)
                    for t in range(TILES):
                        wait(act, qf_t[l], b, t + 1)
                        nc.scalar.activation(q_op[:, :, t * P:(t + 1) * P],
                                             bank16(4 + t % 2)[:, 0:SEQ].rearrange("p (g k) -> p g k", g=GROUPS),
                                             ACT.Copy).then_inc(q_out[l].sem, 1)
                    for k in range(PAIRS):
                        wait(act, s_key[l], b, k + 1)
                        last = (2 * k + 1 - 10) // 5
                        if 2 * k + 1 >= 10:
                            wait(act, pv[l], b, last + 1)
                        slot = 2 * k % 10
                        nc.scalar.activation(probs[:, slot:slot + 2, :],
                                             bank(2 * (k % 2), 2).rearrange("p (c t) -> p c t", c=2),
                                             ACT.Exp).then_inc(exped[l].sem, 1)

                root_of_variance(0)
                wait(act, ctx_loaded, b, 32)
                act.wait_ge(s_memset, 7)
                values(0, ctx_k[:])
                k_operands(0)
                wait(act, kv_mm, b, 1)
                nc.scalar.activation(k1_t[:], bank(7)[:, 0:KEYS], ACT.Identity,
                                     bias=bk_s[:, 0:1]).then_inc(k1t_out.sem, 1)
                attention(0)
                root_of_variance(1)
                wait(act, xq_tr, b, 1)
                nc.scalar.activation(xq_t[:], bank16(6)[:, 0:SEQ], ACT.Copy).then_inc(xqt_out.sem, 1)
                wait(act, step_mm, b, 1)
                nc.scalar.activation(step_row[:], bank(7), ACT.Copy).then_inc(step_out.sem, 1)
                for c in range(CH):
                    wait(act, h_scaled, b, c + 1)
                    nc.scalar.activation(h_conv[:, c], h_pad[:, c, 0:SEQ], ACT.Identity, bias=cb[:, c:c + 1],
                                         scale=cw[:, c, 0:1]).then_inc(tap0.sem, 1)
                k_operands(1)
                wait(act, kv_out, b, 1)
                values(1, kv1[:, :, D:2 * D])
                for c in range(CH):
                    wait(act, taps, b, 2 * c + 2)
                    nc.scalar.activation(h_act[:, c], h_conv[:, c], ACT.Silu).then_inc(silu.sem, 1)
                for t in range(TILES):
                    wait(act, hq_tr, b, t + 1)
                    nc.scalar.activation(hq_t[:, t].rearrange("p c k -> p (c k)"), bank16(t)[:, 0:HIDDEN],
                                         ACT.Copy).then_inc(hqt_out.sem, 1)

                root_of_variance(2)
                wait(act, xn1_tr, b, 1)
                nc.scalar.activation(xn_t[:], bank(0), ACT.Copy).then_inc(xn1_out.sem, 1)
                attention(1)
                wait(act, a_tr, b, 1)
                nc.scalar.activation(attn_t[:], bank(4), ACT.Copy).then_inc(at_out.sem, 1)

                root_of_variance(3)
                wait(act, xn2_tr, b, 1)
                nc.scalar.activation(x_hi[:], bank(6), ACT.Copy).then_inc(xn2_out.sem, 1)
                nc.scalar.activation(xn_t[:], bank(6), ACT.Copy).then_inc(xn2_out.sem, 1)
                wait(act, z_mm, b, 1)
                nc.scalar.activation(z_t[:], bank(7), ACT.Identity, bias=bp_s[:, 0:1]).then_inc(z_out.sem, 1)
                nc.scalar.activation(z_sq[:], bank(7), ACT.Square, bias=bp_s[:, 0:1]).then_inc(z_out.sem, 1)
                wait(act, route, b, 1)
                nc.scalar.activation(r1[:, 1], r1[:, 0], ACT.Sqrt).then_inc(route_n.sem, 1)
                wait(act, route, b, 19)
                nc.scalar.activation(r8[:, 5], r8[:, 4], ACT.Sqrt).then_inc(route_u.sem, 1)
                for e in range(EXPERTS):
                    for c in range(CH):
                        n = CH * e + c
                        wait(act, h_mm, b, n + 1)
                        if e >= 2:
                            wait(act, y_mm, b, e - 1)
                        nc.scalar.activation(hidden[:, e % 2, c], bank(n % 2), ACT.Gelu, bias=eb1[:, n:n + 1],
                                             scale=1.0 / W1_SCALE).then_inc(gelu.sem, 1)

        @block.vector
        def _(dve):
            for l in range(2):
                nc.vector.memset(k_feat[l][:].rearrange("p c h f -> p (c h f)").bitcast(F32), 0.0).then_inc(s_wabs, 1)
                nc.vector.memset(v_main[l][:], 0.0).then_inc(s_wabs, 1)
                nc.vector.memset(v_rest[l][:], 0.0).then_inc(s_wabs, 1)
            nc.vector.memset(q_feat[:].rearrange("p t h f -> p (t h f)").bitcast(F32), 0.0).then_inc(s_wabs, 1)
            nc.vector.memset(ones[:], 1.0).then_inc(s_wabs, 1)
            nc.vector.memset(h_pad[:, :, 0:SEQ + 2:SEQ + 1], 0.0).then_inc(s_wabs, 1)
            dve.wait_ge(s_wabs, 9)
            for l in range(2):
                shift_part = slice(3 * HD, 3 * HD + 2)
                nc.vector.memset(k_feat[l][:, 0, :, shift_part], 1.0).then_inc(s_wabs, 1)
                nc.vector.memset(v_main[l][:, :, HD:HD + 1], 1.0).then_inc(s_wabs, 1)
                for j in range(PER_GROUP):
                    rows = slice(QUAD * j, QUAD * j + REST)
                    nc.vector.memset(k_feat[l][rows, 1, :, shift_part], 1.0).then_inc(s_wabs, 1)
                    nc.vector.memset(v_rest[l][rows, j::PER_GROUP, HD:HD + 1], 1.0).then_inc(s_wabs, 1)
            dve.wait_ge(s_wabs, 29)
            for n in range(7):
                nc.vector.memset(top[:], 0.0).then_inc(s_memset, 1)
                dve.wait_ge(s_memset, n + 1)
            dve.wait_ge(s_const, 48)
            nc.vector.tensor_copy(ident16[:], ident[:]).then_inc(s_ident, 1)
            nc.vector.tensor_scalar(mask_diag[:], ident[:], MASKED, None, ALU.mult).then_inc(s_ident, 1)

            dve.wait_ge(s_bit_w, 64)
            nc.vector.tensor_reduce(abs_sums[:, 0:1], w1_raw[:], AX_X, ALU.add,
                                    apply_absolute_value=True).then_inc(s_bit, 1)
            nc.vector.tensor_reduce(abs_sums[:, 1:2], w2_raw[:].rearrange("p c d -> p (c d)"), AX_X, ALU.add,
                                    apply_absolute_value=True).then_inc(s_bit, 1)
            dve.wait_ge(s_wsum, 1)
            nc.vector.tensor_scalar(w_mean[:], bank(0)[:, 0:2], 1.0 / (HIDDEN * D), 1e-5, ALU.mult,
                                    ALU.max).then_inc(s_bit, 1)
            dve.wait_ge(s_bit, 3)
            nc.vector.reciprocal(w_scale[:], w_mean[:]).then_inc(s_bit, 1)
            dve.wait_ge(s_bit, 4)
            nc.vector.reciprocal(w_step[:], w_scale[:]).then_inc(s_bit, 1)
            done = 5
            for n, (raw, bit) in enumerate(((w1_raw[:], bit_w1[:]),
                                            (w2_raw[:].rearrange("p c d -> p (c d)"),
                                             bit_w2[:].rearrange("p c d -> p (c d)")))):
                nc.vector.tensor_scalar(raw, raw, w_scale[:, n:n + 1], ROUND, ALU.mult, ALU.add).then_inc(s_bit, 1)
                dve.wait_ge(s_bit, done + 1)
                nc.vector.tensor_scalar(raw, raw, ROUND, 1.0, ALU.subtract, ALU.min).then_inc(s_bit, 1)
                dve.wait_ge(s_bit, done + 2)
                nc.vector.tensor_scalar(bit, raw, -1.0, None, ALU.max).then_inc(s_bit, 1)
                done += 3

            dve.wait_ge(s_proj_w, 16 * 7)
            dve.wait_ge(s_kv_w, 16 * 13)
            nc.vector.tensor_tensor(cent_sq[:], cent_s[:], cent_s[:], ALU.mult).then_inc(s_cent_pe, 1)
            dve.wait_ge(s_cent_pe, 1)
            nc.vector.tensor_reduce(cent_n[:, 0:1], cent_sq[:], AX_X, ALU.add).then_inc(s_cent, 1)
            dve.wait_ge(s_cent_a, 1)
            nc.vector.tensor_scalar(cent_n[:, 1:2], cent_n[:, 1:2], 1e-7, None, ALU.max).then_inc(s_cent, 1)
            dve.wait_ge(s_cent, 2)
            nc.vector.reciprocal(cent_n[:, 2:3], cent_n[:, 1:2]).then_inc(s_cent, 1)
            dve.wait_ge(s_cent, 3)
            nc.vector.tensor_scalar(cent_n[:, 2:3], cent_n[:, 2:3], 0.95, 1.0, ALU.mult, ALU.min).then_inc(s_cent, 1)
            dve.wait_ge(s_cent, 4)
            nc.vector.tensor_scalar(cent_s[:], cent_s[:], cent_n[:, 2:3], None, ALU.mult).then_inc(s_cent, 1)
            dve.wait_ge(s_cent_pe, 2)
            nc.vector.tensor_copy(cent_t[:], bank(1)[:, 0:EXPERTS]).then_inc(s_cent, 1)
            dve.wait_ge(s_cent, 6)
            nc.vector.tensor_tensor(cent_t_sq[:], cent_t[:], cent_t[:], ALU.mult).then_inc(s_cent, 1)
            dve.wait_ge(s_cent_pe, 3)
            nc.vector.tensor_scalar(c_norm[:], bank(2)[:, 0:EXPERTS], 0.99, None, ALU.min).then_inc(s_cent, 1)
            dve.wait_ge(s_cent, 8)
            nc.vector.tensor_scalar(c_rest[:], c_norm[:], -1.0, 1.0, ALU.mult, ALU.add).then_inc(s_cent, 1)
            nc.vector.tensor_scalar(bq_s[:], bq_s[:], HD ** -0.5, None, ALU.mult).then_inc(s_cent, 1)
            dve.wait_ge(s_cent, 10)
            dve.wait_ge(s_ew1, 1)
            nc.vector.scalar_tensor_tensor(out=ew1_lo[:].rearrange("p e f -> p (e f)"),
                                           in0=big[:, 0:EXPERTS * HIDDEN], scalar=W1_SCALE,
                                           in1=ew1_hi[:].rearrange("p e f -> p (e f)"), op0=ALU.mult,
                                           op1=ALU.subtract).then_inc(s_ew1_lo, 1)

            with dve.Fori(0, BATCH) as b:

                def layernorm(n, src, dst, scale=None):
                    for t in range(TILES):
                        nc.vector.bn_stats(moments[:, t], src[:, t]).then_inc(ln_mom[n].sem, 1)
                    wait(dve, ln_mom[n], b, TILES)
                    nc.vector.memset(gate[:], 0.0)
                    for t in range(TILES):
                        nc.vector.bn_aggr(mean_var[:, t], moments[:, t]).then_inc(ln_mom[n].sem, 1)
                    wait(dve, ln_std[n], b, 1)
                    nc.vector.reciprocal(rstd[:], std[:]).then_inc(ln_rstd[n].sem, 1)
                    wait(dve, ln_rstd[n], b, 1)
                    nc.vector.tensor_scalar(rstd[:], rstd[:], scale or 1.0, None, ALU.mult).then_inc(ln_rstd[n].sem, 1)
                    wait(dve, ln_rstd[n], b, 2)
                    for t in range(TILES):
                        nc.vector.tensor_scalar(dst[:, t], src[:, t], mean_var[:, t, 0:1], rstd[:, t:t + 1],
                                                ALU.subtract, ALU.mult).then_inc(ln_out[n].sem, 1)
                    wait(dve, ln_out[n], b, TILES)

                def split_q(l):
                    nc.vector.tensor_copy(q_hi[:], q_f[:]).then_inc(q_split[l].sem, 1)
                    wait(dve, q_split[l], b, 1)
                    nc.vector.tensor_tensor(q_feat[:, :, :, HD:2 * HD], q_f[:].rearrange("p t (h d) -> p t h d", d=HD),
                                            q_hi[:].rearrange("p t (h d) -> p t h d", d=HD),
                                            ALU.subtract).then_inc(q_split[l].sem, 1)

                def attention(l):
                    for t in range(TILES):
                        for p in range(3):
                            m = 3 * t + p
                            (h0, n), _ = MAX_HEADS[2 * p], MAX_HEADS[2 * p + 1]
                            wait(dve, s_tok[l], b, m + 1)
                            scores = bank(2 * (m % 2), 2).rearrange("p (c x) -> p c x", c=2)[:, :, 0:n * KEYS]
                            nc.vector.tensor_reduce(neg_max[:, t, h0:h0 + 2 * n].rearrange("p (c h) -> p c h", c=2),
                                                    scores.rearrange("p c (h k) -> p c h k", k=KEYS), AX_X, ALU.max,
                                                    negate=True).then_inc(maxed[l].sem, 1)
                        wait(dve, maxed[l], b, 3 * t + 3)
                        nc.vector.tensor_copy(q_feat[:, t, :, 3 * HD], neg_max[:, t]).then_inc(shift[l].sem, 1)
                        wait(dve, shift[l], b, 2 * t + 1)
                        nc.vector.tensor_tensor(q_feat[:, t, :, 3 * HD + 1], neg_max[:, t], q_feat[:, t, :, 3 * HD],
                                                ALU.subtract).then_inc(shift[l].sem, 1)
                    for g in range(GROUPS):
                        wait(dve, pv[l], b, g + 1)
                        nc.vector.tensor_copy(o_t[:, g], bank(6 + g % 2)).then_inc(o_out[l].sem, 1)
                    wait(dve, o_tok[l], b, 1)
                    o = bank(0, 4).rearrange("p (s f) -> p s f", f=QUAD)
                    nc.vector.reciprocal(denom[:], o[:, :, HD]).then_inc(attn_out[l].sem, 1)
                    wait(dve, attn_out[l], b, 1)
                    nc.vector.tensor_tensor(attn[:].rearrange("p t (h d) -> p (t h) d", d=HD), o[:, :, 0:HD],
                                            denom[:].unsqueeze(2).broadcast_to([P, TILES * HEADS, HD]),
                                            ALU.mult).then_inc(attn_out[l].sem, 1)
                    wait(dve, attn_out[l], b, 2)

                wait(dve, x_loaded, b, 16)
                layernorm(0, x_in, q_f, scale=HD ** -0.5)
                split_q(0)
                wait(dve, kv_mm, b, 1)
                nc.vector.tensor_tensor(kv1[:].rearrange("p c n -> p (c n)"), bank(6), kv_bias[:].rearrange(
                    "p c n -> p (c n)"), ALU.add).then_inc(kv_out.sem, 1)
                attention(0)
                nc.vector.tensor_tensor(x1[:], x_in[:], attn[:], ALU.add).then_inc(x1_out.sem, 1)
                wait(dve, x1_out, b, 1)

                layernorm(1, x1, xn)
                nc.vector.tensor_reduce(top[:], xn[:], AX_X, ALU.max,
                                        apply_absolute_value=True).then_inc(xq_scale.sem, 1)
                wait(dve, xq_scale, b, 1)
                nc.vector.tensor_scalar(top[:], top[:], 1e-5, None, ALU.max).then_inc(xq_scale.sem, 1)
                wait(dve, xq_scale, b, 2)
                nc.vector.reciprocal(a_scale[:], top[:]).then_inc(xq_scale.sem, 1)
                wait(dve, xq_scale, b, 3)
                nc.vector.tensor_scalar(a_scale[:], a_scale[:], 127.0, None, ALU.mult).then_inc(xq_scale.sem, 1)
                wait(dve, xq_scale, b, 4)
                for t in range(TILES):
                    nc.vector.tensor_scalar(x_whole[:, t], xn[:, t], a_scale[:, t:t + 1], ROUND, ALU.mult,
                                            ALU.add).then_inc(xq_out.sem, 1)
                nc.vector.reciprocal(a_step[:], a_scale[:]).then_inc(xq_scale.sem, 1)
                wait(dve, xq_out, b, TILES)
                nc.vector.tensor_scalar(xq[:], x_whole[:], ROUND, None, ALU.subtract).then_inc(xq_out.sem, 1)
                wait(dve, xq_scale, b, 5)
                for t in range(TILES):
                    nc.vector.tensor_scalar(step_diag[:, t], ident[:], a_step[:, t:t + 1], w_step[:, 0:1], ALU.mult,
                                            ALU.mult).then_inc(diag_out.sem, 1)
                wait(dve, step_out, b, 1)
                for c in range(CH):
                    wait(dve, up, b, c + 1)
                    nc.vector.tensor_tensor(h_pad[:, c, 1:SEQ + 1], bank(c), step_row[:],
                                            ALU.mult).then_inc(h_scaled.sem, 1)
                for c in range(CH):
                    wait(dve, tap0, b, c + 1)
                    for k in (1, 2):
                        if k == 2:
                            wait(dve, taps, b, 2 * c + 1)
                        else:
                            wait(dve, h_scaled, b, c + 1)
                        nc.vector.scalar_tensor_tensor(out=h_conv[:, c], in0=h_pad[:, c, k:SEQ + k],
                                                       scalar=cw[:, c, k:k + 1], in1=h_conv[:, c], op0=ALU.mult,
                                                       op1=ALU.add).then_inc(taps.sem, 1)
                wait(dve, h_tr, b, CH)
                nc.vector.tensor_reduce(top[:], bank(4, 4).rearrange("p (t f) -> p t f", t=TILES), AX_X, ALU.max,
                                        apply_absolute_value=True).then_inc(hq_scale.sem, 1)
                wait(dve, hq_scale, b, 1)
                nc.vector.tensor_scalar(top[:], top[:], 1e-5, None, ALU.max).then_inc(hq_scale.sem, 1)
                wait(dve, hq_scale, b, 2)
                nc.vector.reciprocal(a_scale[:], top[:]).then_inc(hq_scale.sem, 1)
                wait(dve, hq_scale, b, 3)
                nc.vector.tensor_scalar(a_scale[:], a_scale[:], 127.0, None, ALU.mult).then_inc(hq_scale.sem, 1)
                wait(dve, hq_scale, b, 4)
                for t in range(TILES):
                    nc.vector.tensor_scalar(h_whole[:, t], bank(4 + t), a_scale[:, t:t + 1], ROUND, ALU.mult,
                                            ALU.add).then_inc(hq_out.sem, 1)
                    wait(dve, hq_out, b, 2 * t + 1)
                    nc.vector.tensor_scalar(hq[:, t], h_whole[:, t], ROUND, None,
                                            ALU.subtract).then_inc(hq_out.sem, 1)
                nc.vector.reciprocal(a_step[:], a_scale[:]).then_inc(hq_scale.sem, 1)
                wait(dve, hq_scale, b, 5)
                nc.vector.tensor_scalar(a_step[:], a_step[:], w_step[:, 1:2], None,
                                        ALU.mult).then_inc(hq_scale.sem, 1)
                wait(dve, hq_scale, b, 6)
                for t in range(TILES):
                    wait(dve, down, b, t + 1)
                    nc.vector.scalar_tensor_tensor(out=x2[:, t], in0=bank(4 + t)[:, 0:D], scalar=a_step[:, t:t + 1],
                                                   in1=x1[:, t], op0=ALU.mult, op1=ALU.add).then_inc(x2_out.sem, 1)
                wait(dve, x2_out, b, TILES)

                layernorm(2, x2, xn)
                wait(dve, q_mm, b, 1)
                nc.vector.scalar_tensor_tensor(out=q_f[:], in0=bank(1).rearrange("p (t d) -> p t d", t=TILES),
                                               scalar=HD ** -0.5, in1=bq_s[:].unsqueeze(1).broadcast_to([P, TILES, D]),
                                               op0=ALU.mult, op1=ALU.add).then_inc(q_ready.sem, 1)
                wait(dve, q_ready, b, 1)
                split_q(1)
                attention(1)
                wait(dve, o_mm, b, 1)
                wait(dve, x2b_out, b, 1)
                nc.vector.tensor_tensor(x3[:], bank(5).rearrange("p (t d) -> p t d", t=TILES), x2_bo[:],
                                        ALU.add).then_inc(x3_out.sem, 1)
                wait(dve, x3_out, b, 1)

                layernorm(3, x3, xn)
                wait(dve, xn2_out, b, 2)
                nc.vector.tensor_tensor(x_lo[:], xn_t[:], x_hi[:], ALU.subtract).then_inc(xlo_out.sem, 1)
                wait(dve, dots, b, 1)
                step = [0]

                def then(instruction):
                    step[0] += 1
                    instruction.then_inc(route.sem, 1)
                    wait(dve, route, b, step[0])

                per_token = bank(4)[:, 0:16 * TILES].rearrange("p (t f) -> p t f", f=16)

                def spread(a):
                    return a.unsqueeze(2).broadcast_to([P, TILES, EXPERTS])

                def all_tokens(a):
                    return a.unsqueeze(1).broadcast_to([P, TILES, EXPERTS])

                then(nc.vector.tensor_copy(r1[:, 0], per_token[:, :, EXPERTS]))
                wait(dve, route_n, b, 1)
                then(nc.vector.tensor_scalar(r1[:, 1], r1[:, 1], 1e-7, None, ALU.max))
                then(nc.vector.reciprocal(r1[:, 2], r1[:, 1]))
                then(nc.vector.tensor_scalar(r1[:, 2], r1[:, 2], 0.95, 1.0, ALU.mult, ALU.min))
                then(nc.vector.tensor_tensor(r1[:, 3], r1[:, 0], r1[:, 2], ALU.mult))
                then(nc.vector.tensor_tensor(r1[:, 3], r1[:, 3], r1[:, 2], ALU.mult))
                then(nc.vector.tensor_scalar(r1[:, 3], r1[:, 3], 0.99, None, ALU.min))
                then(nc.vector.tensor_scalar(r1[:, 4], r1[:, 3], -1.0, 1.0, ALU.mult, ALU.add))
                then(nc.vector.tensor_tensor(r8[:, 0], per_token[:, :, 0:EXPERTS], spread(r1[:, 2]), ALU.mult))
                then(nc.vector.tensor_tensor(r8[:, 1], all_tokens(c_norm[:]), spread(r1[:, 3]), ALU.add))
                then(nc.vector.scalar_tensor_tensor(out=r8[:, 1], in0=r8[:, 0], scalar=-2.0, in1=r8[:, 1],
                                                    op0=ALU.mult, op1=ALU.add))
                then(nc.vector.tensor_scalar(r8[:, 1], r8[:, 1], 0.0, 2.0, ALU.max, ALU.mult))
                then(nc.vector.tensor_tensor(r8[:, 2], all_tokens(c_rest[:]), spread(r1[:, 4]), ALU.mult))
                then(nc.vector.tensor_scalar(r8[:, 2], r8[:, 2], 1e-7, None, ALU.add))
                then(nc.vector.reciprocal(r8[:, 2], r8[:, 2]))
                then(nc.vector.tensor_tensor(r8[:, 3], r8[:, 1], r8[:, 2], ALU.mult))
                then(nc.vector.tensor_scalar(r8[:, 3], r8[:, 3], 1.0, 1.0 + 1e-7, ALU.add, ALU.max))
                then(nc.vector.tensor_scalar(r8[:, 6], r8[:, 3], 1.0, None, ALU.add))
                then(nc.vector.scalar_tensor_tensor(out=r8[:, 4], in0=r8[:, 3], scalar=-1.0, in1=r8[:, 6],
                                                    op0=ALU.add, op1=ALU.mult))
                wait(dve, route_u, b, 1)
                then(nc.vector.scalar_tensor_tensor(out=r8[:, 5], in0=r8[:, 5], scalar=-1.0, in1=r8[:, 3],
                                                    op0=ALU.mult, op1=ALU.subtract))
                nc.vector.memset(gate[:], 0.0)
                for t in range(TILES):
                    nc.vector.max(best[:, t], r8[:, 5, t]).then_inc(route.sem, 1)
                step[0] += TILES
                wait(dve, route, b, step[0])
                nc.vector.memset(gate[:], 0.0)
                for t in range(TILES):
                    nc.vector.max_index(best_i[:, t], best[:, t], r8[:, 5, t]).then_inc(route.sem, 1)
                step[0] += TILES
                wait(dve, route, b, step[0])
                then(nc.vector.tensor_copy(best_f[:], best_i[:]))
                then(nc.vector.tensor_tensor(r1[:, 5], best[:, :, 0], best[:, :, 1], ALU.add))
                then(nc.vector.reciprocal(r1[:, 5], r1[:, 5]))
                then(nc.vector.tensor_tensor(r1[:, 6], best[:, :, 1], r1[:, 5], ALU.mult))
                then(nc.vector.tensor_tensor(r1[:, 7], best[:, :, 0], r1[:, 5], ALU.mult))
                for n in range(2):
                    target = comb[:] if n == 0 else r8[:, 6]
                    then(nc.vector.tensor_tensor(target, all_tokens(iota8[:]), spread(best_f[:, :, n]),
                                                 ALU.is_equal))
                    then(nc.vector.tensor_tensor(target, target, spread(r1[:, 6 + n]), ALU.mult))
                then(nc.vector.tensor_tensor(comb[:], comb[:], r8[:, 6], ALU.add))
                assert step[0] == ROUTE_STEPS, step[0]

                wait(dve, comb_tr, b, 1)
                nc.vector.tensor_copy(comb_t[:], bank(5)[0:EXPERTS, :]).then_inc(combt_out.sem, 1)
                wait(dve, b2_mm, b, 1)
                wait(dve, out_free, b, 0)
                nc.vector.tensor_tensor(y_sum[:], bank(6).rearrange("p (t d) -> p t d", t=TILES), x3[:],
                                        ALU.add).then_inc(y_used.sem, 1)
                for e in range(EXPERTS):
                    wait(dve, y_mm, b, e + 1)
                    for t in range(TILES):
                        wait(dve, y_used, b, 1 if e == 0 else 1 + TILES * (e - 1) + t + 1)
                        nc.vector.scalar_tensor_tensor(out=y_sum[:, t], in0=bank(2 + e % 2)[:, t * D:(t + 1) * D],
                                                       scalar=comb[:, t, e:e + 1], in1=y_sum[:, t], op0=ALU.mult,
                                                       op1=ALU.add).then_inc(y_used.sem, 1)

        @block.tensor
        def _(pe):
            pe.wait_ge(s_memset, 7)
            pe.wait_ge(s_bit, 2)
            nc.tensor.matmul(bank(0)[:, 0:2], ones[:], abs_sums[:], start=True, stop=True).then_inc(s_wsum, 1)
            pe.wait_ge(s_cent, 5)
            nc.tensor.transpose(bank(1)[:, 0:EXPERTS], cent_s[:], ident[0:EXPERTS, 0:EXPERTS]).then_inc(s_cent_pe, 1)
            pe.wait_ge(s_cent, 7)
            nc.tensor.matmul(bank(2)[:, 0:EXPERTS], ones[:], cent_t_sq[:], start=True, stop=True).then_inc(s_cent_pe, 1)
            pe.wait_ge(s_ident, 2)
            pe.wait_ge(s_cent, 10)

            with pe.Fori(0, BATCH) as b:

                def key_features(l):
                    wait(pe, kf_ready[l], b, 3)
                    for c in range(2):
                        for g in range(GROUPS):
                            mm = nc.tensor.transpose(bank16(4 + l)[:, (4 * c + g) * P:(4 * c + g + 1) * P],
                                                     k_feat[l][:, c, 4 * g:4 * g + 4, :].rearrange("p h f -> p (h f)"),
                                                     ident16[:])
                    mm.then_inc(kf_t[l].sem, 1)

                def score_pair(l, k):
                    if k >= 2:
                        wait(pe, exped[l], b, k - 1)
                    for slot in range(2):
                        n = 2 * k + slot
                        g, j = divmod(n, 5)
                        keys, c = (k_main[l][:, 4 * g + j], 0) if j < 4 else (k_rest[l][:, g], 1)
                        dst = bank(2 * (k % 2) + slot)
                        mm = nc.tensor.matmul(dst, keys, q_op[:, g], start=True, stop=(l == 1))
                        if l == 0:
                            mm = nc.tensor.matmul(dst, mask_diag[:], m_key[:, c], start=False, stop=True)
                    mm.then_inc(s_key[l].sem, 1)

                def weighted_values(l, g):
                    wait(pe, exped[l], b, (5 * g + 4) // 2 + 1)
                    if g >= 2:
                        wait(pe, o_out[l], b, g - 1)
                    if g == 0:
                        wait(pe, v_ready[l], b, 5)
                    for c in range(2):
                        for j in range(PER_GROUP):
                            quad = slice(QUAD * j, QUAD * (j + 1))
                            n = 5 * g + (j if c == 0 else 4)
                            mm = nc.tensor.matmul(bank(6 + g % 2)[quad, :], (v_rest if c else v_main)[l][:, 4 * g + j, :],
                                                  probs[:, n % 10, :], start=(c == 0), stop=(c == 1),
                                                  tile_position=(0, QUAD * j))
                    mm.then_inc(pv[l].sem, 1)

                def attention(l):
                    wait(pe, q_split[l], b, 1)
                    for t in range(TILES):
                        mm = nc.tensor.transpose(bank16(6)[:, t * P:(t + 1) * P], q_hi[:, t], ident16[:])
                    mm.then_inc(qh_t[l].sem, 1)
                    wait(pe, kb_ready[l], b, 1)
                    wait(pe, qh_out[l], b, 1)
                    if l == 0:
                        wait(pe, masks, b, 1)

                    def feature_transposes(t):
                        wait(pe, shift[l], b, 2 * t + 2)
                        if t == 0:
                            wait(pe, q_hi2[l], b, 2)
                            wait(pe, q_split[l], b, 2)
                        if t >= 2:
                            wait(pe, q_out[l], b, t - 1)
                        for g in range(GROUPS):
                            mm = nc.tensor.transpose(bank16(4 + t % 2)[:, g * P:(g + 1) * P],
                                                     q_feat[:, t, 4 * g:4 * g + 4, :].rearrange("p h f -> p (h f)"),
                                                     ident16[:])
                        mm.then_inc(qf_t[l].sem, 1)

                    for t in range(TILES):
                        for p in range(3):
                            m = 3 * t + p
                            if m >= 2:
                                wait(pe, maxed[l], b, m - 1)
                            for s in range(2):
                                h0, n = MAX_HEADS[2 * p + s]
                                dst = bank(2 * (m % 2) + s)[:, 0:n * KEYS]
                                mm = nc.tensor.matmul(dst, q_hi_t[:, t * P:(t + 1) * P],
                                                      k_blocks[l][:, h0:h0 + n, :].rearrange("p h k -> p (h k)"),
                                                      start=True, stop=(l == 1))
                                if l == 0:
                                    mm = nc.tensor.matmul(dst.rearrange("p (h k) -> p h k", k=KEYS), mask_diag[:],
                                                          m_tok[:, t].unsqueeze(1).broadcast_to([P, n, KEYS]),
                                                          start=False, stop=True)
                            mm.then_inc(s_tok[l].sem, 1)
                        if t >= 1:
                            feature_transposes(t - 1)
                    feature_transposes(TILES - 1)
                    wait(pe, q_out[l], b, TILES)
                    wait(pe, k_ready[l], b, 2 * PER_GROUP)
                    if l == 0:
                        wait(pe, masks, b, 2)
                    k = 0
                    for g, ahead in enumerate((5, 7, 9, 10)):
                        while k < ahead:
                            score_pair(l, k)
                            k += 1
                        weighted_values(l, g)
                    wait(pe, o_out[l], b, GROUPS)
                    for t in range(TILES):
                        for g in range(GROUPS):
                            mm = nc.tensor.transpose(bank(t)[:, g * P:(g + 1) * P], o_t[:, g, t * P:(t + 1) * P],
                                                     ident[:])
                    mm.then_inc(o_tok[l].sem, 1)

                def turn(dst, src):
                    for t in range(TILES):
                        mm = nc.tensor.transpose(dst[:, t * P:(t + 1) * P], src[:, t],
                                                 ident[:] if dst.dtype == F32 else ident16[:])
                    return mm

                key_features(0)
                wait(pe, ctx_loaded, b, 32)
                pe.wait_ge(s_proj_w, 16 * 7)
                pe.wait_ge(s_kv_w, 16 * 13)
                for c in range(2):
                    nc.tensor.matmul(bank(6)[:, c * 2 * D:(c + 1) * 2 * D], ctx_t[:, c * KEYS:c * KEYS + P], wkv_s[:],
                                     start=True, stop=True)
                nc.tensor.matmul(bank(7)[:, 0:KEYS], wkv_s[:, 0:D], ctx_t[:, 0:KEYS], start=True,
                                 stop=True).then_inc(kv_mm.sem, 1)
                wait(pe, kv_out, b, 1)
                wait(pe, k1t_out, b, 1)
                attention(0)

                wait(pe, xq_out, b, TILES + 1)
                turn(bank16(6), xq).then_inc(xq_tr.sem, 1)
                wait(pe, diag_out, b, TILES)
                nc.tensor.matmul(bank(7), ones[:], step_diag[:].rearrange("p t k -> p (t k)"), start=True,
                                 stop=True).then_inc(step_mm.sem, 1)
                wait(pe, xqt_out, b, 1)
                for c in range(CH):
                    nc.tensor.matmul(bank(c), bit_w1[:, c * P:(c + 1) * P], xq_t[:], start=True,
                                     stop=True).then_inc(up.sem, 1)
                wait(pe, q_out[0], b, TILES)
                key_features(1)
                wait(pe, k_ready[1], b, 2 * PER_GROUP)
                for c in range(CH):
                    wait(pe, silu, b, c + 1)
                    for t in range(TILES):
                        mm = nc.tensor.transpose(bank(4 + t)[:, c * P:(c + 1) * P], h_act[:, c, t * P:(t + 1) * P],
                                                 ident[:])
                    mm.then_inc(h_tr.sem, 1)
                for t in range(TILES):
                    wait(pe, hq_out, b, 2 * t + 2)
                    for c in range(CH):
                        mm = nc.tensor.transpose(bank16(t)[:, c * P:(c + 1) * P], hq[:, t, c * P:(c + 1) * P],
                                                 ident16[:])
                    mm.then_inc(hq_tr.sem, 1)
                for t in range(TILES):
                    wait(pe, hqt_out, b, t + 1)
                    for c in range(CH):
                        mm = nc.tensor.matmul(bank(4 + t)[:, 0:D], hq_t[:, t, c], bit_w2[:, c], start=(c == 0),
                                              stop=(c == CH - 1))
                    mm.then_inc(down.sem, 1)

                wait(pe, ln_out[2], b, TILES)
                turn(bank(0), xn).then_inc(xn1_tr.sem, 1)
                wait(pe, xn1_out, b, 1)
                for t in range(TILES):
                    mm = nc.tensor.matmul(bank(1)[:, t * D:(t + 1) * D], xn_t[:, t * P:(t + 1) * P], wq_s[:],
                                          start=True, stop=True)
                mm.then_inc(q_mm.sem, 1)
                attention(1)
                wait(pe, attn_out[1], b, 2)
                turn(bank(4), attn).then_inc(a_tr.sem, 1)
                wait(pe, at_out, b, 1)
                for t in range(TILES):
                    mm = nc.tensor.matmul(bank(5)[:, t * D:(t + 1) * D], attn_t[:, t * P:(t + 1) * P], wo_s[:],
                                          start=True, stop=True)
                mm.then_inc(o_mm.sem, 1)

                wait(pe, ln_out[3], b, TILES)
                turn(bank(6), xn).then_inc(xn2_tr.sem, 1)
                wait(pe, xn2_out, b, 2)
                nc.tensor.matmul(bank(7), wp_s[:], xn_t[:], start=True, stop=True).then_inc(z_mm.sem, 1)
                wait(pe, z_out, b, 2)
                for t in range(TILES):
                    tokens = slice(t * P, (t + 1) * P)
                    nc.tensor.matmul(bank(4)[:, 16 * t:16 * t + EXPERTS], z_t[:, tokens], cent_t[:], start=True,
                                     stop=True)
                    mm = nc.tensor.matmul(bank(4)[:, 16 * t + EXPERTS:16 * t + EXPERTS + 1], z_sq[:, tokens],
                                          ones[:, 0:1], start=True, stop=True)
                mm.then_inc(dots.sem, 1)
                wait(pe, xlo_out, b, 1)
                pe.wait_ge(s_ew1_lo, 1)
                pe.wait_ge(s_exp_rest, 48)

                def expert_out(e, t):
                    if t == 0:
                        wait(pe, gelu, b, CH * (e + 1))
                        if e >= 2:
                            wait(pe, y_used, b, 1 + TILES * (e - 1))
                    for c in range(CH):
                        mm = nc.tensor.matmul(bank(2 + e % 2)[:, t * D:(t + 1) * D],
                                              hidden[:, e % 2, c, t * P:(t + 1) * P], ew2[:, e, c], start=(c == 0),
                                              stop=(c == CH - 1))
                    if t == TILES - 1:
                        mm.then_inc(y_mm.sem, 1)

                for e in range(EXPERTS):
                    for c in range(CH):
                        n = CH * e + c
                        if n >= 2:
                            wait(pe, gelu, b, n - 1)
                        w = slice(c * P, (c + 1) * P)
                        nc.tensor.matmul(bank(n % 2), ew1_hi[:, e, w], x_hi[:], start=True, stop=False)
                        nc.tensor.matmul(bank(n % 2), ew1_hi[:, e, w], x_lo[:], start=False, stop=False)
                        nc.tensor.matmul(bank(n % 2), ew1_lo[:, e, w], x_hi[:], start=False,
                                         stop=True).then_inc(h_mm.sem, 1)
                        if e >= 1:
                            expert_out(e - 1, c)
                    if e == 1:
                        wait(pe, route, b, ROUTE_STEPS)
                        for t in range(TILES):
                            mm = nc.tensor.transpose(bank(5)[0:EXPERTS, t * P:(t + 1) * P], comb[:, t], ident[:])
                        mm.then_inc(comb_tr.sem, 1)
                        wait(pe, combt_out, b, 1)
                        for t in range(TILES):
                            mm = nc.tensor.matmul(bank(6)[:, t * D:(t + 1) * D], comb_t[:, t * P:(t + 1) * P],
                                                  eb2[:], start=True, stop=True)
                        mm.then_inc(b2_mm.sem, 1)
                for t in range(TILES):
                    expert_out(EXPERTS - 1, t)


def kernel(x, ctx_1024, mask_BxSxS2_bk1, L0_ffn_w1, L0_ffn_conv_w, L0_ffn_conv_b, L0_ffn_w2, L1_xattn_Wq, L1_xattn_bq,
           L1_xattn_Wk, L1_xattn_bk, L1_xattn_Wv, L1_xattn_bv, L1_xattn_Wo, L1_xattn_bo, L1_ffn_centroids, L1_ffn_Wp,
           L1_ffn_bp, L1_ffn_W1, L1_ffn_b1, L1_ffn_W2, L1_ffn_b2):
    import concourse.bacc as _bacc
    from concourse.bass_utils import run_bass_kernel_spmd as _run

    ctx = np.asarray(ctx_1024)
    mask = np.asarray(mask_BxSxS2_bk1)
    ctx_rest = np.zeros((BATCH, PER_GROUP, QUAD, D), ctx.dtype)
    ctx_rest[:, :, :REST] = ctx[:, None, P:]
    ctx_rest = ctx_rest.reshape(BATCH, P, D)
    mask_rest = np.zeros((BATCH, PER_GROUP, QUAD, SEQ), mask.dtype)
    mask_rest[:, :, :REST] = mask.transpose(0, 2, 1)[:, None, P:]
    mask_t = np.stack([mask.transpose(0, 2, 1)[:, :P], mask_rest.reshape(BATCH, P, SEQ)], axis=2)
    arrays = {
        "x": x,
        "ctxt": np.concatenate([ctx.transpose(0, 2, 1), ctx_rest.transpose(0, 2, 1)], axis=2),
        "ctx_km": np.stack([ctx[:, :P], ctx_rest], axis=2),
        "mask_tm": mask,
        "mask_t": mask_t,
        "w1t": np.asarray(L0_ffn_w1).T,
        "conv_w": np.asarray(L0_ffn_conv_w).reshape(HIDDEN, 3),
        "conv_b": np.asarray(L0_ffn_conv_b).reshape(CH, P).T,
        "w2t": np.asarray(L0_ffn_w2).T,
        "wq_t": np.asarray(L1_xattn_Wq).T, "bq": L1_xattn_bq,
        "wk_t": np.asarray(L1_xattn_Wk).T, "bk": L1_xattn_bk, "bk_col": np.asarray(L1_xattn_bk).reshape(D, 1),
        "wv_t": np.asarray(L1_xattn_Wv).T, "bv": L1_xattn_bv,
        "wo_t": np.asarray(L1_xattn_Wo).T, "bo": L1_xattn_bo,
        "cent": L1_ffn_centroids,
        "wp": L1_ffn_Wp, "bp_col": np.asarray(L1_ffn_bp).reshape(D, 1),
        "moe_w1": L1_ffn_W1,
        "moe_b1": np.asarray(L1_ffn_b1).reshape(EXPERTS * CH, P).T,
        "moe_w2": L1_ffn_W2, "moe_b2": L1_ffn_b2,
        "ident_in": np.eye(P, dtype=np.float32),
        "blocks_in": np.kron(np.eye(HEADS, dtype=np.float32), np.ones((HD, 1), np.float32)),
        "iota_in": np.tile(np.arange(EXPERTS, dtype=np.float32), (P, 1)),
    }
    arrays = {f"{n}_dram": np.ascontiguousarray(a) for n, a in arrays.items()}
    nc = _bacc.Bacc("TRN2", target_bir_lowering=False, num_devices=1)
    args = [nc.dram_tensor(n, a.shape, mybir.dt.from_np(a.dtype), kind="ExternalInput").ap()
            for n, a in arrays.items()]
    out = nc.dram_tensor("out_dram", (BATCH, SEQ, D), F32, kind="ExternalOutput").ap()
    build(nc, *args, out)
    r = _run(nc, [arrays], core_ids=[0])
    return r.results[0]["out_dram"]
```

```python
from contextlib import ExitStack

import numpy as np

import concourse.bass as bass
from concourse import mybir

F32 = mybir.dt.float32
F16 = mybir.dt.float16
U8 = mybir.dt.uint8
U32 = mybir.dt.uint32
ALU = mybir.AluOpType
ACT = mybir.ActivationFunctionType
AX_X = mybir.AxisListType.X

P = 128
BATCH, SEQ, D = 4, 512, 128
KEYS = 154
HEADS, HD = 16, 8
GROUPS, PER_GROUP = 4, 4
TILES = SEQ // P
REST = KEYS - P
QUAD = 32
HIDDEN = 512
CH = HIDDEN // P
EXPERTS = 8
ROUND = 12582912.0
W1_SCALE = 256.0
MASKED = -10000.0
LN_EPS = 1e-5
RING = 16
PAIRS = (CH + 1) * GROUPS // 2
I32 = mybir.dt.int32
RSQRT_GUESS = 1597463007
NEWTON = 3
LN_STEPS = 3 + 3 * NEWTON
CENTROID_STEPS = 11 + 3 * NEWTON
DISTANCE_STEPS = 17 + 2 + 3 * NEWTON
RANK_STEPS = DISTANCE_STEPS + 2 + 3 * NEWTON + 2 + 2 * TILES
ROUTE_STEPS = RANK_STEPS + 10
MAX_HEADS = ((0, 3), (3, 3), (6, 3), (9, 3), (12, 2), (14, 2))


EXPERT_STEPS = {"keys": 3, "max0_0": 1, "max0_1": 1, "max0_2": 1, "max0_3": 1, "quant": 7, "conv": 4, "hq": 4,
                "norm2": 4, "query1": 2, "max1_0": 1, "max1_1": 1, "max1_2": 1, "max1_3": 1, "out1": 1, "norm3": 3}
LAST_STEP = EXPERTS * CH + TILES
assert sum(EXPERT_STEPS.values()) == LAST_STEP
EXPERT_SPANS = {}
for _name, _n in EXPERT_STEPS.items():
    _at = sum(len(_r) for _r in EXPERT_SPANS.values())
    EXPERT_SPANS[_name] = range(_at, _at + _n)
EXPERT_ADDS = {name: range(e, e + 1) for e, name in
               enumerate(("quant", "steps", "conv", "hq", "norm2", "shift1", "exp1", "norm3"))}
LATE = 12


class Signal:

    def __init__(self, sem, per, first=0):
        self.sem, self.per, self.first = sem, per, first

    def at(self, b, k):
        return b * self.per + (k + self.first)


def build(nc, x, ctxt, ctx_km, mask_tm, mask_t, w1t, conv_w, conv_b, w2t, wq_t, bq, wk_t, bk, bk_col, wv_t, bv,
          wo_t, bo, cent, wp, bp_col, moe_w1, moe_b1, moe_w2, moe_b2, ident_in, blocks_in, iota_in, out):
    with ExitStack() as ctx:
        def sb(name, shape, dt=F32):
            return ctx.enter_context(nc.sbuf_tensor(name, shape, dt))

        def sem(name):
            return ctx.enter_context(nc.semaphore(name))

        def sig(name, per, first=0):
            return Signal(sem(name), per, first)

        ident = sb("ident", [P, P])
        ident16 = sb("ident16", [P, P], F16)
        mask_diag = sb("mask_diag", [P, P], F16)
        ones = sb("ones", [P, P])
        head_blocks = sb("head_blocks", [P, HEADS])
        iota8 = sb("iota8", [P, EXPERTS])
        bit_w1 = sb("bit_w1", [P, HIDDEN], F16)
        bit_w2 = sb("bit_w2", [P, CH, D], F16)
        abs_sums = sb("abs_sums", [P, 2])
        w_mean = sb("w_mean", [P, 2])
        w_scale = sb("w_scale", [P, 2])
        w_step = sb("w_step", [P, 2])
        cw = sb("cw", [P, CH, 3])
        cb = sb("cb", [P, CH])
        wq_s = sb("wq_s", [P, D])
        wkv_s = sb("wkv_s", [P, 2 * D])
        wo_s = sb("wo_s", [P, D])
        wp_s = sb("wp_s", [P, D])
        bq_s = sb("bq_s", [P, D])
        bo_s = sb("bo_s", [P, D])
        kv_bias = sb("kv_bias", [P, 2, 2 * D])
        bk_s = sb("bk_s", [P, 1])
        bp_s = sb("bp_s", [P, 1])
        cent_s = sb("cent_s", [EXPERTS, D])
        cent_sq = sb("cent_sq", [EXPERTS, D])
        cent_n = sb("cent_n", [EXPERTS, 3])
        cent_t = sb("cent_t", [P, EXPERTS])
        cent_t_sq = sb("cent_t_sq", [P, EXPERTS])
        c_norm = sb("c_norm", [P, EXPERTS])
        c_rest = sb("c_rest", [P, EXPERTS])
        ew1_hi = sb("ew1_hi", [P, EXPERTS, HIDDEN], F16)
        ew1_lo = sb("ew1_lo", [P, EXPERTS, HIDDEN], F16)
        ew2 = sb("ew2", [P, EXPERTS, CH, D])
        eb1 = sb("eb1", [P, EXPERTS * CH])
        eb2 = sb("eb2", [EXPERTS, D])

        x_in = sb("x_in", [P, TILES, D])
        ctx_t = sb("ctx_t", [P, KEYS + P])
        ctx_k = sb("ctx_k", [P, 2, D])
        m_tok8 = sb("m_tok8", [P, TILES, KEYS], U8)
        m_key8 = sb("m_key8", [P, 2, SEQ], U8)
        m_tok = sb("m_tok", [P, TILES, KEYS], F16)
        m_key = sb("m_key", [P, 2, SEQ], F16)

        k_blocks = [sb(f"k_blocks{l}", [P, HEADS, KEYS], F16) for l in range(2)]
        k_feat = [sb(f"k_feat{l}", [P, 2, HEADS, QUAD], F16) for l in range(2)]
        k_main = [sb(f"k_main{l}", [P, HEADS, P], F16) for l in range(2)]
        k_rest = [sb(f"k_rest{l}", [P, GROUPS, P], F16) for l in range(2)]
        v_main = [sb(f"v_main{l}", [P, HEADS, QUAD]) for l in range(2)]
        v_rest = [sb(f"v_rest{l}", [P, HEADS, QUAD]) for l in range(2)]
        kv1 = sb("kv1", [P, 2, 2 * D])
        k1_t = sb("k1_t", [P, KEYS])
        q_f = sb("q_f", [P, TILES, D])
        q_feat = sb("q_feat", [P, TILES, HEADS, QUAD], F16)
        q_hi = sb("q_hi", [P, TILES, D], F16)
        q_hi_t = sb("q_hi_t", [P, SEQ], F16)
        q_op = sb("q_op", [P, GROUPS, SEQ], F16)
        neg_max = sb("neg_max", [P, TILES, HEADS])
        probs = sb("probs", [P, RING, SEQ])
        w1_raw = probs[:, 0, :]
        w2_raw = probs[:, 1, :].rearrange("p (c d) -> p c d", c=CH)
        o_t = sb("o_t", [P, GROUPS, SEQ])
        denom = sb("denom", [P, TILES * HEADS])
        attn = sb("attn", [P, TILES, D])
        attn_t = sb("attn_t", [P, SEQ])

        gate = sb("gate", [P, 1])
        moments = sb("moments", [P, TILES, 6])
        mean_var = sb("mean_var", [P, TILES, 2])
        newton = sb("newton", [P, 3, TILES])
        rstd = sb("rstd", [P, TILES])
        newton8 = sb("newton8", [P, 3, TILES, EXPERTS])
        xn = sb("xn", [P, TILES, D])
        xn_t = sb("xn_t", [P, SEQ])
        x1 = sb("x1", [P, TILES, D])
        x2 = sb("x2", [P, TILES, D])
        x2_bo = sb("x2_bo", [P, TILES, D])
        x3 = sb("x3", [P, TILES, D])
        y_sum = sb("y_sum", [P, TILES, D])

        top = sb("top", [P, TILES])
        a_scale = sb("a_scale", [P, TILES])
        a_step = sb("a_step", [P, TILES])
        x_whole = sb("x_whole", [P, TILES, D])
        xq = sb("xq", [P, TILES, D], F16)
        xq_t = sb("xq_t", [P, SEQ], F16)
        step_diag = sb("step_diag", [P, TILES, P])
        step_row = sb("step_row", [P, SEQ])
        h_pad = sb("h_pad", [P, CH, SEQ + 2])
        h_conv = probs[:, CH:2 * CH, :]
        h_tanh = probs[:, 0:CH, :]
        h_whole = o_t
        hq = sb("hq", [P, TILES, HIDDEN], F16)
        hq_t = sb("hq_t", [P, TILES, CH, P], F16)

        x_hi = sb("x_hi", [P, SEQ], F16)
        x_lo = sb("x_lo", [P, SEQ], F16)
        z_t = sb("z_t", [P, SEQ])
        z_sq = sb("z_sq", [P, SEQ])
        u = sb("u", [P, TILES, EXPERTS])
        r1 = sb("r1", [P, 8, TILES])
        r8 = sb("r8", [P, 8, TILES, EXPERTS])
        best = sb("best", [P, TILES, 8])
        best_i = sb("best_i", [P, TILES, 8], U32)
        best_f = sb("best_f", [P, TILES, 8])
        comb = sb("comb", [P, TILES, EXPERTS])
        comb_t = sb("comb_t", [EXPERTS, SEQ])
        hidden = sb("hidden", [P, 2, CH, SEQ])
        ew1_raw = hidden[:].rearrange("p r c t -> p (r c t)")

        ps = ctx.enter_context(nc.psum_tensor("ps", [P, 8 * 512], F32))

        def bank(i, n=1):
            return ps[:, 512 * i:512 * (i + n)]

        def bank16(i):
            return bank(i).bitcast(F16)

        s_const = sem("s_const_loaded")
        s_bit_w = sem("s_bitnet_weights_loaded")
        s_proj_w = sem("s_projection_weights_loaded")
        s_kv_w = sem("s_key_value_weights_loaded")
        s_exp_w1 = sem("s_expert_w1_loaded")
        s_exp_rest = sem("s_expert_rest_loaded")
        s_memset = sem("s_memset")
        s_pool_set = sem("s_pool_memset")
        s_bias_set = sem("s_bias_cleared")
        s_ident = sem("s_identities")
        s_wabs = sem("s_weight_abs_sums")
        s_wsum = sem("s_weight_sums")
        s_bit = sem("s_bitnet_weights")
        s_cent = sem("s_centroids")
        s_cent_pe = sem("s_centroids_pe")
        s_ew1 = sem("s_expert_w1_high")
        s_ew1_lo = sem("s_expert_w1_low")

        x_loaded = sig("x_loaded", 16)
        ctx_loaded = sig("ctx_loaded", 32)
        mask_loaded = sig("mask_loaded", 32)
        stored = sig("stored", 16, 16)
        masks = sig("masks_converted", 2)
        kb_ready = [sig(f"k_blocks_ready{l}", 1) for l in range(2)]
        kf_ready = [sig(f"k_features_ready{l}", 3) for l in range(2)]
        v_ready = [sig(f"values_ready{l}", 5) for l in range(2)]
        kf_t = [sig(f"k_features_transposed{l}", 1) for l in range(2)]
        k_ready = [sig(f"k_operands_ready{l}", 8) for l in range(2)]
        kv_mm = sig("kv_projected", 1)
        kv_out = sig("kv_biased", 1)
        k1t_out = sig("k1_transposed_biased", 1)
        ln_mom = [sig(f"ln_moments{n}", 8) for n in range(4)]
        ln_rstd = [sig(f"ln_rstd{n}", LN_STEPS) for n in range(4)]
        ln_out = [sig(f"ln_out{n}", TILES) for n in range(4)]
        q_ready = sig("q_projected_scaled", 1)
        q_split = [sig(f"q_split{l}", 2) for l in range(2)]
        q_hi2 = [sig(f"q_hi_copied{l}", 2) for l in range(2)]
        qh_t = [sig(f"q_hi_transposed{l}", 1) for l in range(2)]
        qh_out = [sig(f"q_hi_ready{l}", 1) for l in range(2)]
        s_tok = [sig(f"token_scores{l}", 3 * TILES) for l in range(2)]
        maxed = [sig(f"maxima{l}", 3 * TILES) for l in range(2)]
        shift = [sig(f"shift_features{l}", 2 * TILES) for l in range(2)]
        qf_t = [sig(f"q_features_transposed{l}", TILES) for l in range(2)]
        q_out = [sig(f"q_operand_ready{l}", TILES) for l in range(2)]
        s_key = [sig(f"key_scores{l}", PAIRS) for l in range(2)]
        exped = [sig(f"exponentials{l}", PAIRS) for l in range(2)]
        pv = [sig(f"weighted_values{l}", GROUPS) for l in range(2)]
        o_out = [sig(f"weighted_values_copied{l}", GROUPS) for l in range(2)]
        o_tok = [sig(f"outputs_by_token{l}", 1) for l in range(2)]
        attn_out = [sig(f"attention_normalised{l}", 2) for l in range(2)]
        x1_out = sig("x1_ready", 1)
        xq_scale = sig("xq_scale", 5)
        xq_out = sig("xq_ready", 5)
        diag_out = sig("step_diagonals", TILES)
        xq_tr = sig("xq_transposed", 1)
        xqt_out = sig("xq_t_ready", 1)
        step_mm = sig("step_row_product", 1)
        step_out = sig("step_row_ready", 1)
        up = sig("bitnet_up_product", CH)
        h_scaled = sig("h_scaled", CH)
        tap0 = sig("conv_tap0", CH)
        taps = sig("conv_taps", 2 * CH)
        tanh = sig("tanh", CH)
        silu = sig("silu_twice", CH)
        h_tr = sig("h_transposed", CH)
        hq_scale = sig("hq_scale", 6)
        hq_out = sig("hq_ready", 2 * TILES)
        hq_tr = sig("hq_transposed", TILES)
        hqt_out = sig("hq_t_ready", TILES)
        down = sig("bitnet_down_product", TILES)
        x2_out = sig("x2_ready", TILES)
        x2b_out = sig("x2_with_bias", 1)
        xn1_tr = sig("xn_transposed1", 1)
        xn1_out = sig("xn_t_ready1", 1)
        q_mm = sig("q_product", 1)
        a_tr = sig("attention_transposed", 1)
        at_out = sig("attention_t_ready", 1)
        o_mm = sig("output_product", 1)
        x3_out = sig("x3_ready", 1)
        xn2_tr = sig("xn_transposed2", 1)
        xn2_out = sig("xn_t_ready2", 2)
        xlo_out = sig("x_lo_ready", 1)
        z_mm = sig("z_product", 1)
        z_out = sig("z_ready", 2)
        dots = sig("centroid_dots", 1)
        dots_out = sig("centroid_dots_copied", 2)
        route = sig("routing_steps", ROUTE_STEPS)
        comb_tr = sig("comb_transposed", 1)
        combt_out = sig("comb_t_ready", 1)
        b2_mm = sig("expert_bias_product", 1)
        h_mm = sig("expert_hidden_product", EXPERTS * CH)
        gelu = sig("gelu", EXPERTS * CH)
        y_mm = sig("expert_output", EXPERTS)
        y_used = sig("expert_output_added", 1 + TILES * EXPERTS)

        def wait(eng, signal, b, k):
            eng.wait_ge(signal.sem, signal.at(b, k))

        block = ctx.enter_context(nc.Block())

        @block.sync
        def _(sp):
            sp.sem_inc(stored.sem, 16)

            def load_batch(b):
                sp.dma_start(x_in[:], x[b].rearrange("(t p) d -> p t d", p=P)).then_inc(x_loaded.sem, 16)
                sp.dma_start(ctx_t[:], ctxt[b]).then_inc(ctx_loaded.sem, 16)
                sp.dma_start(ctx_k[:], ctx_km[b]).then_inc(ctx_loaded.sem, 16)
                sp.dma_start(m_tok8[:], mask_tm[b].rearrange("(t p) k -> p t k", p=P)).then_inc(mask_loaded.sem, 16)
                sp.dma_start(m_key8[:], mask_t[b]).then_inc(mask_loaded.sem, 16)

            load_batch(0)
            sp.dma_start(w1_raw, w1t).then_inc(s_bit_w, 16)
            sp.dma_start(w2_raw, w2t.rearrange("(c p) d -> p c d", p=P)).then_inc(s_bit_w, 16)
            sp.dma_start(cw[:], conv_w.rearrange("(c p) k -> p c k", p=P)).then_inc(s_bit_w, 16)
            sp.dma_start(cb[:], conv_b).then_inc(s_bit_w, 16)
            sp.dma_start(ew1_raw.rearrange("p (e f) -> p e f", e=EXPERTS), moe_w1.rearrange("e d f -> d e f")).then_inc(s_exp_w1, 16)
            sp.dma_start(ew2[:], moe_w2.rearrange("e (c p) d -> p e c d", p=P)).then_inc(s_exp_rest, 16)
            sp.dma_start(eb1[:], moe_b1).then_inc(s_exp_rest, 16)
            sp.dma_start(eb2[:], moe_b2).then_inc(s_exp_rest, 16)

            def load_next(b):
                wait(sp, x1_out, b - 1, 1)
                load_batch(b)

            def store(m):
                wait(sp, y_used, m, 1 + TILES * EXPERTS)
                sp.dma_start(out[m].rearrange("(t p) d -> p t d", p=P), y_sum[:]).then_inc(stored.sem, 16)

            load_next(1)
            with sp.Fori(2, BATCH) as b:
                load_next(b)
                store(b - 2)
            store(BATCH - 2)
            store(BATCH - 1)
            sp.wait_ge(stored.sem, 16 * (BATCH + 1))

        @block.gpsimd
        def _(pool):
            for n, t in enumerate([*k_main, *k_rest]):
                nc.gpsimd.memset(t[:].rearrange("p a b -> p (a b)").bitcast(F32), 0.0).then_inc(s_pool_set, 1)
            nc.gpsimd.memset(kv_bias[:], 0.0).then_inc(s_bias_set, 1)
            pool.dma_start(ident[:], ident_in).then_inc(s_const, 16)
            pool.dma_start(head_blocks[:], blocks_in).then_inc(s_const, 16)
            pool.dma_start(iota8[:], iota_in).then_inc(s_const, 16)
            pool.dma_start(wkv_s[:, 0:D], wk_t).then_inc(s_kv_w, 16)
            pool.dma_start(wkv_s[:, D:2 * D], wv_t).then_inc(s_kv_w, 16)
            pool.dma_start(bk_s[:], bk_col).then_inc(s_kv_w, 16)
            pool.wait_ge(s_bias_set, 1)
            for c, vec in enumerate((bk, bv)):
                part = slice(c * D, (c + 1) * D)
                pool.dma_start(kv_bias[:, 0, part], vec.partition_broadcast(P)).then_inc(s_kv_w, 16)
                for j in range(PER_GROUP):
                    pool.dma_start(kv_bias[QUAD * j:QUAD * j + REST, 1, part],
                                   vec.partition_broadcast(REST)).then_inc(s_kv_w, 16)
            pool.wait_ge(s_const, 48)
            pool.wait_ge(s_memset, 7)
            with pool.Fori(0, BATCH) as b:

                def blocks(l, k_t):
                    nc.gpsimd.tensor_tensor(k_blocks[l][:], k_t.unsqueeze(1).broadcast_to([P, HEADS, KEYS]),
                                            head_blocks[:].unsqueeze(2).broadcast_to([P, HEADS, KEYS]),
                                            ALU.mult).then_inc(kb_ready[l].sem, 1)

                def features(l, keys):
                    by_head = keys.rearrange("p c (h d) -> p c h d", d=HD)
                    nc.gpsimd.tensor_copy(k_feat[l][:, :, :, 0:HD], by_head).then_inc(kf_ready[l].sem, 1)
                    nc.gpsimd.tensor_copy(k_feat[l][:, :, :, HD:2 * HD], by_head).then_inc(kf_ready[l].sem, 1)
                    wait(pool, kf_ready[l], b, 1)
                    nc.gpsimd.tensor_tensor(k_feat[l][:, :, :, 2 * HD:3 * HD], by_head, k_feat[l][:, :, :, 0:HD],
                                            ALU.subtract).then_inc(kf_ready[l].sem, 1)

                wait(pool, ctx_loaded, b, 32)
                wait(pool, mask_loaded, b, 32)
                blocks(0, ctx_t[:, 0:KEYS])
                nc.gpsimd.tensor_copy(m_tok[:], m_tok8[:]).then_inc(masks.sem, 1)
                features(0, ctx_k[:])
                nc.gpsimd.tensor_copy(m_key[:], m_key8[:]).then_inc(masks.sem, 1)
                wait(pool, k1t_out, b, 1)
                wait(pool, kv_out, b, 1)
                blocks(1, k1_t[:])
                features(1, kv1[:, :, 0:D])
                wait(pool, x2_out, b, TILES)
                nc.gpsimd.tensor_tensor(x2_bo[:], x2[:], bo_s[:].unsqueeze(1).broadcast_to([P, TILES, D]),
                                        ALU.add).then_inc(x2b_out.sem, 1)

        @block.scalar
        def _(act):
            act.dma_start(wq_s[:], wq_t).then_inc(s_proj_w, 16)
            act.dma_start(bq_s[:], bq.partition_broadcast(P)).then_inc(s_proj_w, 16)
            act.dma_start(wo_s[:], wo_t).then_inc(s_proj_w, 16)
            act.dma_start(bo_s[:], bo.partition_broadcast(P)).then_inc(s_proj_w, 16)
            act.dma_start(wp_s[:], wp).then_inc(s_proj_w, 16)
            act.dma_start(bp_s[:], bp_col).then_inc(s_proj_w, 16)
            act.dma_start(cent_s[:], cent).then_inc(s_proj_w, 16)

            def routing_operands(m):
                wait(act, xn2_tr, m, 1)
                nc.scalar.activation(x_hi[:], bank(2), ACT.Copy).then_inc(xn2_out.sem, 1)
                nc.scalar.activation(xn_t[:], bank(2), ACT.Copy).then_inc(xn2_out.sem, 1)
                wait(act, z_mm, m, 1)
                nc.scalar.activation(z_t[:], bank(3), ACT.Identity, bias=bp_s[:, 0:1]).then_inc(z_out.sem, 1)
                nc.scalar.activation(z_sq[:], bank(3), ACT.Square, bias=bp_s[:, 0:1]).then_inc(z_out.sem, 1)

            def weights_by_expert(m):
                wait(act, comb_tr, m, 1)
                nc.scalar.activation(comb_t[:], bank(4)[0:EXPERTS, :], ACT.Copy).then_inc(combt_out.sem, 1)

            def gelus(m, steps):
                for n in steps:
                    if n < EXPERTS * CH:
                        e, c = divmod(n, CH)
                        wait(act, h_mm, m, n + 1)
                        if e >= 2:
                            wait(act, y_mm, m, e - 1)
                        nc.scalar.activation(hidden[:, e % 2, c], bank(5), ACT.Gelu, bias=eb1[:, n:n + 1],
                                             scale=1.0 / W1_SCALE).then_inc(gelu.sem, 1)

            def turn(b, experts):
                def experts_at(point, part=slice(None)):
                    if experts:
                        gelus(b - 1, EXPERT_SPANS[point][part])

                def k_operands(l):
                    wait(act, kf_t[l], b, 1)
                    src = bank16(4).rearrange("p (c g k) -> p c g k", c=2, g=GROUPS)
                    if l == 0:
                        act.wait_ge(s_pool_set, 4)
                    for j in range(PER_GROUP):
                        quad = slice(QUAD * j, QUAD * (j + 1))
                        nc.scalar.activation(k_main[l][quad, j::PER_GROUP, :], src[quad, 0],
                                             ACT.Copy).then_inc(k_ready[l].sem, 1)
                        nc.scalar.activation(k_rest[l][quad, :, quad], src[quad, 1, :, quad],
                                             ACT.Copy).then_inc(k_ready[l].sem, 1)

                def values(l, src):
                    v_by_head = src.rearrange("p c (h d) -> p c h d", d=HD)
                    nc.scalar.activation(v_main[l][:, :, 0:HD], v_by_head[:, 0], ACT.Copy).then_inc(v_ready[l].sem, 1)
                    for j in range(PER_GROUP):
                        quad = slice(QUAD * j, QUAD * (j + 1))
                        nc.scalar.activation(v_rest[l][quad, j::PER_GROUP, 0:HD], v_by_head[quad, 1, j::PER_GROUP],
                                             ACT.Copy).then_inc(v_ready[l].sem, 1)

                def attention(l):
                    wait(act, q_split[l], b, 1)
                    for part in (slice(0, HD), slice(2 * HD, 3 * HD)):
                        nc.scalar.activation(q_feat[:, :, :, part], q_hi[:].rearrange("p t (h d) -> p t h d", d=HD),
                                             ACT.Copy).then_inc(q_hi2[l].sem, 1)
                    wait(act, qh_t[l], b, 1)
                    nc.scalar.activation(q_hi_t[:], bank16(4)[:, 0:SEQ], ACT.Copy).then_inc(qh_out[l].sem, 1)

                    def q_operand(t):
                        wait(act, qf_t[l], b, t + 1)
                        nc.scalar.activation(q_op[:, :, t * P:(t + 1) * P],
                                             bank16(4)[:, 0:SEQ].rearrange("p (g k) -> p g k", g=GROUPS),
                                             ACT.Copy).then_inc(q_out[l].sem, 1)

                    for t in range(TILES):
                        experts_at(f"max{l}_{t}")
                        if t >= 1:
                            q_operand(t - 1)
                    q_operand(TILES - 1)
                    for k in range(PAIRS):
                        wait(act, s_key[l], b, k + 1)
                        if 2 * k + 1 >= RING:
                            wait(act, pv[l], b, (2 * k + 1 - RING) // 5 + 1)
                        slot = 2 * k % RING
                        nc.scalar.activation(probs[:, slot:slot + 2, :],
                                             bank(2 * (k % 2), 2).rearrange("p (c t) -> p c t", c=2),
                                             ACT.Exp).then_inc(exped[l].sem, 1)

                wait(act, ctx_loaded, b, 32)
                act.wait_ge(s_memset, 7)
                values(0, ctx_k[:])
                k_operands(0)
                wait(act, kv_mm, b, 1)
                nc.scalar.activation(k1_t[:], bank(1)[:, 0:KEYS], ACT.Identity,
                                     bias=bk_s[:, 0:1]).then_inc(k1t_out.sem, 1)
                if experts:
                    routing_operands(b - 1)
                experts_at("keys")
                attention(0)

                if experts:
                    weights_by_expert(b - 1)
                else:
                    act.wait_ge(s_exp_w1, 16)
                    nc.scalar.activation(ew1_hi[:].rearrange("p e f -> p (e f)"), ew1_raw, ACT.Copy,
                                         scale=W1_SCALE).then_inc(s_ew1, 1)
                experts_at("quant")
                wait(act, xq_tr, b, 1)
                nc.scalar.activation(xq_t[:], bank16(0)[:, 0:SEQ], ACT.Copy).then_inc(xqt_out.sem, 1)
                wait(act, step_mm, b, 1)
                nc.scalar.activation(step_row[:], bank(4), ACT.Copy).then_inc(step_out.sem, 1)
                for c in range(CH):
                    wait(act, h_scaled, b, c + 1)
                    nc.scalar.activation(h_conv[:, c], h_pad[:, c, 0:SEQ], ACT.Identity, bias=cb[:, c:c + 1],
                                         scale=cw[:, c, 0:1]).then_inc(tap0.sem, 1)
                experts_at("conv", slice(0, 2))
                k_operands(1)
                experts_at("conv", slice(2, None))
                for c in range(CH):
                    wait(act, taps, b, 2 * c + 2)
                    nc.scalar.activation(h_tanh[:, c], h_conv[:, c], ACT.Tanh, scale=0.5).then_inc(tanh.sem, 1)
                experts_at("hq")
                for t in range(TILES):
                    wait(act, hq_tr, b, t + 1)
                    nc.scalar.activation(hq_t[:, t].rearrange("p c k -> p (c k)"), bank16(4)[:, 0:HIDDEN],
                                         ACT.Copy).then_inc(hqt_out.sem, 1)

                experts_at("norm2")
                wait(act, kv_out, b, 1)
                values(1, kv1[:, :, D:2 * D])
                wait(act, xn1_tr, b, 1)
                nc.scalar.activation(xn_t[:], bank(4), ACT.Copy).then_inc(xn1_out.sem, 1)
                experts_at("query1")
                attention(1)
                experts_at("out1")
                wait(act, a_tr, b, 1)
                nc.scalar.activation(attn_t[:], bank(4), ACT.Copy).then_inc(at_out.sem, 1)

                experts_at("norm3")

            turn(0, False)
            with act.Fori(1, BATCH) as b:
                turn(b, True)
            routing_operands(BATCH - 1)
            gelus(BATCH - 1, range(LATE))
            weights_by_expert(BATCH - 1)
            gelus(BATCH - 1, range(LATE, LAST_STEP))

        @block.vector
        def _(dve):
            def inverse_root(then, a, root, t):
                then(nc.vector.tensor_scalar(root.bitcast(I32), a.bitcast(I32), 1, None, ALU.logical_shift_right))
                then(nc.vector.tensor_scalar(root.bitcast(I32), root.bitcast(I32), -1, RSQRT_GUESS, ALU.mult, ALU.add))
                for _ in range(NEWTON):
                    then(nc.vector.tensor_tensor(t, root, root, ALU.mult))
                    then(nc.vector.scalar_tensor_tensor(out=t, in0=t, scalar=-0.5, in1=a, op0=ALU.mult, op1=ALU.mult))
                    then(nc.vector.scalar_tensor_tensor(out=root, in0=t, scalar=1.5, in1=root, op0=ALU.add,
                                                        op1=ALU.mult))

            for l in range(2):
                nc.vector.memset(k_feat[l][:].rearrange("p c h f -> p (c h f)").bitcast(F32), 0.0).then_inc(s_wabs, 1)
                nc.vector.memset(v_main[l][:], 0.0).then_inc(s_wabs, 1)
                nc.vector.memset(v_rest[l][:], 0.0).then_inc(s_wabs, 1)
            nc.vector.memset(q_feat[:].rearrange("p t h f -> p (t h f)").bitcast(F32), 0.0).then_inc(s_wabs, 1)
            nc.vector.memset(ones[:], 1.0).then_inc(s_wabs, 1)
            nc.vector.memset(h_pad[:, :, 0:SEQ + 2:SEQ + 1], 0.0).then_inc(s_wabs, 1)
            dve.wait_ge(s_wabs, 9)
            for l in range(2):
                shift_part = slice(3 * HD, 3 * HD + 2)
                nc.vector.memset(k_feat[l][:, 0, :, shift_part], 1.0).then_inc(s_wabs, 1)
                nc.vector.memset(v_main[l][:, :, HD:HD + 1], 1.0).then_inc(s_wabs, 1)
                for j in range(PER_GROUP):
                    rows = slice(QUAD * j, QUAD * j + REST)
                    nc.vector.memset(k_feat[l][rows, 1, :, shift_part], 1.0).then_inc(s_wabs, 1)
                    nc.vector.memset(v_rest[l][rows, j::PER_GROUP, HD:HD + 1], 1.0).then_inc(s_wabs, 1)
            dve.wait_ge(s_wabs, 29)
            for n in range(7):
                nc.vector.memset(top[:], 0.0).then_inc(s_memset, 1)
                dve.wait_ge(s_memset, n + 1)
            dve.wait_ge(s_const, 48)
            nc.vector.tensor_copy(ident16[:], ident[:]).then_inc(s_ident, 1)
            nc.vector.tensor_scalar(mask_diag[:], ident[:], MASKED, None, ALU.mult).then_inc(s_ident, 1)

            dve.wait_ge(s_bit_w, 64)
            nc.vector.tensor_reduce(abs_sums[:, 0:1], w1_raw, AX_X, ALU.add,
                                    apply_absolute_value=True).then_inc(s_bit, 1)
            nc.vector.tensor_reduce(abs_sums[:, 1:2], probs[:, 1, :], AX_X, ALU.add,
                                    apply_absolute_value=True).then_inc(s_bit, 1)
            dve.wait_ge(s_wsum, 1)
            nc.vector.tensor_scalar(w_mean[:], bank(0)[:, 0:2], 1.0 / (HIDDEN * D), 1e-5, ALU.mult,
                                    ALU.max).then_inc(s_bit, 1)
            dve.wait_ge(s_bit, 3)
            nc.vector.reciprocal(w_scale[:], w_mean[:]).then_inc(s_bit, 1)
            dve.wait_ge(s_bit, 4)
            nc.vector.reciprocal(w_step[:], w_scale[:]).then_inc(s_bit, 1)
            done = 5
            for n, (raw, bit) in enumerate(((w1_raw, bit_w1[:]), (probs[:, 1, :], bit_w2[:].rearrange("p c d -> p (c d)")))):
                nc.vector.tensor_scalar(raw, raw, w_scale[:, n:n + 1], ROUND, ALU.mult, ALU.add).then_inc(s_bit, 1)
                dve.wait_ge(s_bit, done + 1)
                nc.vector.tensor_scalar(raw, raw, ROUND, 1.0, ALU.subtract, ALU.min).then_inc(s_bit, 1)
                dve.wait_ge(s_bit, done + 2)
                nc.vector.tensor_scalar(bit, raw, -1.0, None, ALU.max).then_inc(s_bit, 1)
                done += 3

            dve.wait_ge(s_proj_w, 16 * 7)
            dve.wait_ge(s_kv_w, 16 * 13)
            nc.vector.tensor_tensor(cent_sq[:], cent_s[:], cent_s[:], ALU.mult).then_inc(s_cent_pe, 1)
            dve.wait_ge(s_cent_pe, 1)
            nc.vector.tensor_reduce(cent_n[:, 0:1], cent_sq[:], AX_X, ALU.add).then_inc(s_cent, 1)
            dve.wait_ge(s_cent, 1)
            nc.vector.tensor_scalar(cent_n[:, 0:1], cent_n[:, 0:1], 1e-14, None, ALU.max).then_inc(s_cent, 1)
            dve.wait_ge(s_cent, 2)
            done = [2]

            def next_centroid_step(instruction):
                done[0] += 1
                instruction.then_inc(s_cent, 1)
                dve.wait_ge(s_cent, done[0])

            inverse_root(next_centroid_step, cent_n[:, 0:1], cent_n[:, 1:2], cent_n[:, 2:3])
            next_centroid_step(nc.vector.tensor_scalar(cent_n[:, 2:3], cent_n[:, 1:2], 0.95, 1.0, ALU.mult, ALU.min))
            next_centroid_step(nc.vector.tensor_scalar(cent_s[:], cent_s[:], cent_n[:, 2:3], None, ALU.mult))
            dve.wait_ge(s_cent_pe, 2)
            next_centroid_step(nc.vector.tensor_copy(cent_t[:], bank(1)[:, 0:EXPERTS]))
            next_centroid_step(nc.vector.tensor_tensor(cent_t_sq[:], cent_t[:], cent_t[:], ALU.mult))
            dve.wait_ge(s_cent_pe, 3)
            next_centroid_step(nc.vector.tensor_scalar(c_norm[:], bank(2)[:, 0:EXPERTS], 0.99, None, ALU.min))
            next_centroid_step(nc.vector.tensor_scalar(c_rest[:], c_norm[:], -1.0, 1.0, ALU.mult, ALU.add))
            next_centroid_step(nc.vector.tensor_scalar(bq_s[:], bq_s[:], HD ** -0.5, None, ALU.mult))
            assert done[0] == CENTROID_STEPS, done

            def spread(a):
                return a.unsqueeze(2).broadcast_to([P, TILES, EXPERTS])

            def all_tokens(a):
                return a.unsqueeze(1).broadcast_to([P, TILES, EXPERTS])

            def copy_dots(m):
                wait(dve, xn2_out, m, 2)
                nc.vector.tensor_tensor(x_lo[:], xn_t[:], x_hi[:], ALU.subtract).then_inc(xlo_out.sem, 1)
                wait(dve, dots, m, 1)
                per_token = bank(2)[:, 0:16 * TILES].rearrange("p (t f) -> p t f", f=16)
                nc.vector.tensor_copy(r8[:, 7], per_token[:, :, 0:EXPERTS]).then_inc(dots_out.sem, 1)
                nc.vector.tensor_copy(r1[:, 0], per_token[:, :, EXPERTS]).then_inc(dots_out.sem, 1)
                wait(dve, dots_out, m, 2)

            def stepper(m, first):
                step = [first]

                def then(instruction):
                    step[0] += 1
                    instruction.then_inc(route.sem, 1)
                    wait(dve, route, m, step[0])
                return step, then

            def route_distances(m):
                step, then = stepper(m, 0)
                then(nc.vector.tensor_scalar(r1[:, 1], r1[:, 0], 1e-14, None, ALU.max))
                inverse_root(then, r1[:, 1], r1[:, 2], r1[:, 5])
                then(nc.vector.tensor_scalar(r1[:, 2], r1[:, 2], 0.95, 1.0, ALU.mult, ALU.min))
                then(nc.vector.tensor_tensor(r1[:, 3], r1[:, 0], r1[:, 2], ALU.mult))
                then(nc.vector.tensor_tensor(r1[:, 3], r1[:, 3], r1[:, 2], ALU.mult))
                then(nc.vector.tensor_scalar(r1[:, 3], r1[:, 3], 0.99, None, ALU.min))
                then(nc.vector.tensor_scalar(r1[:, 4], r1[:, 3], -1.0, 1.0, ALU.mult, ALU.add))
                then(nc.vector.tensor_tensor(r8[:, 0], r8[:, 7], spread(r1[:, 2]), ALU.mult))
                then(nc.vector.tensor_tensor(r8[:, 1], all_tokens(c_norm[:]), spread(r1[:, 3]), ALU.add))
                then(nc.vector.scalar_tensor_tensor(out=r8[:, 1], in0=r8[:, 0], scalar=-2.0, in1=r8[:, 1],
                                                    op0=ALU.mult, op1=ALU.add))
                then(nc.vector.tensor_scalar(r8[:, 1], r8[:, 1], 0.0, 2.0, ALU.max, ALU.mult))
                then(nc.vector.tensor_tensor(r8[:, 2], all_tokens(c_rest[:]), spread(r1[:, 4]), ALU.mult))
                then(nc.vector.tensor_scalar(r8[:, 2], r8[:, 2], 1e-7, None, ALU.add))
                then(nc.vector.reciprocal(r8[:, 2], r8[:, 2]))
                then(nc.vector.tensor_tensor(r8[:, 3], r8[:, 1], r8[:, 2], ALU.mult))
                then(nc.vector.tensor_scalar(r8[:, 3], r8[:, 3], 1.0, 1.0 + 1e-7, ALU.add, ALU.max))
                then(nc.vector.tensor_scalar(r8[:, 6], r8[:, 3], 1.0, None, ALU.add))
                then(nc.vector.scalar_tensor_tensor(out=r8[:, 4], in0=r8[:, 3], scalar=-1.0, in1=r8[:, 6],
                                                    op0=ALU.add, op1=ALU.mult))
                assert step[0] == DISTANCE_STEPS, step[0]

            def route_ranks(m):
                step, then = stepper(m, DISTANCE_STEPS)
                inverse_root(then, r8[:, 4], r8[:, 5], r8[:, 6])
                then(nc.vector.tensor_tensor(r8[:, 5], r8[:, 5], r8[:, 4], ALU.mult))
                then(nc.vector.scalar_tensor_tensor(out=u[:], in0=r8[:, 5], scalar=-1.0, in1=r8[:, 3],
                                                    op0=ALU.mult, op1=ALU.subtract))
                nc.vector.memset(gate[:], 0.0)
                for t in range(TILES):
                    nc.vector.max(best[:, t], u[:, t]).then_inc(route.sem, 1)
                step[0] += TILES
                wait(dve, route, m, step[0])
                nc.vector.memset(gate[:], 0.0)
                for t in range(TILES):
                    nc.vector.max_index(best_i[:, t], best[:, t], u[:, t]).then_inc(route.sem, 1)
                step[0] += TILES
                wait(dve, route, m, step[0])
                assert step[0] == RANK_STEPS, step[0]

            def route_weights(m):
                step, then = stepper(m, RANK_STEPS)
                then(nc.vector.tensor_copy(best_f[:], best_i[:]))
                then(nc.vector.tensor_tensor(r1[:, 5], best[:, :, 0], best[:, :, 1], ALU.add))
                then(nc.vector.reciprocal(r1[:, 5], r1[:, 5]))
                then(nc.vector.tensor_tensor(r1[:, 6], best[:, :, 1], r1[:, 5], ALU.mult))
                then(nc.vector.tensor_tensor(r1[:, 7], best[:, :, 0], r1[:, 5], ALU.mult))
                for n in range(2):
                    target = comb[:] if n == 0 else r8[:, 6]
                    then(nc.vector.tensor_tensor(target, all_tokens(iota8[:]), spread(best_f[:, :, n]),
                                                 ALU.is_equal))
                    then(nc.vector.tensor_tensor(target, target, spread(r1[:, 6 + n]), ALU.mult))
                then(nc.vector.tensor_tensor(comb[:], comb[:], r8[:, 6], ALU.add))
                assert step[0] == ROUTE_STEPS, step[0]

            def start_sum(m):
                wait(dve, b2_mm, m, 1)
                wait(dve, stored, m, 0)
                nc.vector.tensor_tensor(y_sum[:], bank(4).rearrange("p (t d) -> p t d", t=TILES), x3[:],
                                        ALU.add).then_inc(y_used.sem, 1)

            def expert_adds(m, experts_range):
                for e in experts_range:
                    wait(dve, y_mm, m, e + 1)
                    for t in range(TILES):
                        wait(dve, y_used, m, 1 if e == 0 else 1 + TILES * (e - 1) + t + 1)
                        nc.vector.scalar_tensor_tensor(out=y_sum[:, t], in0=bank(6 + e % 2)[:, t * D:(t + 1) * D],
                                                       scalar=comb[:, t, e:e + 1], in1=y_sum[:, t], op0=ALU.mult,
                                                       op1=ALU.add).then_inc(y_used.sem, 1)

            def turn(b, experts):
                def experts_at(point):
                    if experts:
                        expert_adds(b - 1, EXPERT_ADDS[point])

                def layernorm(n, src, dst, shrink=1.0):
                    for t in range(TILES):
                        nc.vector.bn_stats(moments[:, t], src[:, t]).then_inc(ln_mom[n].sem, 1)
                    wait(dve, ln_mom[n], b, TILES)
                    nc.vector.memset(gate[:], 0.0)
                    for t in range(TILES):
                        nc.vector.bn_aggr(mean_var[:, t], moments[:, t]).then_inc(ln_mom[n].sem, 1)
                    wait(dve, ln_mom[n], b, 2 * TILES)
                    count = [0]

                    def then(instruction):
                        count[0] += 1
                        instruction.then_inc(ln_rstd[n].sem, 1)
                        wait(dve, ln_rstd[n], b, count[0])

                    then(nc.vector.tensor_scalar(newton[:, 0], mean_var[:, :, 1], LN_EPS, shrink, ALU.add, ALU.mult))
                    inverse_root(then, newton[:, 0], rstd[:], newton[:, 1])
                    assert count[0] == LN_STEPS
                    for t in range(TILES):
                        nc.vector.tensor_scalar(dst[:, t], src[:, t], mean_var[:, t, 0:1], rstd[:, t:t + 1],
                                                ALU.subtract, ALU.mult).then_inc(ln_out[n].sem, 1)
                    wait(dve, ln_out[n], b, TILES)

                def split_q(l):
                    nc.vector.tensor_copy(q_hi[:], q_f[:]).then_inc(q_split[l].sem, 1)
                    wait(dve, q_split[l], b, 1)
                    nc.vector.tensor_tensor(q_feat[:, :, :, HD:2 * HD], q_f[:].rearrange("p t (h d) -> p t h d", d=HD),
                                            q_hi[:].rearrange("p t (h d) -> p t h d", d=HD),
                                            ALU.subtract).then_inc(q_split[l].sem, 1)

                def attention(l, meanwhile):
                    for t in range(TILES):
                        for p in range(3):
                            m = 3 * t + p
                            (h0, n), _ = MAX_HEADS[2 * p], MAX_HEADS[2 * p + 1]
                            wait(dve, s_tok[l], b, m + 1)
                            scores = bank(2 * (m % 2), 2).rearrange("p (c x) -> p c x", c=2)[:, :, 0:n * KEYS]
                            nc.vector.tensor_reduce(neg_max[:, t, h0:h0 + 2 * n].rearrange("p (c h) -> p c h", c=2),
                                                    scores.rearrange("p c (h k) -> p c h k", k=KEYS), AX_X, ALU.max,
                                                    negate=True).then_inc(maxed[l].sem, 1)
                        wait(dve, maxed[l], b, 3 * t + 3)
                        nc.vector.tensor_copy(q_feat[:, t, :, 3 * HD], neg_max[:, t]).then_inc(shift[l].sem, 1)
                        wait(dve, shift[l], b, 2 * t + 1)
                        nc.vector.tensor_tensor(q_feat[:, t, :, 3 * HD + 1], neg_max[:, t], q_feat[:, t, :, 3 * HD],
                                                ALU.subtract).then_inc(shift[l].sem, 1)
                    if l == 1 and not experts:
                        dve.wait_ge(s_ew1, 1)
                        nc.vector.scalar_tensor_tensor(out=ew1_lo[:].rearrange("p e f -> p (e f)"), in0=ew1_raw,
                                                       scalar=W1_SCALE, in1=ew1_hi[:].rearrange("p e f -> p (e f)"),
                                                       op0=ALU.mult, op1=ALU.subtract).then_inc(s_ew1_lo, 1)
                    for g in range(GROUPS):
                        if experts:
                            meanwhile[g]()
                        wait(dve, pv[l], b, g + 1)
                        nc.vector.tensor_copy(o_t[:, g], bank(4)).then_inc(o_out[l].sem, 1)
                    wait(dve, o_tok[l], b, 1)
                    o = bank(0, 4).rearrange("p (s f) -> p s f", f=QUAD)
                    nc.vector.reciprocal(denom[:], o[:, :, HD]).then_inc(attn_out[l].sem, 1)
                    wait(dve, attn_out[l], b, 1)
                    nc.vector.tensor_tensor(attn[:].rearrange("p t (h d) -> p (t h) d", d=HD), o[:, :, 0:HD],
                                            denom[:].unsqueeze(2).broadcast_to([P, TILES * HEADS, HD]),
                                            ALU.mult).then_inc(attn_out[l].sem, 1)
                    wait(dve, attn_out[l], b, 2)

                wait(dve, x_loaded, b, 16)
                layernorm(0, x_in, q_f, shrink=float(HD))
                split_q(0)
                if experts:
                    copy_dots(b - 1)
                wait(dve, kv_mm, b, 1)
                nc.vector.tensor_tensor(kv1[:].rearrange("p c n -> p (c n)"), bank(0), kv_bias[:].rearrange(
                    "p c n -> p (c n)"), ALU.add).then_inc(kv_out.sem, 1)
                attention(0, [lambda: route_distances(b - 1), lambda: route_ranks(b - 1),
                              lambda: route_weights(b - 1), lambda: None])
                nc.vector.tensor_tensor(x1[:], x_in[:], attn[:], ALU.add).then_inc(x1_out.sem, 1)
                wait(dve, x1_out, b, 1)

                layernorm(1, x1, xn)
                if experts:
                    start_sum(b - 1)
                experts_at("quant")
                nc.vector.tensor_reduce(top[:], xn[:], AX_X, ALU.max,
                                        apply_absolute_value=True).then_inc(xq_scale.sem, 1)
                wait(dve, xq_scale, b, 1)
                nc.vector.tensor_scalar(top[:], top[:], 1e-5, None, ALU.max).then_inc(xq_scale.sem, 1)
                wait(dve, xq_scale, b, 2)
                nc.vector.reciprocal(a_scale[:], top[:]).then_inc(xq_scale.sem, 1)
                wait(dve, xq_scale, b, 3)
                nc.vector.tensor_scalar(a_scale[:], a_scale[:], 127.0, None, ALU.mult).then_inc(xq_scale.sem, 1)
                wait(dve, xq_scale, b, 4)
                for t in range(TILES):
                    nc.vector.tensor_scalar(x_whole[:, t], xn[:, t], a_scale[:, t:t + 1], ROUND, ALU.mult,
                                            ALU.add).then_inc(xq_out.sem, 1)
                nc.vector.reciprocal(a_step[:], a_scale[:]).then_inc(xq_scale.sem, 1)
                wait(dve, xq_out, b, TILES)
                nc.vector.tensor_scalar(xq[:], x_whole[:], ROUND, None, ALU.subtract).then_inc(xq_out.sem, 1)
                wait(dve, xq_scale, b, 5)
                for t in range(TILES):
                    nc.vector.tensor_scalar(step_diag[:, t], ident[:], a_step[:, t:t + 1], w_step[:, 0:1], ALU.mult,
                                            ALU.mult).then_inc(diag_out.sem, 1)
                experts_at("steps")
                wait(dve, step_out, b, 1)
                for c in range(CH):
                    wait(dve, up, b, c + 1)
                    nc.vector.tensor_tensor(h_pad[:, c, 1:SEQ + 1], bank(c), step_row[:],
                                            ALU.mult).then_inc(h_scaled.sem, 1)
                for c in range(CH):
                    wait(dve, tap0, b, c + 1)
                    for k in (1, 2):
                        if k == 2:
                            wait(dve, taps, b, 2 * c + 1)
                        else:
                            wait(dve, h_scaled, b, c + 1)
                        nc.vector.scalar_tensor_tensor(out=h_conv[:, c], in0=h_pad[:, c, k:SEQ + k],
                                                       scalar=cw[:, c, k:k + 1], in1=h_conv[:, c], op0=ALU.mult,
                                                       op1=ALU.add).then_inc(taps.sem, 1)
                experts_at("conv")
                for c in range(CH):
                    wait(dve, tanh, b, c + 1)
                    nc.vector.scalar_tensor_tensor(out=h_tanh[:, c], in0=h_tanh[:, c], scalar=1.0, in1=h_conv[:, c],
                                                   op0=ALU.add, op1=ALU.mult).then_inc(silu.sem, 1)
                wait(dve, h_tr, b, CH)
                nc.vector.tensor_reduce(top[:], bank(0, 4).rearrange("p (t f) -> p t f", t=TILES), AX_X, ALU.max,
                                        apply_absolute_value=True).then_inc(hq_scale.sem, 1)
                wait(dve, hq_scale, b, 1)
                nc.vector.tensor_scalar(top[:], top[:], 2e-5, None, ALU.max).then_inc(hq_scale.sem, 1)
                wait(dve, hq_scale, b, 2)
                nc.vector.reciprocal(a_scale[:], top[:]).then_inc(hq_scale.sem, 1)
                wait(dve, hq_scale, b, 3)
                nc.vector.tensor_scalar(a_scale[:], a_scale[:], 127.0, None, ALU.mult).then_inc(hq_scale.sem, 1)
                wait(dve, hq_scale, b, 4)
                for t in range(TILES):
                    nc.vector.tensor_scalar(h_whole[:, t], bank(t), a_scale[:, t:t + 1], ROUND, ALU.mult,
                                            ALU.add).then_inc(hq_out.sem, 1)
                    wait(dve, hq_out, b, 2 * t + 1)
                    nc.vector.tensor_scalar(hq[:, t], h_whole[:, t], ROUND, None,
                                            ALU.subtract).then_inc(hq_out.sem, 1)
                nc.vector.reciprocal(a_step[:], a_scale[:]).then_inc(hq_scale.sem, 1)
                wait(dve, hq_scale, b, 5)
                nc.vector.tensor_scalar(a_step[:], a_step[:], w_step[:, 1:2], 0.5, ALU.mult,
                                        ALU.mult).then_inc(hq_scale.sem, 1)
                wait(dve, hq_scale, b, 6)
                experts_at("hq")
                for t in range(TILES):
                    wait(dve, down, b, t + 1)
                    nc.vector.scalar_tensor_tensor(out=x2[:, t], in0=bank(t)[:, 0:D], scalar=a_step[:, t:t + 1],
                                                   in1=x1[:, t], op0=ALU.mult, op1=ALU.add).then_inc(x2_out.sem, 1)
                wait(dve, x2_out, b, TILES)

                layernorm(2, x2, xn)
                experts_at("norm2")
                wait(dve, q_mm, b, 1)
                nc.vector.scalar_tensor_tensor(out=q_f[:], in0=bank(0).rearrange("p (t d) -> p t d", t=TILES),
                                               scalar=HD ** -0.5, in1=bq_s[:].unsqueeze(1).broadcast_to([P, TILES, D]),
                                               op0=ALU.mult, op1=ALU.add).then_inc(q_ready.sem, 1)
                wait(dve, q_ready, b, 1)
                split_q(1)
                attention(1, [lambda: experts_at("shift1"), lambda: None, lambda: experts_at("exp1"), lambda: None])
                wait(dve, o_mm, b, 1)
                wait(dve, x2b_out, b, 1)
                nc.vector.tensor_tensor(x3[:], bank(0).rearrange("p (t d) -> p t d", t=TILES), x2_bo[:],
                                        ALU.add).then_inc(x3_out.sem, 1)
                wait(dve, x3_out, b, 1)

                layernorm(3, x3, xn)
                experts_at("norm3")

            turn(0, False)
            with dve.Fori(1, BATCH) as b:
                turn(b, True)
            copy_dots(BATCH - 1)
            route_distances(BATCH - 1)
            route_ranks(BATCH - 1)
            route_weights(BATCH - 1)
            start_sum(BATCH - 1)
            expert_adds(BATCH - 1, range(EXPERTS))

        @block.tensor
        def _(pe):
            pe.wait_ge(s_memset, 7)
            pe.wait_ge(s_bit, 2)
            nc.tensor.matmul(bank(0)[:, 0:2], ones[:], abs_sums[:], start=True, stop=True).then_inc(s_wsum, 1)
            pe.wait_ge(s_cent, CENTROID_STEPS - 5)
            nc.tensor.transpose(bank(1)[:, 0:EXPERTS], cent_s[:], ident[0:EXPERTS, 0:EXPERTS]).then_inc(s_cent_pe, 1)
            pe.wait_ge(s_cent, CENTROID_STEPS - 3)
            nc.tensor.matmul(bank(2)[:, 0:EXPERTS], ones[:], cent_t_sq[:], start=True, stop=True).then_inc(s_cent_pe, 1)
            pe.wait_ge(s_ident, 2)
            pe.wait_ge(s_cent, CENTROID_STEPS)

            def transposed(dst, src):
                for t in range(TILES):
                    mm = nc.tensor.transpose(dst[:, t * P:(t + 1) * P], src[:, t],
                                             ident[:] if dst.dtype == F32 else ident16[:])
                return mm

            def routing_products(m):
                wait(pe, ln_out[3], m, TILES)
                transposed(bank(2), xn).then_inc(xn2_tr.sem, 1)
                wait(pe, xn2_out, m, 2)
                nc.tensor.matmul(bank(3), wp_s[:], xn_t[:], start=True, stop=True).then_inc(z_mm.sem, 1)
                wait(pe, z_out, m, 2)
                for t in range(TILES):
                    tokens = slice(t * P, (t + 1) * P)
                    nc.tensor.matmul(bank(2)[:, 16 * t:16 * t + EXPERTS], z_t[:, tokens], cent_t[:], start=True,
                                     stop=True)
                    mm = nc.tensor.matmul(bank(2)[:, 16 * t + EXPERTS:16 * t + EXPERTS + 1], z_sq[:, tokens],
                                          ones[:, 0:1], start=True, stop=True)
                mm.then_inc(dots.sem, 1)

            def bias_products(m):
                wait(pe, route, m, ROUTE_STEPS)
                pe.wait_ge(s_exp_rest, 48)
                for t in range(TILES):
                    mm = nc.tensor.transpose(bank(4)[0:EXPERTS, t * P:(t + 1) * P], comb[:, t], ident[:])
                mm.then_inc(comb_tr.sem, 1)
                wait(pe, combt_out, m, 1)
                for t in range(TILES):
                    mm = nc.tensor.matmul(bank(4)[:, t * D:(t + 1) * D], comb_t[:, t * P:(t + 1) * P], eb2[:],
                                          start=True, stop=True)
                mm.then_inc(b2_mm.sem, 1)

            def expert_steps(m, steps):
                for n in steps:
                    if n == 0:
                        wait(pe, xlo_out, m, 1)
                        pe.wait_ge(s_ew1_lo, 1)
                        pe.wait_ge(s_exp_rest, 48)
                    if n < EXPERTS * CH:
                        e, c = divmod(n, CH)
                        if n >= 1:
                            wait(pe, gelu, m, n)
                        w = slice(c * P, (c + 1) * P)
                        nc.tensor.matmul(bank(5), ew1_hi[:, e, w], x_hi[:], start=True, stop=False)
                        nc.tensor.matmul(bank(5), ew1_hi[:, e, w], x_lo[:], start=False, stop=False)
                        nc.tensor.matmul(bank(5), ew1_lo[:, e, w], x_hi[:], start=False,
                                         stop=True).then_inc(h_mm.sem, 1)
                    if n >= CH:
                        e, t = divmod(n - CH, TILES)
                        if t == 0:
                            wait(pe, gelu, m, CH * (e + 1))
                            if e >= 2:
                                wait(pe, y_used, m, 1 + TILES * (e - 1))
                        for c in range(CH):
                            mm = nc.tensor.matmul(bank(6 + e % 2)[:, t * D:(t + 1) * D],
                                                  hidden[:, e % 2, c, t * P:(t + 1) * P], ew2[:, e, c],
                                                  start=(c == 0), stop=(c == CH - 1))
                        if t == TILES - 1:
                            mm.then_inc(y_mm.sem, 1)

            def turn(b, experts):
                def experts_at(point):
                    if experts:
                        expert_steps(b - 1, EXPERT_SPANS[point])

                def key_features(l):
                    wait(pe, kf_ready[l], b, 3)
                    for c in range(2):
                        for g in range(GROUPS):
                            mm = nc.tensor.transpose(bank16(4)[:, (4 * c + g) * P:(4 * c + g + 1) * P],
                                                     k_feat[l][:, c, 4 * g:4 * g + 4, :].rearrange("p h f -> p (h f)"),
                                                     ident16[:])
                    mm.then_inc(kf_t[l].sem, 1)

                def score_pair(l, k):
                    if k >= 2:
                        wait(pe, exped[l], b, k - 1)
                    for slot in range(2):
                        n = 2 * k + slot
                        g, j = divmod(n, 5)
                        keys, c = (k_main[l][:, 4 * g + j], 0) if j < 4 else (k_rest[l][:, g], 1)
                        dst = bank(2 * (k % 2) + slot)
                        mm = nc.tensor.matmul(dst, keys, q_op[:, g], start=True, stop=(l == 1))
                        if l == 0:
                            mm = nc.tensor.matmul(dst, mask_diag[:], m_key[:, c], start=False, stop=True)
                    mm.then_inc(s_key[l].sem, 1)

                def weighted_values(l, g):
                    wait(pe, exped[l], b, (5 * g + 4) // 2 + 1)
                    if g >= 1:
                        wait(pe, o_out[l], b, g)
                    if g == 0:
                        wait(pe, v_ready[l], b, 5)
                    for c in range(2):
                        for j in range(PER_GROUP):
                            quad = slice(QUAD * j, QUAD * (j + 1))
                            n = 5 * g + (j if c == 0 else 4)
                            mm = nc.tensor.matmul(bank(4)[quad, :], (v_rest if c else v_main)[l][:, 4 * g + j, :],
                                                  probs[:, n % RING, :], start=(c == 0), stop=(c == 1),
                                                  tile_position=(0, QUAD * j))
                    mm.then_inc(pv[l].sem, 1)

                def attention(l):
                    wait(pe, q_split[l], b, 1)
                    for t in range(TILES):
                        mm = nc.tensor.transpose(bank16(4)[:, t * P:(t + 1) * P], q_hi[:, t], ident16[:])
                    mm.then_inc(qh_t[l].sem, 1)
                    wait(pe, kb_ready[l], b, 1)
                    wait(pe, qh_out[l], b, 1)
                    if l == 0:
                        wait(pe, masks, b, 1)

                    def feature_transposes(t):
                        wait(pe, shift[l], b, 2 * t + 2)
                        if t == 0:
                            wait(pe, q_hi2[l], b, 2)
                            wait(pe, q_split[l], b, 2)
                        if t >= 1:
                            wait(pe, q_out[l], b, t)
                        for g in range(GROUPS):
                            mm = nc.tensor.transpose(bank16(4)[:, g * P:(g + 1) * P],
                                                     q_feat[:, t, 4 * g:4 * g + 4, :].rearrange("p h f -> p (h f)"),
                                                     ident16[:])
                        mm.then_inc(qf_t[l].sem, 1)

                    for t in range(TILES):
                        for p in range(3):
                            m = 3 * t + p
                            if m >= 2:
                                wait(pe, maxed[l], b, m - 1)
                            for s in range(2):
                                h0, n = MAX_HEADS[2 * p + s]
                                dst = bank(2 * (m % 2) + s)[:, 0:n * KEYS]
                                mm = nc.tensor.matmul(dst, q_hi_t[:, t * P:(t + 1) * P],
                                                      k_blocks[l][:, h0:h0 + n, :].rearrange("p h k -> p (h k)"),
                                                      start=True, stop=(l == 1))
                                if l == 0:
                                    mm = nc.tensor.matmul(dst.rearrange("p (h k) -> p h k", k=KEYS), mask_diag[:],
                                                          m_tok[:, t].unsqueeze(1).broadcast_to([P, n, KEYS]),
                                                          start=False, stop=True)
                            mm.then_inc(s_tok[l].sem, 1)
                            if p == 0:
                                experts_at(f"max{l}_{t}")
                            if p == 1 and t >= 1:
                                feature_transposes(t - 1)
                    feature_transposes(TILES - 1)
                    wait(pe, q_out[l], b, TILES)
                    wait(pe, k_ready[l], b, 2 * PER_GROUP)
                    if l == 0:
                        wait(pe, masks, b, 2)
                    k = 0
                    for g, ahead in enumerate((5, 8, 10, 10)):
                        while k < ahead:
                            score_pair(l, k)
                            k += 1
                        weighted_values(l, g)
                    wait(pe, o_out[l], b, GROUPS)
                    for t in range(TILES):
                        for g in range(GROUPS):
                            mm = nc.tensor.transpose(bank(t)[:, g * P:(g + 1) * P], o_t[:, g, t * P:(t + 1) * P],
                                                     ident[:])
                    mm.then_inc(o_tok[l].sem, 1)

                key_features(0)
                wait(pe, ctx_loaded, b, 32)
                pe.wait_ge(s_proj_w, 16 * 7)
                pe.wait_ge(s_kv_w, 16 * 13)
                if experts:
                    wait(pe, x3_out, b - 1, 1)
                for c in range(2):
                    nc.tensor.matmul(bank(0)[:, c * 2 * D:(c + 1) * 2 * D], ctx_t[:, c * KEYS:c * KEYS + P], wkv_s[:],
                                     start=True, stop=True)
                nc.tensor.matmul(bank(1)[:, 0:KEYS], wkv_s[:, 0:D], ctx_t[:, 0:KEYS], start=True,
                                 stop=True).then_inc(kv_mm.sem, 1)
                if experts:
                    routing_products(b - 1)
                experts_at("keys")
                if experts:
                    wait(pe, dots_out, b - 1, 2)
                wait(pe, k_ready[0], b, 2 * PER_GROUP)
                wait(pe, kv_out, b, 1)
                wait(pe, k1t_out, b, 1)
                attention(0)

                if experts:
                    bias_products(b - 1)
                experts_at("quant")
                if experts:
                    wait(pe, y_used, b - 1, 1)
                wait(pe, xq_out, b, TILES + 1)
                transposed(bank16(0), xq).then_inc(xq_tr.sem, 1)
                wait(pe, diag_out, b, TILES)
                nc.tensor.matmul(bank(4), ones[:], step_diag[:].rearrange("p t k -> p (t k)"), start=True,
                                 stop=True).then_inc(step_mm.sem, 1)
                wait(pe, xqt_out, b, 1)
                for c in range(CH):
                    nc.tensor.matmul(bank(c), bit_w1[:, c * P:(c + 1) * P], xq_t[:], start=True,
                                     stop=True).then_inc(up.sem, 1)
                wait(pe, step_out, b, 1)
                key_features(1)
                experts_at("conv")
                wait(pe, h_scaled, b, CH)
                for c in range(CH):
                    wait(pe, silu, b, c + 1)
                    for t in range(TILES):
                        mm = nc.tensor.transpose(bank(t)[:, c * P:(c + 1) * P], h_tanh[:, c, t * P:(t + 1) * P],
                                                 ident[:])
                    mm.then_inc(h_tr.sem, 1)
                experts_at("hq")
                wait(pe, k_ready[1], b, 2 * PER_GROUP)

                def down_product(t):
                    for c in range(CH):
                        mm = nc.tensor.matmul(bank(t)[:, 0:D], hq_t[:, t, c], bit_w2[:, c], start=(c == 0),
                                              stop=(c == CH - 1))
                    mm.then_inc(down.sem, 1)

                for t in range(TILES):
                    wait(pe, hq_out, b, 2 * t + 2)
                    if t >= 1:
                        wait(pe, hqt_out, b, t)
                    for c in range(CH):
                        mm = nc.tensor.transpose(bank16(4)[:, c * P:(c + 1) * P], hq[:, t, c * P:(c + 1) * P],
                                                 ident16[:])
                    mm.then_inc(hq_tr.sem, 1)
                    if t >= 1:
                        down_product(t - 1)
                wait(pe, hqt_out, b, TILES)
                down_product(TILES - 1)

                experts_at("norm2")
                wait(pe, ln_out[2], b, TILES)
                transposed(bank(4), xn).then_inc(xn1_tr.sem, 1)
                wait(pe, xn1_out, b, 1)
                for t in range(TILES):
                    mm = nc.tensor.matmul(bank(0)[:, t * D:(t + 1) * D], xn_t[:, t * P:(t + 1) * P], wq_s[:],
                                          start=True, stop=True)
                mm.then_inc(q_mm.sem, 1)
                experts_at("query1")
                attention(1)
                experts_at("out1")
                wait(pe, attn_out[1], b, 2)
                transposed(bank(4), attn).then_inc(a_tr.sem, 1)
                wait(pe, at_out, b, 1)
                for t in range(TILES):
                    mm = nc.tensor.matmul(bank(0)[:, t * D:(t + 1) * D], attn_t[:, t * P:(t + 1) * P], wo_s[:],
                                          start=True, stop=True)
                mm.then_inc(o_mm.sem, 1)

                experts_at("norm3")

            turn(0, False)
            with pe.Fori(1, BATCH) as b:
                turn(b, True)
            routing_products(BATCH - 1)
            expert_steps(BATCH - 1, range(LATE))
            bias_products(BATCH - 1)
            expert_steps(BATCH - 1, range(LATE, LAST_STEP))


def kernel(x, ctx_1024, mask_BxSxS2_bk1, L0_ffn_w1, L0_ffn_conv_w, L0_ffn_conv_b, L0_ffn_w2, L1_xattn_Wq, L1_xattn_bq,
           L1_xattn_Wk, L1_xattn_bk, L1_xattn_Wv, L1_xattn_bv, L1_xattn_Wo, L1_xattn_bo, L1_ffn_centroids, L1_ffn_Wp,
           L1_ffn_bp, L1_ffn_W1, L1_ffn_b1, L1_ffn_W2, L1_ffn_b2):
    import concourse.bacc as _bacc
    from concourse.bass_utils import run_bass_kernel_spmd as _run

    ctx = np.asarray(ctx_1024)
    mask = np.asarray(mask_BxSxS2_bk1)
    ctx_rest = np.zeros((BATCH, PER_GROUP, QUAD, D), ctx.dtype)
    ctx_rest[:, :, :REST] = ctx[:, None, P:]
    ctx_rest = ctx_rest.reshape(BATCH, P, D)
    mask_rest = np.zeros((BATCH, PER_GROUP, QUAD, SEQ), mask.dtype)
    mask_rest[:, :, :REST] = mask.transpose(0, 2, 1)[:, None, P:]
    mask_t = np.stack([mask.transpose(0, 2, 1)[:, :P], mask_rest.reshape(BATCH, P, SEQ)], axis=2)
    arrays = {
        "x": x,
        "ctxt": np.concatenate([ctx.transpose(0, 2, 1), ctx_rest.transpose(0, 2, 1)], axis=2),
        "ctx_km": np.stack([ctx[:, :P], ctx_rest], axis=2),
        "mask_tm": mask,
        "mask_t": mask_t,
        "w1t": np.asarray(L0_ffn_w1).T,
        "conv_w": np.asarray(L0_ffn_conv_w).reshape(HIDDEN, 3),
        "conv_b": np.asarray(L0_ffn_conv_b).reshape(CH, P).T,
        "w2t": np.asarray(L0_ffn_w2).T,
        "wq_t": np.asarray(L1_xattn_Wq).T, "bq": L1_xattn_bq,
        "wk_t": np.asarray(L1_xattn_Wk).T, "bk": L1_xattn_bk, "bk_col": np.asarray(L1_xattn_bk).reshape(D, 1),
        "wv_t": np.asarray(L1_xattn_Wv).T, "bv": L1_xattn_bv,
        "wo_t": np.asarray(L1_xattn_Wo).T, "bo": L1_xattn_bo,
        "cent": L1_ffn_centroids,
        "wp": L1_ffn_Wp, "bp_col": np.asarray(L1_ffn_bp).reshape(D, 1),
        "moe_w1": L1_ffn_W1,
        "moe_b1": np.asarray(L1_ffn_b1).reshape(EXPERTS * CH, P).T,
        "moe_w2": L1_ffn_W2, "moe_b2": L1_ffn_b2,
        "ident_in": np.eye(P, dtype=np.float32),
        "blocks_in": np.kron(np.eye(HEADS, dtype=np.float32), np.ones((HD, 1), np.float32)),
        "iota_in": np.tile(np.arange(EXPERTS, dtype=np.float32), (P, 1)),
    }
    arrays = {f"{n}_dram": np.ascontiguousarray(a) for n, a in arrays.items()}
    nc = _bacc.Bacc("TRN2", target_bir_lowering=False, num_devices=1)
    args = [nc.dram_tensor(n, a.shape, mybir.dt.from_np(a.dtype), kind="ExternalInput").ap()
            for n, a in arrays.items()]
    out = nc.dram_tensor("out_dram", (BATCH, SEQ, D), F32, kind="ExternalOutput").ap()
    build(nc, *args, out)
    r = _run(nc, [arrays], core_ids=[0])
    return r.results[0]["out_dram"]
```

```python
from contextlib import ExitStack

import numpy as np

import concourse.bass as bass
from concourse import mybir

F32 = mybir.dt.float32
F16 = mybir.dt.float16
U8 = mybir.dt.uint8
U32 = mybir.dt.uint32
ALU = mybir.AluOpType
ACT = mybir.ActivationFunctionType
AX_X = mybir.AxisListType.X

P = 128
BATCH, SEQ, D = 4, 512, 128
KEYS = 154
HEADS, HD = 16, 8
GROUPS, PER_GROUP = 4, 4
TILES = SEQ // P
REST = KEYS - P
QUAD = 32
HIDDEN = 512
CH = HIDDEN // P
EXPERTS = 8
ROUND = 12582912.0
W1_SCALE = 256.0
CONV_SCALE = 256.0
MASKED = -10000.0
LN_EPS = 1e-5
RING = 16
PAIRS = (CH + 1) * GROUPS // 2
I32 = mybir.dt.int32
RSQRT_GUESS = 1597463007
NEWTON = 3
LN_STEPS = 3 + 3 * NEWTON
CENTROID_STEPS = 7 + 3 * NEWTON
DISTANCE_STEPS = 18 + 2 + 3 * NEWTON
RANK_STEPS = DISTANCE_STEPS + 2 + 3 * NEWTON + 2 + 2 * TILES
ROUTE_STEPS = RANK_STEPS + 10
MAX_HEADS = ((0, 3), (3, 3), (6, 3), (9, 3), (12, 2), (14, 2))


EXPERT_STEPS = {"max0_0": (1, 0), "max0_1": (1, 0), "max0_4": (1, 0), "max0_5": (1, 0), "max0_6": (1, 0),
                "max0_7": (1, 0), "max0_9": (1, 0), "shift0": (0, 1), "ready0": (0, 1), "bias": (0, 1),
                "quant": (6, 5), "copied_xs": (1, 0), "conv_0": (0, 1), "conv_2": (0, 1), "conv_3": (0, 1),
                "hq": (2, 3), "hq_0": (1, 1), "hq_1": (1, 0), "hq_2": (1, 0), "norm2": (3, 3), "copied_norm2": (1, 1),
                "query1": (1, 1), "copied_query1": (0, 1), "max1_0": (1, 0), "max1_1": (0, 1), "max1_2": (1, 0),
                "max1_3": (0, 1), "max1_5": (1, 0), "max1_6": (1, 0), "max1_7": (0, 1), "max1_8": (1, 0),
                "max1_10": (1, 0), "max1_11": (0, 1), "shift1": (0, 1), "ready1": (0, 1), "out1": (1, 1),
                "copied1": (1, 0), "norm3": (0, 4)}
HIDDEN_STEPS, OUTPUT_STEPS = {}, {}
for _kind, _steps in enumerate((HIDDEN_STEPS, OUTPUT_STEPS)):
    _at = 0
    for _name, _n in EXPERT_STEPS.items():
        _steps[_name] = range(_at, _at + _n[_kind])
        _at += _n[_kind]
    assert _at == EXPERTS * (CH, TILES)[_kind]
EXPERT_ADDS = {"quant": range(0, 2), "hq": range(2, 3), "norm2": range(3, 4), "query1": range(4, 5),
               "shift1": range(5, 6), "out1": range(6, 7), "norm3": range(7, 8)}
LATE = 3


def last_entry(b):
    return isinstance(b, int) and b == BATCH - 1


class Signal:

    def __init__(self, sem, per, first=0):
        self.sem, self.per, self.first = sem, per, first

    def at(self, b, k):
        return b * self.per + (k + self.first)


def build(nc, x, ctxt, ctx_km, mask_tm, mask_t, w1t, conv_w, conv_b, w2t, wq_t, bq, wk_t, bk_col, wv_t, kv_bias_in,
          wo_t, bo, cent, wp, wpt, bp, bp_col, moe_w1, moe_b1, moe_w2, moe_b2, ident_in, blocks_in, iota_in, out):
    with ExitStack() as ctx:
        def sb(name, shape, dt=F32):
            return ctx.enter_context(nc.sbuf_tensor(name, shape, dt))

        def sem(name):
            return ctx.enter_context(nc.semaphore(name))

        def sig(name, per, first=0):
            return Signal(sem(name), per, first)

        ident = sb("ident", [P, P])
        ident16 = sb("ident16", [P, P], F16)
        mask_diag = sb("mask_diag", [P, P], F16)
        ones = sb("ones", [P, P])
        head_blocks = sb("head_blocks", [P, HEADS])
        iota8 = sb("iota8", [P, EXPERTS])
        bit_w1 = sb("bit_w1", [P, HIDDEN], F16)
        bit_w2 = sb("bit_w2", [P, CH, D], F16)
        minus_round = sb("minus_round", [P, 1])
        abs_sums = sb("abs_sums", [P, 2])
        w_mean = sb("w_mean", [P, 2])
        w_scale = sb("w_scale", [P, 2])
        w_step = sb("w_step", [P, 2])
        cb = sb("cb", [P, CH])
        tap_hi = sb("tap_hi", [P, 3, HIDDEN], F16)
        tap_lo = sb("tap_lo", [P, 3, HIDDEN], F16)
        wq_s = sb("wq_s", [P, D])
        wkv_s = sb("wkv_s", [P, 2 * D])
        wo_s = sb("wo_s", [P, D])
        wp_c = sb("wp_c", [P, D + EXPERTS])
        zc_bias = sb("zc_bias", [P, D + EXPERTS])
        bq_s = sb("bq_s", [P, D])
        bo_s = sb("bo_s", [P, D])
        kv_bias = sb("kv_bias", [P, 2, 2 * D])
        bk_s = sb("bk_s", [P, 1])
        bp_s = sb("bp_s", [P, 1])
        cent_s = sb("cent_s", [EXPERTS, D])
        cent_n = sb("cent_n", [EXPERTS, 3])
        cent_t = sb("cent_t", [P, EXPERTS])
        cent_t_sq = sb("cent_t_sq", [P, EXPERTS])
        c_norm = sb("c_norm", [P, EXPERTS])
        c_rest = sb("c_rest", [P, EXPERTS])
        ew1_hi = sb("ew1_hi", [P, EXPERTS, HIDDEN], F16)
        ew1_lo = sb("ew1_lo", [P, EXPERTS, HIDDEN], F16)
        ew2 = sb("ew2", [P, EXPERTS, CH, D])
        eb1 = sb("eb1", [P, EXPERTS * CH])
        eb2 = sb("eb2", [EXPERTS, D])

        x_in = sb("x_in", [P, TILES, D])
        ctx_t = sb("ctx_t", [P, KEYS + P])
        ctx_k = sb("ctx_k", [P, 2, D])
        m_tok8 = sb("m_tok8", [P, TILES, KEYS], U8)
        m_key8 = sb("m_key8", [P, 2, SEQ], U8)
        m_tok = sb("m_tok", [P, TILES, KEYS], F16)
        m_key = sb("m_key", [P, 2, SEQ], F16)

        k_blocks = [sb(f"k_blocks{l}", [P, HEADS, KEYS], F16) for l in range(2)]
        k_feat = [sb(f"k_feat{l}", [P, 2, HEADS, QUAD], F16) for l in range(2)]
        k_main = [sb(f"k_main{l}", [P, HEADS, P], F16) for l in range(2)]
        k_rest = [sb(f"k_rest{l}", [P, GROUPS, P], F16) for l in range(2)]
        v_main = [sb(f"v_main{l}", [P, HEADS, QUAD]) for l in range(2)]
        v_rest = [sb(f"v_rest{l}", [P, HEADS, QUAD]) for l in range(2)]
        kv1 = sb("kv1", [P, 2, 2 * D])
        k1_t = sb("k1_t", [P, KEYS])
        q_f = sb("q_f", [P, TILES, D])
        q_feat = sb("q_feat", [P, TILES, HEADS, QUAD], F16)
        q_hi = sb("q_hi", [P, TILES, D], F16)
        q_hi_t = sb("q_hi_t", [P, SEQ], F16)
        q_op = sb("q_op", [P, GROUPS, SEQ], F16)
        neg_max = sb("neg_max", [P, TILES, HEADS])
        probs = sb("probs", [P, RING, SEQ])
        o_t = sb("o_t", [P, GROUPS, SEQ])
        denom = sb("denom", [P, TILES * HEADS])
        attn = sb("attn", [P, TILES, D])
        attn_t = sb("attn_t", [P, SEQ])
        cent_sq = attn_t[0:EXPERTS, 0:D]

        gate = sb("gate", [P, 1])
        table = sb("table", [P, 1])
        moments = sb("moments", [P, TILES, 6])
        mean_var = sb("mean_var", [P, TILES, 2])
        newton = sb("newton", [P, 2, TILES])
        rstd = sb("rstd", [P, TILES])
        xn = sb("xn", [P, TILES, D])
        xn_t = sb("xn_t", [P, SEQ])
        x1 = sb("x1", [P, TILES, D])
        x2 = sb("x2", [P, TILES, D])
        x2_bo = sb("x2_bo", [P, TILES, D])
        x3 = sb("x3", [P, TILES, D])
        y_sum = sb("y_sum", [P, TILES, D])

        top = sb("top", [P, TILES])
        a_scale = sb("a_scale", [P, TILES])
        a_step = sb("a_step", [P, TILES])
        x_whole = sb("x_whole", [P, TILES, D])
        xs_hi = sb("xs_hi", [P, SEQ + 2], F16)
        xs_lo = sb("xs_lo", [P, SEQ + 2], F16)
        w1_raw = x_whole[:].rearrange("p t d -> p (t d)")
        w2_raw = x2[:].rearrange("p t d -> p (t d)")
        tap_rows = [a[:].rearrange("p t d -> p (t d)") for a in (y_sum, x3, x2_bo)]
        h_act = probs[:, 0:CH, :]
        h_whole = o_t
        hq = sb("hq", [P, TILES, HIDDEN], F16)
        hq_t = sb("hq_t", [P, TILES, CH, P], F16)

        x_hi = sb("x_hi", [P, SEQ], F16)
        x_lo = sb("x_lo", [P, SEQ], F16)
        zc = sb("zc", [P, TILES, D + EXPERTS])
        z_sq = sb("z_sq", [P, TILES, D])
        wp_t = z_sq[:, 0, :]
        bp_mat = z_sq[:, 1, :]
        u = sb("u", [P, TILES, EXPERTS])
        r1 = sb("r1", [P, 8, TILES])
        r8 = sb("r8", [P, 8, TILES, EXPERTS])
        best = sb("best", [P, TILES, 8])
        best_i = sb("best_i", [P, TILES, 8], U32)
        best_f = sb("best_f", [P, TILES, 8])
        comb = sb("comb", [P, TILES, EXPERTS])
        comb_t = sb("comb_t", [EXPERTS, SEQ])
        hidden = sb("hidden", [P, 2, CH, SEQ])
        ew1_raw = hidden[:].rearrange("p r c t -> p (r c t)")

        ps = ctx.enter_context(nc.psum_tensor("ps", [P, 8 * 512], F32))

        def bank(i, n=1):
            return ps[:, 512 * i:512 * (i + n)]

        def hidden_bank(m, n):
            return bank(0 if last_entry(m) and n % 2 else 5)

        def bank16(i):
            return bank(i).bitcast(F16)

        s_const = sem("s_const_loaded")
        s_bit_w = sem("s_bitnet_weights_loaded")
        s_proj_w = sem("s_projection_weights_loaded")
        s_kv_w = sem("s_key_value_weights_loaded")
        s_exp_w1 = sem("s_expert_w1_loaded")
        s_exp_rest = sem("s_expert_rest_loaded")
        s_memset = sem("s_operand_constants")
        s_pool_set = sem("s_pool_memset")
        s_ident = sem("s_identities")
        s_parts = sem("s_constant_parts_set")
        s_wsum = sem("s_weight_sums")
        s_bit = sem("s_bitnet_weights")
        s_cent = sem("s_centroids")
        s_cent_pe = sem("s_centroids_pe")
        s_bq = sem("s_query_bias")
        s_bp = sem("s_projection_bias")
        s_ew1 = sem("s_expert_w1_high")
        s_ew1_lo = sem("s_expert_w1_low")

        x_loaded = sig("x_loaded", 16)
        ctx_loaded = sig("ctx_loaded", 32)
        mask_loaded = sig("mask_loaded", 32)
        stored = sig("stored", 16, 16)
        masks = sig("masks_converted", 2)
        kb_ready = [sig(f"k_blocks_ready{l}", 1) for l in range(2)]
        kf_ready = [sig(f"k_features_ready{l}", 3) for l in range(2)]
        v_ready = [sig(f"values_ready{l}", 5) for l in range(2)]
        kf_t = [sig(f"k_features_transposed{l}", 1) for l in range(2)]
        k_ready = [sig(f"k_operands_ready{l}", 8) for l in range(2)]
        kv_mm = sig("kv_projected", 1)
        kv_out = sig("kv_biased", 1)
        k1t_out = sig("k1_transposed_biased", 1)
        ln_mom = [sig(f"ln_moments{n}", 8) for n in range(4)]
        ln_rstd = [sig(f"ln_rstd{n}", LN_STEPS) for n in range(4)]
        ln_out = [sig(f"ln_out{n}", TILES) for n in range(4)]
        q_ready = sig("q_projected_scaled", 1)
        q_split = [sig(f"q_split{l}", 2) for l in range(2)]
        q_hi2 = [sig(f"q_hi_copied{l}", 2) for l in range(2)]
        qh_t = [sig(f"q_hi_transposed{l}", 1) for l in range(2)]
        qh_out = [sig(f"q_hi_ready{l}", 1) for l in range(2)]
        s_tok = [sig(f"token_scores{l}", 3 * TILES) for l in range(2)]
        maxed = [sig(f"maxima{l}", 3 * TILES) for l in range(2)]
        shift = [sig(f"shift_features{l}", 2 * TILES) for l in range(2)]
        qf_t = [sig(f"q_features_transposed{l}", TILES) for l in range(2)]
        q_out = [sig(f"q_operand_ready{l}", TILES) for l in range(2)]
        s_key = [sig(f"key_scores{l}", PAIRS) for l in range(2)]
        exped = [sig(f"exponentials{l}", PAIRS) for l in range(2)]
        pv = [sig(f"weighted_values{l}", GROUPS) for l in range(2)]
        o_out = [sig(f"weighted_values_copied{l}", GROUPS) for l in range(2)]
        o_tok = [sig(f"outputs_by_token{l}", 1) for l in range(2)]
        attn_out = [sig(f"attention_normalised{l}", 2) for l in range(2)]
        x1_out = sig("x1_ready", 1)
        xq_scale = sig("xq_scale", 5)
        xq_out = sig("quantised_input", 2 * TILES)
        xs_tr = sig("quantised_input_transposed", 1)
        xs_hi_out = sig("xs_hi_ready", 1)
        xs_lo_out = sig("xs_lo_ready", 1)
        conv = sig("convolved_up_product", CH)
        silu = sig("silu", CH)
        h_tr = sig("h_transposed", CH)
        hq_scale = sig("hq_scale", 6)
        hq_whole = sig("hq_rounded", TILES)
        hq_out = sig("hq_ready", TILES)
        hq_tr = sig("hq_transposed", TILES)
        hqt_out = sig("hq_t_ready", TILES)
        down = sig("bitnet_down_product", TILES)
        x2_out = sig("x2_ready", TILES)
        x2b_out = sig("x2_with_bias", 1)
        xn1_tr = sig("xn_transposed1", 1)
        xn1_out = sig("xn_t_ready1", 1)
        q_mm = sig("q_product", 1)
        a_tr = sig("attention_transposed", 1)
        at_out = sig("attention_t_ready", 1)
        o_mm = sig("output_product", 1)
        x3_out = sig("x3_ready", 1)
        xn2_tr = sig("xn_transposed2", 1)
        xn2_out = sig("xn_t_ready2", 2)
        xlo_out = sig("x_lo_ready", 1)
        z_mm = sig("z_and_dots_product", 1)
        z_out = sig("z_and_dots_biased", 1)
        z_squared = sig("z_squared", 1)
        route = sig("routing_steps", ROUTE_STEPS)
        comb_tr = sig("comb_transposed", 1)
        combt_out = sig("comb_t_ready", 1)
        b2_mm = sig("expert_bias_product", 1)
        h_mm = sig("expert_hidden_product", EXPERTS * CH)
        gelu = sig("gelu", EXPERTS * CH)
        y_mm = sig("expert_output", EXPERTS)
        y_used = sig("expert_output_added", 1 + TILES * EXPERTS)

        def wait(eng, signal, b, k):
            eng.wait_ge(signal.sem, signal.at(b, k))

        block = ctx.enter_context(nc.Block())

        @block.sync
        def _(sp):
            sp.sem_inc(stored.sem, 16)

            def load_batch(b):
                sp.dma_start(x_in[:], x[b].rearrange("(t p) d -> p t d", p=P)).then_inc(x_loaded.sem, 16)
                sp.dma_start(ctx_t[:], ctxt[b]).then_inc(ctx_loaded.sem, 16)
                sp.dma_start(ctx_k[:], ctx_km[b]).then_inc(ctx_loaded.sem, 16)
                sp.dma_start(m_tok8[:], mask_tm[b].rearrange("(t p) k -> p t k", p=P)).then_inc(mask_loaded.sem, 16)
                sp.dma_start(m_key8[:], mask_t[b]).then_inc(mask_loaded.sem, 16)

            load_batch(0)
            sp.dma_start(w1_raw, w1t).then_inc(s_bit_w, 16)
            sp.dma_start(w2_raw.rearrange("p (c d) -> p c d", c=CH),
                         w2t.rearrange("(c p) d -> p c d", p=P)).then_inc(s_bit_w, 16)
            for k in range(3):
                sp.dma_start(tap_rows[k], conv_w[k].partition_broadcast(P)).then_inc(s_bit_w, 16)
            sp.dma_start(cb[:], conv_b).then_inc(s_bit_w, 16)
            sp.dma_start(iota8[:], iota_in).then_inc(s_proj_w, 16)
            sp.dma_start(wq_s[:], wq_t).then_inc(s_proj_w, 16)
            sp.dma_start(bq_s[:], bq.partition_broadcast(P)).then_inc(s_proj_w, 16)
            sp.dma_start(wo_s[:], wo_t).then_inc(s_proj_w, 16)
            sp.dma_start(bo_s[:], bo.partition_broadcast(P)).then_inc(s_proj_w, 16)
            sp.dma_start(wp_c[:, 0:D], wp).then_inc(s_proj_w, 16)
            sp.dma_start(wp_t, wpt).then_inc(s_proj_w, 16)
            sp.dma_start(zc_bias[:, 0:D], bp.partition_broadcast(P)).then_inc(s_proj_w, 16)
            sp.dma_start(bp_s[:], bp_col).then_inc(s_proj_w, 16)
            sp.dma_start(cent_s[:], cent).then_inc(s_proj_w, 16)
            sp.wait_ge(s_proj_w, 16 * 10)
            sp.dma_start(ew1_raw.rearrange("p (e f) -> p e f", e=EXPERTS),
                         moe_w1.rearrange("e d f -> d e f")).then_inc(s_exp_w1, 16)
            sp.dma_start(ew2[:], moe_w2.rearrange("e (c p) d -> p e c d", p=P)).then_inc(s_exp_rest, 16)
            sp.dma_start(eb1[:], moe_b1).then_inc(s_exp_rest, 16)
            sp.dma_start(eb2[:], moe_b2).then_inc(s_exp_rest, 16)

            def load_next(b):
                wait(sp, x1_out, b - 1, 1)
                load_batch(b)

            def store(m):
                wait(sp, y_used, m, 1 + TILES * EXPERTS)
                sp.dma_start(out[m].rearrange("(t p) d -> p t d", p=P), y_sum[:]).then_inc(stored.sem, 16)

            load_next(1)
            with sp.Fori(2, BATCH) as b:
                load_next(b)
                store(b - 2)
            store(BATCH - 2)
            store(BATCH - 1)
            sp.wait_ge(stored.sem, 16 * (BATCH + 1))

        @block.gpsimd
        def _(pool):
            for n, t in enumerate([*k_main, *k_rest]):
                nc.gpsimd.memset(t[:].rearrange("p a b -> p (a b)").bitcast(F32), 0.0).then_inc(s_pool_set, 1)
            pool.wait_ge(s_const, 32)

            def square(m):
                wait(pool, z_out, m, 1)
                nc.gpsimd.tensor_tensor(z_sq[:], zc[:, :, 0:D], zc[:, :, 0:D], ALU.mult).then_inc(z_squared.sem, 1)

            def turn(b, experts):

                def blocks(l, k_t):
                    nc.gpsimd.tensor_tensor(k_blocks[l][:], k_t.unsqueeze(1).broadcast_to([P, HEADS, KEYS]),
                                            head_blocks[:].unsqueeze(2).broadcast_to([P, HEADS, KEYS]),
                                            ALU.mult).then_inc(kb_ready[l].sem, 1)

                def features(l, keys):
                    by_head = keys.rearrange("p c (h d) -> p c h d", d=HD)
                    nc.gpsimd.tensor_copy(k_feat[l][:, :, :, 0:HD], by_head).then_inc(kf_ready[l].sem, 1)
                    nc.gpsimd.tensor_copy(k_feat[l][:, :, :, HD:2 * HD], by_head).then_inc(kf_ready[l].sem, 1)
                    wait(pool, kf_ready[l], b, 1)
                    nc.gpsimd.tensor_tensor(k_feat[l][:, :, :, 2 * HD:3 * HD], by_head, k_feat[l][:, :, :, 0:HD],
                                            ALU.subtract).then_inc(kf_ready[l].sem, 1)

                wait(pool, ctx_loaded, b, 32)
                if experts:
                    wait(pool, mask_loaded, b, 32)
                blocks(0, ctx_t[:, 0:KEYS])
                if experts:
                    nc.gpsimd.tensor_copy(m_tok[:], m_tok8[:]).then_inc(masks.sem, 1)
                else:
                    pool.wait_ge(s_memset, 1)
                features(0, ctx_k[:])
                if not experts:
                    wait(pool, masks, b, 1)
                    pool.wait_ge(s_memset, 2)
                nc.gpsimd.tensor_copy(m_key[:], m_key8[:]).then_inc(masks.sem, 1)
                wait(pool, k1t_out, b, 1)
                wait(pool, kv_out, b, 1)
                if experts:
                    square(b - 1)
                blocks(1, k1_t[:])
                features(1, kv1[:, :, 0:D])
                wait(pool, x2_out, b, TILES)
                nc.gpsimd.tensor_tensor(x2_bo[:], x2[:], bo_s[:].unsqueeze(1).broadcast_to([P, TILES, D]),
                                        ALU.add).then_inc(x2b_out.sem, 1)

            turn(0, False)
            with pool.Fori(1, BATCH) as b:
                turn(b, True)
            square(BATCH - 1)

        @block.scalar
        def _(act):
            act.dma_start(head_blocks[:], blocks_in).then_inc(s_const, 16)
            act.dma_start(ident[:], ident_in).then_inc(s_const, 16)
            act.dma_start(wkv_s[:, 0:D], wk_t).then_inc(s_kv_w, 16)
            act.dma_start(wkv_s[:, D:2 * D], wv_t).then_inc(s_kv_w, 16)
            act.dma_start(bk_s[:], bk_col).then_inc(s_kv_w, 16)
            act.dma_start(kv_bias[:], kv_bias_in).then_inc(s_kv_w, 16)

            def normalised_transposed(m):
                wait(act, xn2_tr, m, 1)
                nc.scalar.activation(xn_t[:], bank(3), ACT.Copy).then_inc(xn2_out.sem, 1)
                nc.scalar.activation(x_hi[:], bank(3), ACT.Copy).then_inc(xn2_out.sem, 1)

            def weights_by_expert(m):
                wait(act, comb_tr, m, 1)
                nc.scalar.activation(comb_t[:], bank(4)[0:EXPERTS, :], ACT.Copy).then_inc(combt_out.sem, 1)

            def gelus(m, steps):
                for n in steps:
                    e, c = divmod(n, CH)
                    wait(act, h_mm, m, n + 1)
                    if e >= 2:
                        wait(act, y_mm, m, e - 1)
                    nc.scalar.activation(hidden[:, e % 2, c], hidden_bank(m, n), ACT.Gelu, bias=eb1[:, n:n + 1],
                                         scale=1.0 / W1_SCALE).then_inc(gelu.sem, 1)

            def bring_table(function):
                nc.scalar.activation(table[:], ones[:, 0:1], function)

            def k_operands(b, l, quads=range(PER_GROUP)):
                wait(act, kf_t[l], b, 1)
                src = bank16(4 + l).rearrange("p (c g k) -> p c g k", c=2, g=GROUPS)
                if l == 0:
                    act.wait_ge(s_pool_set, 4)
                for j in quads:
                    quad = slice(QUAD * j, QUAD * (j + 1))
                    nc.scalar.activation(k_main[l][quad, j::PER_GROUP, :], src[quad, 0],
                                         ACT.Copy).then_inc(k_ready[l].sem, 1)
                    nc.scalar.activation(k_rest[l][quad, :, quad], src[quad, 1, :, quad],
                                         ACT.Copy).then_inc(k_ready[l].sem, 1)

            def values(b, l, src):
                v_by_head = src.rearrange("p c (h d) -> p c h d", d=HD)
                nc.scalar.activation(v_main[l][:, :, 0:HD], v_by_head[:, 0], ACT.Copy).then_inc(v_ready[l].sem, 1)
                for j in range(PER_GROUP):
                    quad = slice(QUAD * j, QUAD * (j + 1))
                    nc.scalar.activation(v_rest[l][quad, j::PER_GROUP, 0:HD], v_by_head[quad, 1, j::PER_GROUP],
                                         ACT.Copy).then_inc(v_ready[l].sem, 1)

            def q_transposed(b, l):
                wait(act, qh_t[l], b, 1)
                nc.scalar.activation(q_hi_t[:], bank16(2 if l == 0 else 4)[:, 0:SEQ],
                                     ACT.Copy).then_inc(qh_out[l].sem, 1)

            def first_operands(b, keys):
                wait(act, ctx_loaded, b, 32)
                if keys:
                    k_operands(b, 0)
                q_transposed(b, 0)
                wait(act, kv_mm, b, 1)
                nc.scalar.activation(k1_t[:], bank(1)[:, 0:KEYS], ACT.Identity,
                                     bias=bk_s[:, 0:1]).then_inc(k1t_out.sem, 1)
                if not keys:
                    act.wait_ge(s_memset, 2)
                values(b, 0, ctx_k[:])

            def turn(b, experts, last=False):
                def experts_at(point, part=slice(None)):
                    if experts:
                        gelus(b - 1, HIDDEN_STEPS.get(point, range(0))[part])

                def attention(l):
                    wait(act, q_split[l], b, 1)
                    for part in (slice(0, HD), slice(2 * HD, 3 * HD)):
                        nc.scalar.activation(q_feat[:, :, :, part], q_hi[:].rearrange("p t (h d) -> p t h d", d=HD),
                                             ACT.Copy).then_inc(q_hi2[l].sem, 1)
                    if l == 0 and not experts:
                        k_operands(b, 0)

                    def q_operand(t):
                        wait(act, qf_t[l], b, t + 1)
                        nc.scalar.activation(q_op[:, :, t * P:(t + 1) * P],
                                             bank16(4)[:, 0:SEQ].rearrange("p (g k) -> p g k", g=GROUPS),
                                             ACT.Copy).then_inc(q_out[l].sem, 1)

                    for t in range(TILES):
                        for p in range(3):
                            experts_at(f"max{l}_{3 * t + p}")
                            if p == 1 and t >= 1:
                                q_operand(t - 1)
                    bring_table(ACT.Exp)
                    q_operand(TILES - 1)
                    for k in range(PAIRS):
                        wait(act, s_key[l], b, k + 1)
                        if 2 * k + 1 >= RING:
                            wait(act, pv[l], b, (2 * k + 1 - RING) // 5 + 1)
                        slot = 2 * k % RING
                        nc.scalar.activation(probs[:, slot:slot + 2, :],
                                             bank(2 * (k % 2), 2).rearrange("p (c t) -> p c t", c=2),
                                             ACT.Exp).then_inc(exped[l].sem, 1)
                        if l == 0 and 3 <= k < 3 + PER_GROUP:
                            k_operands(b, 1, range(k - 3, k - 2))
                    if experts:
                        bring_table(ACT.Gelu)

                if experts:
                    bring_table(ACT.Gelu)
                    normalised_transposed(b - 1)
                attention(0)

                if experts:
                    weights_by_expert(b - 1)
                else:
                    act.wait_ge(s_exp_w1, 16)
                    nc.scalar.activation(ew1_hi[:].rearrange("p e f -> p (e f)"), ew1_raw, ACT.Copy,
                                         scale=W1_SCALE).then_inc(s_ew1, 1)
                experts_at("quant")
                wait(act, xs_tr, b, 1)
                nc.scalar.activation(xs_hi[:, 1:SEQ + 1], bank(0), ACT.Copy).then_inc(xs_hi_out.sem, 1)
                experts_at("copied_xs")
                bring_table(ACT.Silu)
                for c in range(CH):
                    wait(act, conv, b, c + 1)
                    nc.scalar.activation(h_act[:, c], bank(4), ACT.Silu, bias=cb[:, c:c + 1],
                                         scale=1.0 / CONV_SCALE).then_inc(silu.sem, 1)
                if experts:
                    bring_table(ACT.Gelu)
                experts_at("hq")
                for t in range(TILES + 1):
                    if t < TILES:
                        wait(act, hq_whole, b, t + 1)
                        nc.scalar.activation(hq[:, t], h_whole[:, t], ACT.Identity,
                                             bias=minus_round[:, 0:1]).then_inc(hq_out.sem, 1)
                    if t >= 1:
                        wait(act, hq_tr, b, t)
                        nc.scalar.activation(hq_t[:, t - 1].rearrange("p c k -> p (c k)"), bank16(4)[:, 0:HIDDEN],
                                             ACT.Copy).then_inc(hqt_out.sem, 1)
                        experts_at(f"hq_{t - 1}")

                wait(act, kv_out, b, 1)
                values(b, 1, kv1[:, :, D:2 * D])
                experts_at("norm2")
                wait(act, xn1_tr, b, 1)
                nc.scalar.activation(xn_t[:], bank(4), ACT.Copy).then_inc(xn1_out.sem, 1)
                experts_at("copied_norm2")
                experts_at("query1")
                q_transposed(b, 1)
                attention(1)
                experts_at("out1")
                wait(act, a_tr, b, 1)
                nc.scalar.activation(attn_t[:], bank(4), ACT.Copy).then_inc(at_out.sem, 1)

                experts_at("copied1")
                if not last:
                    first_operands(b + 1, True)

            wait(act, mask_loaded, 0, 32)
            nc.scalar.activation(m_tok[:], m_tok8[:], ACT.Copy).then_inc(masks.sem, 1)
            first_operands(0, False)
            turn(0, False)
            with act.Fori(1, BATCH - 1) as b:
                turn(b, True)
            turn(BATCH - 1, True, last=True)
            normalised_transposed(BATCH - 1)
            gelus(BATCH - 1, range(CH * LATE))
            weights_by_expert(BATCH - 1)
            gelus(BATCH - 1, range(CH * LATE, CH * EXPERTS))

        @block.vector
        def _(dve):
            def inverse_root(then, a, root, t):
                then(nc.vector.tensor_scalar(root.bitcast(I32), a.bitcast(I32), 1, None, ALU.logical_shift_right))
                then(nc.vector.tensor_scalar(root.bitcast(I32), root.bitcast(I32), -1, RSQRT_GUESS, ALU.mult, ALU.add))
                for _ in range(NEWTON):
                    then(nc.vector.tensor_tensor(t, root, root, ALU.mult))
                    then(nc.vector.scalar_tensor_tensor(out=t, in0=t, scalar=-0.5, in1=a, op0=ALU.mult, op1=ALU.mult))
                    then(nc.vector.scalar_tensor_tensor(out=root, in0=t, scalar=1.5, in1=root, op0=ALU.add,
                                                        op1=ALU.mult))

            shift_part = slice(3 * HD, 3 * HD + 2)
            padded_rows = [slice(QUAD * j, QUAD * j + REST) for j in range(PER_GROUP)]

            def shift_ones(l):
                nc.vector.memset(k_feat[l][:, 0, :, shift_part], 1.0).then_inc(s_parts, 1)
                for rows in padded_rows:
                    nc.vector.memset(k_feat[l][rows, 1, :, shift_part], 1.0).then_inc(s_parts, 1)

            def zero_features(l):
                nc.vector.memset(k_feat[l][:].rearrange("p c h f -> p (c h f)").bitcast(F32), 0.0).then_inc(s_parts, 1)

            def later_zeros():
                zero_features(1)
                for l in range(2):
                    nc.vector.memset(v_main[l][:], 0.0).then_inc(s_parts, 1)
                    nc.vector.memset(v_rest[l][:], 0.0).then_inc(s_parts, 1)
                for half in (xs_hi, xs_lo):
                    nc.vector.memset(half[:, 0:SEQ + 2:SEQ + 1], 0.0).then_inc(s_parts, 1)

            def later_ones():
                dve.wait_ge(s_parts, 15)
                shift_ones(1)
                for l in range(2):
                    nc.vector.memset(v_main[l][:, :, HD:HD + 1], 1.0).then_inc(s_parts, 1)
                    for j, rows in enumerate(padded_rows):
                        nc.vector.memset(v_rest[l][rows, j::PER_GROUP, HD:HD + 1], 1.0).then_inc(s_parts, 1)
                dve.wait_ge(s_parts, 30)
                nc.vector.memset(top[:], 0.0).then_inc(s_memset, 1)

            zero_features(0)
            nc.vector.memset(q_feat[:].rearrange("p t h f -> p (t h f)").bitcast(F32), 0.0).then_inc(s_parts, 1)
            nc.vector.memset(ones[:], 1.0).then_inc(s_parts, 1)
            dve.wait_ge(s_parts, 3)
            shift_ones(0)
            dve.wait_ge(s_parts, 8)
            nc.vector.memset(top[:], 0.0).then_inc(s_memset, 1)
            dve.wait_ge(s_const, 32)
            nc.vector.tensor_copy(ident16[:], ident[:]).then_inc(s_ident, 1)
            nc.vector.tensor_scalar(mask_diag[:], ident[:], MASKED, None, ALU.mult).then_inc(s_ident, 1)
            nc.vector.memset(minus_round[:], -ROUND).then_inc(s_ident, 1)

            def sum_bitnet_weights():
                dve.wait_ge(s_bit_w, 16 * 6)
                nc.vector.tensor_reduce(abs_sums[:, 0:1], w1_raw, AX_X, ALU.add,
                                        apply_absolute_value=True).then_inc(s_bit, 1)
                nc.vector.tensor_reduce(abs_sums[:, 1:2], w2_raw, AX_X, ALU.add,
                                        apply_absolute_value=True).then_inc(s_bit, 1)

            def make_bitnet_weights():
                dve.wait_ge(s_wsum, 1)
                nc.vector.tensor_scalar(w_mean[:], bank(7)[:, 0:2], 1.0 / (HIDDEN * D), 1e-5, ALU.mult,
                                        ALU.max).then_inc(s_bit, 1)
                dve.wait_ge(s_bit, 3)
                nc.vector.reciprocal(w_scale[:], w_mean[:]).then_inc(s_bit, 1)
                dve.wait_ge(s_bit, 4)
                nc.vector.reciprocal(w_step[:], w_scale[:]).then_inc(s_bit, 1)
                done = 5
                for n, (raw, bit) in enumerate(((w1_raw, bit_w1[:]),
                                                (w2_raw, bit_w2[:].rearrange("p c d -> p (c d)")))):
                    nc.vector.tensor_scalar(raw, raw, w_scale[:, n:n + 1], ROUND, ALU.mult, ALU.add).then_inc(s_bit, 1)
                    dve.wait_ge(s_bit, done + 1)
                    nc.vector.tensor_scalar(raw, raw, ROUND, 1.0, ALU.subtract, ALU.min).then_inc(s_bit, 1)
                    dve.wait_ge(s_bit, done + 2)
                    nc.vector.tensor_scalar(bit, raw, -1.0, None, ALU.max).then_inc(s_bit, 1)
                    done += 3

            def make_taps():
                done = 11
                dve.wait_ge(s_bit, done)
                for row in tap_rows:
                    nc.vector.tensor_scalar(row, row, w_step[:, 0:1], CONV_SCALE, ALU.mult, ALU.mult).then_inc(s_bit, 1)
                done += 3
                dve.wait_ge(s_bit, done)
                for row in tap_rows:
                    nc.vector.tensor_tensor(row, row, bit_w1[:], ALU.mult).then_inc(s_bit, 1)
                done += 3
                dve.wait_ge(s_bit, done)
                for k, row in enumerate(tap_rows):
                    nc.vector.tensor_copy(tap_hi[:, k], row).then_inc(s_bit, 1)
                done += 3
                dve.wait_ge(s_bit, done)
                for k, row in enumerate(tap_rows):
                    nc.vector.tensor_tensor(tap_lo[:, k], row, tap_hi[:, k], ALU.subtract).then_inc(s_bit, 1)


            done = [0]

            def next_centroid_step(instruction):
                done[0] += 1
                instruction.then_inc(s_cent, 1)
                dve.wait_ge(s_cent, done[0])

            def project_centroids():
                dve.wait_ge(s_proj_w, 16 * 10)
                next_centroid_step(nc.vector.tensor_tensor(cent_sq, cent_s[:], cent_s[:], ALU.mult))
                next_centroid_step(nc.vector.tensor_reduce(cent_n[:, 0:1], cent_sq, AX_X, ALU.add))
                next_centroid_step(nc.vector.tensor_scalar(cent_n[:, 0:1], cent_n[:, 0:1], 1e-14, None, ALU.max))
                inverse_root(next_centroid_step, cent_n[:, 0:1], cent_n[:, 1:2], cent_n[:, 2:3])
                next_centroid_step(nc.vector.tensor_scalar(cent_n[:, 2:3], cent_n[:, 1:2], 0.95, 1.0, ALU.mult,
                                                           ALU.min))
                next_centroid_step(nc.vector.tensor_scalar(cent_s[:], cent_s[:], cent_n[:, 2:3], None, ALU.mult))
                nc.vector.tensor_scalar(bq_s[:], bq_s[:], HD ** -0.5, None, ALU.mult).then_inc(s_bq, 1)
                nc.vector.tensor_scalar(bp_mat, ones[:], bp_s[:, 0:1], None, ALU.mult).then_inc(s_bp, 1)
                assert done[0] == CENTROID_STEPS

            def transpose_centroids():
                dve.wait_ge(s_cent_pe, 1)
                next_centroid_step(nc.vector.tensor_copy(cent_t[:], bank(6)[:, 0:EXPERTS]))
                next_centroid_step(nc.vector.tensor_tensor(cent_t_sq[:], cent_t[:], cent_t[:], ALU.mult))

            def centroid_constants():
                dve.wait_ge(s_cent_pe, 2)
                next_centroid_step(nc.vector.tensor_scalar(c_norm[:], bank(7)[:, 0:EXPERTS], 0.99, None, ALU.min))
                next_centroid_step(nc.vector.tensor_scalar(c_rest[:], c_norm[:], -1.0, 1.0, ALU.mult, ALU.add))
                next_centroid_step(nc.vector.tensor_copy(zc_bias[:, D:], bank(7)[:, 16:16 + EXPERTS]))
                next_centroid_step(nc.vector.tensor_copy(wp_c[:, D:], bank(7)[:, 32:32 + EXPERTS]))

            def spread(a):
                return a.unsqueeze(2).broadcast_to([P, TILES, EXPERTS])

            def all_tokens(a):
                return a.unsqueeze(1).broadcast_to([P, TILES, EXPERTS])

            def low_half(m):
                wait(dve, xn2_out, m, 2)
                nc.vector.tensor_tensor(x_lo[:], xn_t[:], x_hi[:], ALU.subtract).then_inc(xlo_out.sem, 1)

            def projection(m):
                wait(dve, z_mm, m, 1)
                nc.vector.tensor_tensor(
                    zc[:].rearrange("p (c t) f -> p c t f", c=2),
                    bank(2, 2).rearrange("p (c x) -> p c x", c=2)[:, :, 0:2 * (D + EXPERTS)].rearrange(
                        "p c (t f) -> p c t f", t=2),
                    zc_bias[:].unsqueeze(1).unsqueeze(1).broadcast_to([P, 2, 2, D + EXPERTS]),
                    ALU.add).then_inc(z_out.sem, 1)

            def stepper(m, first):
                step = [first]

                def then(instruction):
                    step[0] += 1
                    instruction.then_inc(route.sem, 1)
                    wait(dve, route, m, step[0])
                return step, then

            def route_distances(m):
                step, then = stepper(m, 0)
                wait(dve, z_squared, m, 1)
                wait(dve, z_out, m, 1)
                then(nc.vector.tensor_reduce(r1[:, 0], z_sq[:], AX_X, ALU.add))
                then(nc.vector.tensor_scalar(r1[:, 1], r1[:, 0], 1e-14, None, ALU.max))
                inverse_root(then, r1[:, 1], r1[:, 2], r1[:, 5])
                then(nc.vector.tensor_scalar(r1[:, 2], r1[:, 2], 0.95, 1.0, ALU.mult, ALU.min))
                then(nc.vector.tensor_tensor(r1[:, 3], r1[:, 0], r1[:, 2], ALU.mult))
                then(nc.vector.tensor_tensor(r1[:, 3], r1[:, 3], r1[:, 2], ALU.mult))
                then(nc.vector.tensor_scalar(r1[:, 3], r1[:, 3], 0.99, None, ALU.min))
                then(nc.vector.tensor_scalar(r1[:, 4], r1[:, 3], -1.0, 1.0, ALU.mult, ALU.add))
                then(nc.vector.tensor_tensor(r8[:, 0], zc[:, :, D:], spread(r1[:, 2]), ALU.mult))
                then(nc.vector.tensor_tensor(r8[:, 1], all_tokens(c_norm[:]), spread(r1[:, 3]), ALU.add))
                then(nc.vector.scalar_tensor_tensor(out=r8[:, 1], in0=r8[:, 0], scalar=-2.0, in1=r8[:, 1],
                                                    op0=ALU.mult, op1=ALU.add))
                then(nc.vector.tensor_scalar(r8[:, 1], r8[:, 1], 0.0, 2.0, ALU.max, ALU.mult))
                then(nc.vector.tensor_tensor(r8[:, 2], all_tokens(c_rest[:]), spread(r1[:, 4]), ALU.mult))
                then(nc.vector.tensor_scalar(r8[:, 2], r8[:, 2], 1e-7, None, ALU.add))
                then(nc.vector.reciprocal(r8[:, 2], r8[:, 2]))
                then(nc.vector.tensor_tensor(r8[:, 3], r8[:, 1], r8[:, 2], ALU.mult))
                then(nc.vector.tensor_scalar(r8[:, 3], r8[:, 3], 1.0, 1.0 + 1e-7, ALU.add, ALU.max))
                then(nc.vector.tensor_scalar(r8[:, 6], r8[:, 3], 1.0, None, ALU.add))
                then(nc.vector.scalar_tensor_tensor(out=r8[:, 4], in0=r8[:, 3], scalar=-1.0, in1=r8[:, 6],
                                                    op0=ALU.add, op1=ALU.mult))
                assert step[0] == DISTANCE_STEPS, step[0]

            def route_ranks(m):
                step, then = stepper(m, DISTANCE_STEPS)
                inverse_root(then, r8[:, 4], r8[:, 5], r8[:, 6])
                then(nc.vector.tensor_tensor(r8[:, 5], r8[:, 5], r8[:, 4], ALU.mult))
                then(nc.vector.scalar_tensor_tensor(out=u[:], in0=r8[:, 5], scalar=-1.0, in1=r8[:, 3],
                                                    op0=ALU.mult, op1=ALU.subtract))
                nc.vector.memset(gate[:], 0.0)
                for t in range(TILES):
                    nc.vector.max(best[:, t], u[:, t]).then_inc(route.sem, 1)
                step[0] += TILES
                wait(dve, route, m, step[0])
                nc.vector.memset(gate[:], 0.0)
                for t in range(TILES):
                    nc.vector.max_index(best_i[:, t], best[:, t], u[:, t]).then_inc(route.sem, 1)
                step[0] += TILES
                wait(dve, route, m, step[0])
                assert step[0] == RANK_STEPS, step[0]

            def route_weights(m):
                step, then = stepper(m, RANK_STEPS)
                then(nc.vector.tensor_copy(best_f[:], best_i[:]))
                then(nc.vector.tensor_tensor(r1[:, 5], best[:, :, 0], best[:, :, 1], ALU.add))
                then(nc.vector.reciprocal(r1[:, 5], r1[:, 5]))
                then(nc.vector.tensor_tensor(r1[:, 6], best[:, :, 1], r1[:, 5], ALU.mult))
                then(nc.vector.tensor_tensor(r1[:, 7], best[:, :, 0], r1[:, 5], ALU.mult))
                for n in range(2):
                    target = comb[:] if n == 0 else r8[:, 6]
                    then(nc.vector.tensor_tensor(target, all_tokens(iota8[:]), spread(best_f[:, :, n]),
                                                 ALU.is_equal))
                    then(nc.vector.tensor_tensor(target, target, spread(r1[:, 6 + n]), ALU.mult))
                then(nc.vector.tensor_tensor(comb[:], comb[:], r8[:, 6], ALU.add))
                assert step[0] == ROUTE_STEPS, step[0]

            def start_sum(m):
                wait(dve, b2_mm, m, 1)
                wait(dve, stored, m, 0)
                nc.vector.tensor_tensor(y_sum[:], bank(4).rearrange("p (t d) -> p t d", t=TILES), x3[:],
                                        ALU.add).then_inc(y_used.sem, 1)

            def expert_adds(m, experts_range):
                for e in experts_range:
                    wait(dve, y_mm, m, e + 1)
                    for t in range(TILES):
                        wait(dve, y_used, m, 1 if e == 0 else 1 + TILES * (e - 1) + t + 1)
                        nc.vector.scalar_tensor_tensor(out=y_sum[:, t], in0=bank(6 + e % 2)[:, t * D:(t + 1) * D],
                                                       scalar=comb[:, t, e:e + 1], in1=y_sum[:, t], op0=ALU.mult,
                                                       op1=ALU.add).then_inc(y_used.sem, 1)

            def layernorm(b, n, src, dst, shrink=1.0, stats=True):
                if stats:
                    for t in range(TILES):
                        nc.vector.bn_stats(moments[:, t], src[:, t]).then_inc(ln_mom[n].sem, 1)
                wait(dve, ln_mom[n], b, TILES)
                nc.vector.memset(gate[:], 0.0)
                for t in range(TILES):
                    nc.vector.bn_aggr(mean_var[:, t], moments[:, t]).then_inc(ln_mom[n].sem, 1)
                wait(dve, ln_mom[n], b, 2 * TILES)
                count = [0]

                def then(instruction):
                    count[0] += 1
                    instruction.then_inc(ln_rstd[n].sem, 1)
                    wait(dve, ln_rstd[n], b, count[0])

                then(nc.vector.tensor_scalar(newton[:, 0], mean_var[:, :, 1], LN_EPS, shrink, ALU.add, ALU.mult))
                inverse_root(then, newton[:, 0], rstd[:], newton[:, 1])
                assert count[0] == LN_STEPS
                for t in range(TILES):
                    nc.vector.tensor_scalar(dst[:, t], src[:, t], mean_var[:, t, 0:1], rstd[:, t:t + 1],
                                            ALU.subtract, ALU.mult).then_inc(ln_out[n].sem, 1)
                wait(dve, ln_out[n], b, TILES)

            def split_q(b, l):
                nc.vector.tensor_copy(q_hi[:], q_f[:]).then_inc(q_split[l].sem, 1)
                wait(dve, q_split[l], b, 1)
                nc.vector.tensor_tensor(q_feat[:, :, :, HD:2 * HD], q_f[:].rearrange("p t (h d) -> p t h d", d=HD),
                                        q_hi[:].rearrange("p t (h d) -> p t h d", d=HD),
                                        ALU.subtract).then_inc(q_split[l].sem, 1)

            def first_norm(b):
                wait(dve, x_loaded, b, 16)
                layernorm(b, 0, x_in, q_f, shrink=float(HD))
                split_q(b, 0)

            def low_expert_weights():
                dve.wait_ge(s_ew1, 1)
                nc.vector.scalar_tensor_tensor(out=ew1_lo[:].rearrange("p e f -> p (e f)"), in0=ew1_raw,
                                               scalar=W1_SCALE, in1=ew1_hi[:].rearrange("p e f -> p (e f)"),
                                               op0=ALU.mult, op1=ALU.subtract).then_inc(s_ew1_lo, 1)

            def bias_keys_values(b):
                wait(dve, kv_mm, b, 1)
                nc.vector.tensor_tensor(kv1[:].rearrange("p c n -> p (c n)"), bank(0), kv_bias[:].rearrange(
                    "p c n -> p (c n)"), ALU.add).then_inc(kv_out.sem, 1)

            def turn(b, experts, last=False):
                def experts_at(point):
                    if experts:
                        expert_adds(b - 1, EXPERT_ADDS[point])

                def maxima(l):
                    for t in range(TILES):
                        for p in range(3):
                            m = 3 * t + p
                            (h0, n), _ = MAX_HEADS[2 * p], MAX_HEADS[2 * p + 1]
                            wait(dve, s_tok[l], b, m + 1)
                            scores = bank(2 * (m % 2), 2).rearrange("p (c x) -> p c x", c=2)[:, :, 0:n * KEYS]
                            nc.vector.tensor_reduce(neg_max[:, t, h0:h0 + 2 * n].rearrange("p (c h) -> p c h", c=2),
                                                    scores.rearrange("p c (h k) -> p c h k", k=KEYS), AX_X, ALU.max,
                                                    negate=True).then_inc(maxed[l].sem, 1)
                        wait(dve, maxed[l], b, 3 * t + 3)
                        nc.vector.tensor_copy(q_feat[:, t, :, 3 * HD], neg_max[:, t]).then_inc(shift[l].sem, 1)
                        wait(dve, shift[l], b, 2 * t + 1)
                        nc.vector.tensor_tensor(q_feat[:, t, :, 3 * HD + 1], neg_max[:, t], q_feat[:, t, :, 3 * HD],
                                                ALU.subtract).then_inc(shift[l].sem, 1)

                def copy_outputs(l, g):
                    wait(dve, pv[l], b, g + 1)
                    nc.vector.tensor_copy(o_t[:, g], bank(4 + g % 2)).then_inc(o_out[l].sem, 1)

                def normalise(l):
                    wait(dve, o_tok[l], b, 1)
                    o = bank(0, 4).rearrange("p (s f) -> p s f", f=QUAD)
                    nc.vector.reciprocal(denom[:], o[:, :, HD]).then_inc(attn_out[l].sem, 1)
                    wait(dve, attn_out[l], b, 1)
                    nc.vector.tensor_tensor(attn[:].rearrange("p t (h d) -> p (t h) d", d=HD), o[:, :, 0:HD],
                                            denom[:].unsqueeze(2).broadcast_to([P, TILES * HEADS, HD]),
                                            ALU.mult).then_inc(attn_out[l].sem, 1)
                    wait(dve, attn_out[l], b, 2)

                if experts:
                    low_half(b - 1)
                    projection(b - 1)
                maxima(0)
                if experts:
                    route_distances(b - 1)
                else:
                    make_bitnet_weights()
                    make_taps()
                copy_outputs(0, 0)
                if experts:
                    route_ranks(b - 1)
                else:
                    project_centroids()
                copy_outputs(0, 1)
                if experts:
                    route_weights(b - 1)
                copy_outputs(0, 2)
                copy_outputs(0, 3)
                normalise(0)
                nc.vector.tensor_tensor(x1[:], x_in[:], attn[:], ALU.add).then_inc(x1_out.sem, 1)
                wait(dve, x1_out, b, 1)

                layernorm(b, 1, x1, xn)
                nc.vector.tensor_reduce(top[:], xn[:], AX_X, ALU.max,
                                        apply_absolute_value=True).then_inc(xq_scale.sem, 1)
                wait(dve, xq_scale, b, 1)
                nc.vector.tensor_scalar(top[:], top[:], 1e-5, None, ALU.max).then_inc(xq_scale.sem, 1)
                wait(dve, xq_scale, b, 2)
                nc.vector.reciprocal(a_scale[:], top[:]).then_inc(xq_scale.sem, 1)
                wait(dve, xq_scale, b, 3)
                nc.vector.tensor_scalar(a_scale[:], a_scale[:], 127.0, None, ALU.mult).then_inc(xq_scale.sem, 1)
                wait(dve, xq_scale, b, 4)
                for t in range(TILES):
                    nc.vector.tensor_scalar(x_whole[:, t], xn[:, t], a_scale[:, t:t + 1], ROUND, ALU.mult,
                                            ALU.add).then_inc(xq_out.sem, 1)
                nc.vector.reciprocal(a_step[:], a_scale[:]).then_inc(xq_scale.sem, 1)
                wait(dve, xq_out, b, TILES)
                wait(dve, xq_scale, b, 5)
                for t in range(TILES):
                    nc.vector.tensor_scalar(x_whole[:, t], x_whole[:, t], ROUND, a_step[:, t:t + 1], ALU.subtract,
                                            ALU.mult).then_inc(xq_out.sem, 1)
                if experts:
                    start_sum(b - 1)
                wait(dve, xs_hi_out, b, 1)
                nc.vector.tensor_tensor(xs_lo[:, 1:SEQ + 1], bank(0), xs_hi[:, 1:SEQ + 1],
                                        ALU.subtract).then_inc(xs_lo_out.sem, 1)
                experts_at("quant")
                wait(dve, h_tr, b, CH)
                nc.vector.tensor_reduce(top[:], bank(0, 4).rearrange("p (t f) -> p t f", t=TILES), AX_X, ALU.max,
                                        apply_absolute_value=True).then_inc(hq_scale.sem, 1)
                wait(dve, hq_scale, b, 1)
                nc.vector.tensor_scalar(top[:], top[:], 1e-5, None, ALU.max).then_inc(hq_scale.sem, 1)
                wait(dve, hq_scale, b, 2)
                nc.vector.reciprocal(a_scale[:], top[:]).then_inc(hq_scale.sem, 1)
                wait(dve, hq_scale, b, 3)
                nc.vector.tensor_scalar(a_scale[:], a_scale[:], 127.0, None, ALU.mult).then_inc(hq_scale.sem, 1)
                wait(dve, hq_scale, b, 4)
                for t in range(TILES):
                    nc.vector.tensor_scalar(h_whole[:, t], bank(t), a_scale[:, t:t + 1], ROUND, ALU.mult,
                                            ALU.add).then_inc(hq_whole.sem, 1)
                nc.vector.reciprocal(a_step[:], a_scale[:]).then_inc(hq_scale.sem, 1)
                wait(dve, hq_scale, b, 5)
                nc.vector.tensor_scalar(a_step[:], a_step[:], w_step[:, 1:2], None,
                                        ALU.mult).then_inc(hq_scale.sem, 1)
                wait(dve, hq_scale, b, 6)
                experts_at("hq")
                for t in range(TILES):
                    wait(dve, down, b, t + 1)
                    nc.vector.scalar_tensor_tensor(out=x2[:, t], in0=bank(t)[:, 0:D], scalar=a_step[:, t:t + 1],
                                                   in1=x1[:, t], op0=ALU.mult, op1=ALU.add).then_inc(x2_out.sem, 1)
                    wait(dve, x2_out, b, t + 1)
                    nc.vector.memset(gate[:], 0.0)
                    nc.vector.bn_stats(moments[:, t], x2[:, t]).then_inc(ln_mom[2].sem, 1)

                layernorm(b, 2, x2, xn, stats=False)
                experts_at("norm2")
                if not experts:
                    dve.wait_ge(s_bq, 1)
                wait(dve, q_mm, b, 1)
                nc.vector.scalar_tensor_tensor(out=q_f[:], in0=bank(0).rearrange("p (t d) -> p t d", t=TILES),
                                               scalar=HD ** -0.5, in1=bq_s[:].unsqueeze(1).broadcast_to([P, TILES, D]),
                                               op0=ALU.mult, op1=ALU.add).then_inc(q_ready.sem, 1)
                wait(dve, q_ready, b, 1)
                split_q(b, 1)
                experts_at("query1")
                maxima(1)
                experts_at("shift1")
                if not experts:
                    transpose_centroids()
                    low_expert_weights()
                copy_outputs(1, 0)
                if not last:
                    first_norm(b + 1)
                for g in range(1, GROUPS):
                    copy_outputs(1, g)
                normalise(1)
                experts_at("out1")
                wait(dve, o_mm, b, 1)
                wait(dve, x2b_out, b, 1)
                nc.vector.tensor_tensor(x3[:], bank(0).rearrange("p (t d) -> p t d", t=TILES), x2_bo[:],
                                        ALU.add).then_inc(x3_out.sem, 1)
                wait(dve, x3_out, b, 1)

                layernorm(b, 3, x3, xn)
                if not experts:
                    centroid_constants()
                if not last:
                    bias_keys_values(b + 1)
                experts_at("norm3")

            first_norm(0)
            later_zeros()
            bias_keys_values(0)
            later_ones()
            sum_bitnet_weights()
            turn(0, False)
            with dve.Fori(1, BATCH - 1) as b:
                turn(b, True)
            turn(BATCH - 1, True, last=True)
            low_half(BATCH - 1)
            projection(BATCH - 1)
            route_distances(BATCH - 1)
            route_ranks(BATCH - 1)
            route_weights(BATCH - 1)
            start_sum(BATCH - 1)
            expert_adds(BATCH - 1, range(EXPERTS))

        @block.tensor
        def _(pe):
            pe.wait_ge(s_memset, 1)
            pe.wait_ge(s_ident, 3)

            def transposed(dst, src):
                for t in range(TILES):
                    mm = nc.tensor.transpose(dst[:, t * P:(t + 1) * P], src[:, t],
                                             ident[:] if dst.dtype == F32 else ident16[:])
                return mm

            def norm_transposes(m):
                wait(pe, ln_out[3], m, TILES)
                transposed(bank(3), xn).then_inc(xn2_tr.sem, 1)

            def projection(m, b):
                wait(pe, xn2_out, m, 2)
                wait(pe, qh_out[0], b, 1)
                pe.wait_ge(s_cent, CENTROID_STEPS + 6)
                n = D + EXPERTS
                for t in range(TILES):
                    mm = nc.tensor.matmul(bank(2 + t // 2)[:, t % 2 * n:(t % 2 + 1) * n], xn_t[:, t * P:(t + 1) * P],
                                          wp_c[:], start=True, stop=True)
                mm.then_inc(z_mm.sem, 1)

            def weight_transposes(m):
                wait(pe, route, m, ROUTE_STEPS)
                pe.wait_ge(s_exp_rest, 48)
                for t in range(TILES):
                    mm = nc.tensor.transpose(bank(4)[0:EXPERTS, t * P:(t + 1) * P], comb[:, t], ident[:])
                mm.then_inc(comb_tr.sem, 1)

            def bias_products(m):
                wait(pe, combt_out, m, 1)
                for t in range(TILES):
                    mm = nc.tensor.matmul(bank(4)[:, t * D:(t + 1) * D], comb_t[:, t * P:(t + 1) * P], eb2[:],
                                          start=True, stop=True)
                mm.then_inc(b2_mm.sem, 1)

            def hidden_step(m, n):
                if n == 0:
                    wait(pe, xlo_out, m, 1)
                    pe.wait_ge(s_ew1_lo, 1)
                    pe.wait_ge(s_exp_rest, 48)
                elif last_entry(m):
                    if n >= 2:
                        wait(pe, gelu, m, n - 1)
                else:
                    wait(pe, gelu, m, n)
                e, c = divmod(n, CH)
                w = slice(c * P, (c + 1) * P)
                dst = hidden_bank(m, n)
                nc.tensor.matmul(dst, ew1_hi[:, e, w], x_hi[:], start=True, stop=False)
                nc.tensor.matmul(dst, ew1_hi[:, e, w], x_lo[:], start=False, stop=False)
                nc.tensor.matmul(dst, ew1_lo[:, e, w], x_hi[:], start=False, stop=True).then_inc(h_mm.sem, 1)

            def output_step(m, n):
                e, t = divmod(n, TILES)
                if t == 0:
                    wait(pe, gelu, m, CH * (e + 1))
                    if e >= 2:
                        wait(pe, y_used, m, 1 + TILES * (e - 1))
                for c in range(CH):
                    mm = nc.tensor.matmul(bank(6 + e % 2)[:, t * D:(t + 1) * D],
                                          hidden[:, e % 2, c, t * P:(t + 1) * P], ew2[:, e, c],
                                          start=(c == 0), stop=(c == CH - 1))
                if t == TILES - 1:
                    mm.then_inc(y_mm.sem, 1)

            def expert_steps(m, hidden_steps, output_steps):
                hidden_steps, output_steps = list(hidden_steps), list(output_steps)
                while hidden_steps or output_steps:
                    if hidden_steps:
                        hidden_step(m, hidden_steps.pop(0))
                    if output_steps and (not hidden_steps or
                                         hidden_steps[0] >= CH * (output_steps[0] // TILES + 1)):
                        output_step(m, output_steps.pop(0))

            def key_features(b, l):
                wait(pe, kf_ready[l], b, 3)
                for c in range(2):
                    for g in range(GROUPS):
                        mm = nc.tensor.transpose(bank16(4 + l)[:, (4 * c + g) * P:(4 * c + g + 1) * P],
                                                 k_feat[l][:, c, 4 * g:4 * g + 4, :].rearrange("p h f -> p (h f)"),
                                                 ident16[:])
                mm.then_inc(kf_t[l].sem, 1)

            def q_transposes(b, l):
                wait(pe, q_split[l], b, 1)
                for t in range(TILES):
                    mm = nc.tensor.transpose(bank16(2 if l == 0 else 4)[:, t * P:(t + 1) * P], q_hi[:, t], ident16[:])
                mm.then_inc(qh_t[l].sem, 1)

            def first_products(b, later):
                if later:
                    key_features(b, 0)
                q_transposes(b, 0)
                wait(pe, ctx_loaded, b, 32)
                nc.tensor.matmul(bank(1)[:, 0:KEYS], wkv_s[:, 0:D], ctx_t[:, 0:KEYS], start=True, stop=True)
                if later:
                    wait(pe, x3_out, b - 1, 1)
                for c in range(2):
                    mm = nc.tensor.matmul(bank(0)[:, c * 2 * D:(c + 1) * 2 * D], ctx_t[:, c * KEYS:c * KEYS + P],
                                          wkv_s[:], start=True, stop=True)
                mm.then_inc(kv_mm.sem, 1)

            def turn(b, experts, last=False):
                def experts_at(point):
                    if experts:
                        expert_steps(b - 1, HIDDEN_STEPS.get(point, ()), OUTPUT_STEPS.get(point, ()))

                def score_pair(l, k):
                    if k >= 2:
                        wait(pe, exped[l], b, k - 1)
                    for slot in range(2):
                        n = 2 * k + slot
                        g, j = divmod(n, 5)
                        keys, c = (k_main[l][:, 4 * g + j], 0) if j < 4 else (k_rest[l][:, g], 1)
                        dst = bank(2 * (k % 2) + slot)
                        mm = nc.tensor.matmul(dst, keys, q_op[:, g], start=True, stop=(l == 1))
                        if l == 0:
                            mm = nc.tensor.matmul(dst, mask_diag[:], m_key[:, c], start=False, stop=True)
                    mm.then_inc(s_key[l].sem, 1)

                def weighted_values(l, g):
                    wait(pe, exped[l], b, (5 * g + 4) // 2 + 1)
                    if g >= 2:
                        wait(pe, o_out[l], b, g - 1)
                    if g == 0:
                        wait(pe, v_ready[l], b, 5)
                    for c in range(2):
                        for j in range(PER_GROUP):
                            quad = slice(QUAD * j, QUAD * (j + 1))
                            n = 5 * g + (j if c == 0 else 4)
                            values = (v_rest if c else v_main)[l]
                            mm = nc.tensor.matmul(bank(4 + g % 2)[quad, :], values[:, 4 * g + j, :],
                                                  probs[:, n % RING, :], start=(c == 0), stop=(c == 1),
                                                  tile_position=(0, QUAD * j))
                    mm.then_inc(pv[l].sem, 1)

                def attention(l):
                    wait(pe, kb_ready[l], b, 1)
                    wait(pe, qh_out[l], b, 1)
                    if l == 0:
                        wait(pe, masks, b, 1)

                    def feature_transposes(t):
                        wait(pe, shift[l], b, 2 * t + 2)
                        if t == 0:
                            wait(pe, k_ready[l], b, 2 * PER_GROUP)
                            wait(pe, q_hi2[l], b, 2)
                            wait(pe, q_split[l], b, 2)
                        if t >= 1:
                            wait(pe, q_out[l], b, t)
                        for g in range(GROUPS):
                            mm = nc.tensor.transpose(bank16(4)[:, g * P:(g + 1) * P],
                                                     q_feat[:, t, 4 * g:4 * g + 4, :].rearrange("p h f -> p (h f)"),
                                                     ident16[:])
                        mm.then_inc(qf_t[l].sem, 1)

                    for t in range(TILES):
                        for p in range(3):
                            m = 3 * t + p
                            if m >= 2:
                                wait(pe, maxed[l], b, m - 1)
                            for s in range(2):
                                h0, n = MAX_HEADS[2 * p + s]
                                dst = bank(2 * (m % 2) + s)[:, 0:n * KEYS]
                                mm = nc.tensor.matmul(dst, q_hi_t[:, t * P:(t + 1) * P],
                                                      k_blocks[l][:, h0:h0 + n, :].rearrange("p h k -> p (h k)"),
                                                      start=True, stop=(l == 1))
                                if l == 0:
                                    mm = nc.tensor.matmul(dst.rearrange("p (h k) -> p h k", k=KEYS), mask_diag[:],
                                                          m_tok[:, t].unsqueeze(1).broadcast_to([P, n, KEYS]),
                                                          start=False, stop=True)
                            mm.then_inc(s_tok[l].sem, 1)
                            if m == 0 and l == 0 and experts:
                                projection(b - 1, b)
                            experts_at(f"max{l}_{m}")
                            if m == 0 and l == 0 and experts:
                                wait(pe, z_out, b - 1, 1)
                            if m == 2 and l == 0 and not experts:
                                key_features(b, 0)
                                pe.wait_ge(s_bit, 2)
                                nc.tensor.matmul(bank(7)[:, 0:2], ones[:], abs_sums[:], start=True,
                                                 stop=True).then_inc(s_wsum, 1)
                            if p == 1 and t >= 1:
                                feature_transposes(t - 1)
                    experts_at(f"shift{l}")
                    feature_transposes(TILES - 1)
                    experts_at(f"ready{l}")
                    wait(pe, q_out[l], b, TILES)
                    wait(pe, k_ready[l], b, 2 * PER_GROUP)
                    if l == 0:
                        wait(pe, masks, b, 2)
                    k = 0
                    for g, ahead in enumerate((5, 8, 10, 10)):
                        while k < ahead:
                            score_pair(l, k)
                            k += 1
                            if l == 0 and k == 3:
                                key_features(b, 1)
                        if l == 0 and g == 1:
                            wait(pe, k_ready[1], b, 2 * PER_GROUP)
                        weighted_values(l, g)
                        if l == 1 and g == 1:
                            experts_at("exp1")
                    for g in range(GROUPS):
                        wait(pe, o_out[l], b, g + 1)
                        for t in range(TILES):
                            mm = nc.tensor.transpose(bank(t)[:, g * P:(g + 1) * P], o_t[:, g, t * P:(t + 1) * P],
                                                     ident[:])
                    mm.then_inc(o_tok[l].sem, 1)

                if experts:
                    norm_transposes(b - 1)
                wait(pe, kv_out, b, 1)
                wait(pe, k1t_out, b, 1)
                attention(0)

                if experts:
                    weight_transposes(b - 1)
                    experts_at("bias")
                    bias_products(b - 1)
                else:
                    pe.wait_ge(s_cent, CENTROID_STEPS)
                    nc.tensor.transpose(bank(6)[:, 0:EXPERTS], cent_s[:],
                                        ident[0:EXPERTS, 0:EXPERTS]).then_inc(s_cent_pe, 1)
                experts_at("quant")
                if experts:
                    wait(pe, y_used, b - 1, 1)
                wait(pe, xq_out, b, 2 * TILES)
                transposed(bank(0), x_whole).then_inc(xs_tr.sem, 1)
                experts_at("copied_xs")
                wait(pe, xs_hi_out, b, 1)
                for c in range(CH):
                    w = slice(c * P, (c + 1) * P)
                    for k in range(3):
                        nc.tensor.matmul(bank(4), tap_hi[:, k, w], xs_hi[:, k:SEQ + k], start=(k == 0), stop=False)
                    for k in range(3):
                        nc.tensor.matmul(bank(4), tap_lo[:, k, w], xs_hi[:, k:SEQ + k], start=False, stop=False)
                    if c == 0:
                        wait(pe, xs_lo_out, b, 1)
                    for k in range(3):
                        mm = nc.tensor.matmul(bank(4), tap_hi[:, k, w], xs_lo[:, k:SEQ + k], start=False,
                                              stop=(k == 2))
                    mm.then_inc(conv.sem, 1)
                    experts_at(f"conv_{c}")
                    wait(pe, silu, b, c + 1)
                    for t in range(TILES):
                        mm = nc.tensor.transpose(bank(t)[:, c * P:(c + 1) * P], h_act[:, c, t * P:(t + 1) * P],
                                                 ident[:])
                    mm.then_inc(h_tr.sem, 1)
                experts_at("hq")

                def down_product(t):
                    for c in range(CH):
                        mm = nc.tensor.matmul(bank(t)[:, 0:D], hq_t[:, t, c], bit_w2[:, c], start=(c == 0),
                                              stop=(c == CH - 1))
                    mm.then_inc(down.sem, 1)

                for t in range(TILES):
                    wait(pe, hq_out, b, t + 1)
                    if t >= 1:
                        wait(pe, hqt_out, b, t)
                    for c in range(CH):
                        mm = nc.tensor.transpose(bank16(4)[:, c * P:(c + 1) * P], hq[:, t, c * P:(c + 1) * P],
                                                 ident16[:])
                    mm.then_inc(hq_tr.sem, 1)
                    experts_at(f"hq_{t}")
                    if t >= 1:
                        down_product(t - 1)
                wait(pe, hqt_out, b, TILES)
                down_product(TILES - 1)

                experts_at("norm2")
                wait(pe, ln_out[2], b, TILES)
                transposed(bank(4), xn).then_inc(xn1_tr.sem, 1)
                experts_at("copied_norm2")
                wait(pe, xn1_out, b, 1)
                if not experts:
                    pe.wait_ge(s_proj_w, 16 * 10)
                for t in range(TILES):
                    mm = nc.tensor.matmul(bank(0)[:, t * D:(t + 1) * D], xn_t[:, t * P:(t + 1) * P], wq_s[:],
                                          start=True, stop=True)
                mm.then_inc(q_mm.sem, 1)
                experts_at("query1")
                q_transposes(b, 1)
                experts_at("copied_query1")
                attention(1)
                experts_at("out1")
                wait(pe, attn_out[1], b, 2)
                transposed(bank(4), attn).then_inc(a_tr.sem, 1)
                experts_at("copied1")
                wait(pe, at_out, b, 1)
                for t in range(TILES):
                    mm = nc.tensor.matmul(bank(0)[:, t * D:(t + 1) * D], attn_t[:, t * P:(t + 1) * P], wo_s[:],
                                          start=True, stop=True)
                mm.then_inc(o_mm.sem, 1)

                if not experts:
                    pe.wait_ge(s_cent, CENTROID_STEPS + 2)
                    pe.wait_ge(s_bp, 1)
                    nc.tensor.matmul(bank(7)[:, 0:EXPERTS], ones[:], cent_t_sq[:], start=True, stop=True)
                    nc.tensor.matmul(bank(7)[:, 16:16 + EXPERTS], bp_mat, cent_t[:], start=True, stop=True)
                    nc.tensor.matmul(bank(7)[:, 32:32 + EXPERTS], wp_t, cent_t[:], start=True,
                                     stop=True).then_inc(s_cent_pe, 1)
                if not last:
                    first_products(b + 1, True)
                experts_at("norm3")

            pe.wait_ge(s_kv_w, 16 * 4)
            first_products(0, False)
            turn(0, False)
            with pe.Fori(1, BATCH - 1) as b:
                turn(b, True)
            turn(BATCH - 1, True, last=True)
            norm_transposes(BATCH - 1)
            projection(BATCH - 1, BATCH - 1)
            late = CH * LATE
            expert_steps(BATCH - 1, range(CH), range(0))
            expert_steps(BATCH - 1, range(CH, late), range(late - CH))
            weight_transposes(BATCH - 1)
            bias_products(BATCH - 1)
            expert_steps(BATCH - 1, range(late, CH * EXPERTS), range(late - CH, CH * (EXPERTS - 1)))
            expert_steps(BATCH - 1, range(0), range(CH * (EXPERTS - 1), CH * EXPERTS))


def kernel(x, ctx_1024, mask_BxSxS2_bk1, L0_ffn_w1, L0_ffn_conv_w, L0_ffn_conv_b, L0_ffn_w2, L1_xattn_Wq, L1_xattn_bq,
           L1_xattn_Wk, L1_xattn_bk, L1_xattn_Wv, L1_xattn_bv, L1_xattn_Wo, L1_xattn_bo, L1_ffn_centroids, L1_ffn_Wp,
           L1_ffn_bp, L1_ffn_W1, L1_ffn_b1, L1_ffn_W2, L1_ffn_b2):
    import concourse.bacc as _bacc
    from concourse.bass_utils import run_bass_kernel_spmd as _run

    ctx = np.asarray(ctx_1024)
    mask = np.asarray(mask_BxSxS2_bk1)
    ctx_rest = np.zeros((BATCH, PER_GROUP, QUAD, D), ctx.dtype)
    ctx_rest[:, :, :REST] = ctx[:, None, P:]
    ctx_rest = ctx_rest.reshape(BATCH, P, D)
    mask_rest = np.zeros((BATCH, PER_GROUP, QUAD, SEQ), mask.dtype)
    mask_rest[:, :, :REST] = mask.transpose(0, 2, 1)[:, None, P:]
    mask_t = np.stack([mask.transpose(0, 2, 1)[:, :P], mask_rest.reshape(BATCH, P, SEQ)], axis=2)
    bkv = np.concatenate([np.asarray(L1_xattn_bk), np.asarray(L1_xattn_bv)])
    kv_bias = np.zeros((PER_GROUP, QUAD, 2, 2 * D), bkv.dtype)
    kv_bias[:, :, 0] = bkv
    kv_bias[:, :REST, 1] = bkv
    arrays = {
        "x": x,
        "ctxt": np.concatenate([ctx.transpose(0, 2, 1), ctx_rest.transpose(0, 2, 1)], axis=2),
        "ctx_km": np.stack([ctx[:, :P], ctx_rest], axis=2),
        "mask_tm": mask,
        "mask_t": mask_t,
        "w1t": np.asarray(L0_ffn_w1).T,
        "conv_w": np.asarray(L0_ffn_conv_w).reshape(HIDDEN, 3).T,
        "conv_b": np.asarray(L0_ffn_conv_b).reshape(CH, P).T,
        "w2t": np.asarray(L0_ffn_w2).T,
        "wq_t": np.asarray(L1_xattn_Wq).T, "bq": L1_xattn_bq,
        "wk_t": np.asarray(L1_xattn_Wk).T, "bk_col": np.asarray(L1_xattn_bk).reshape(D, 1),
        "wv_t": np.asarray(L1_xattn_Wv).T, "kv_bias_in": kv_bias.reshape(P, 2, 2 * D),
        "wo_t": np.asarray(L1_xattn_Wo).T, "bo": L1_xattn_bo,
        "cent": L1_ffn_centroids,
        "wp": L1_ffn_Wp, "wpt": np.asarray(L1_ffn_Wp).T, "bp": L1_ffn_bp, "bp_col": np.asarray(L1_ffn_bp).reshape(D, 1),
        "moe_w1": L1_ffn_W1,
        "moe_b1": np.asarray(L1_ffn_b1).reshape(EXPERTS * CH, P).T,
        "moe_w2": L1_ffn_W2, "moe_b2": L1_ffn_b2,
        "ident_in": np.eye(P, dtype=np.float32),
        "blocks_in": np.kron(np.eye(HEADS, dtype=np.float32), np.ones((HD, 1), np.float32)),
        "iota_in": np.tile(np.arange(EXPERTS, dtype=np.float32), (P, 1)),
    }
    arrays = {f"{n}_dram": np.ascontiguousarray(a) for n, a in arrays.items()}
    nc = _bacc.Bacc("TRN2", target_bir_lowering=False, num_devices=1)
    args = [nc.dram_tensor(n, a.shape, mybir.dt.from_np(a.dtype), kind="ExternalInput").ap()
            for n, a in arrays.items()]
    out = nc.dram_tensor("out_dram", (BATCH, SEQ, D), F32, kind="ExternalOutput").ap()
    build(nc, *args, out)
    r = _run(nc, [arrays], core_ids=[0])
    return r.results[0]["out_dram"]
```
